# Optimizing a Trainium2 kernel written in Bass

```python
import numpy as np
import jax
import jax.numpy as jnp

def _softmax(x, axis=-1):
    return jax.nn.softmax(x, axis=axis)

def _gelu(x):
    return jax.nn.gelu(x, approximate=True)

def _silu(x):
    return jax.nn.silu(x)

def _sigmoid(x):
    return jax.nn.sigmoid(x)

def _layernorm(x, axis=-1, eps=1e-05):
    m = jnp.mean(x, axis=axis, keepdims=True)
    v = jnp.var(x, axis=axis, keepdims=True)
    return (x - m) / jnp.sqrt(v + eps)

def _scatter_add(tgt, idx, src, axis=0):
    return tgt.at[idx].add(src)

def _segment_sum(src, seg, n):
    return jax.ops.segment_sum(src, seg, n)
kernel_name = 'mk_seq_preln_d4_jaxref_r8_bd7ac8'

def setup_inputs(seed: int=0):
    np.random.seed(seed)
    _w = jnp.asarray

    def _L0_attn_setup():
        import math
        import jax, jax.numpy as jnp
        import numpy as np
        CHUNK = 32
        EPS = 1e-05

        def l2norm(x):
            return x * jax.lax.rsqrt(jnp.sum(x * x, -1, keepdims=True))

        def causal_dwconv(x, w):
            C, K = w.shape
            return jax.lax.conv_general_dilated(x, w[:, None, :], (1,), [(K - 1, 0)], feature_group_count=C)

        def per_head_stats(x):
            mean = jnp.mean(x, -1, keepdims=True)
            var = jnp.mean(x * x, -1, keepdims=True) - mean * mean
            abs_mean = jnp.mean(jnp.abs(x), -1, keepdims=True)
            l2 = jnp.sqrt(jnp.sum(x * x, -1, keepdims=True))
            return jnp.concatenate([mean, var, abs_mean, l2], -1)

        def delta_rule_chunkwise(q, k, v, beta, chunk=CHUNK):
            b, h, L, dk = q.shape
            dv = v.shape[-1]
            pad = -L % chunk
            if pad:
                pc = ((0, 0), (0, 0), (0, pad), (0, 0))
                q, k, v = (jnp.pad(t, pc) for t in (q, k, v))
                beta = jnp.pad(beta, ((0, 0), (0, 0), (0, pad)))
            Lp = L + pad
            n = Lp // chunk
            q = l2norm(q)
            k = l2norm(k)
            v = v * beta[..., None]
            kb = k * beta[..., None]
            resh = lambda t: t.reshape(b, h, n, chunk, t.shape[-1])
            q, k, v, kb = map(resh, (q, k, v, kb))
            tri = jnp.triu(jnp.ones((chunk, chunk), bool))
            strict = jnp.triu(jnp.ones((chunk, chunk), bool), 1)
            A = jnp.where(tri, 0.0, -jnp.einsum('bhncd,bhned->bhnce', kb, k))
            for i in range(1, chunk):
                upd = jnp.einsum('...k,...kj->...j', A[..., i, :], A[..., :, :i])
                A = A.at[..., i, :i].add(upd)
            inv = A + jnp.eye(chunk, dtype=A.dtype)
            u = inv @ v
            w = inv @ kb

            def step(S, xs):
                qi, ki, ui, wi = xs
                attn = jnp.where(strict, 0.0, qi @ jnp.swapaxes(ki, -1, -2))
                u_adj = ui - wi @ S
                out_i = qi @ S + attn @ u_adj
                S = S + jnp.swapaxes(ki, -1, -2) @ u_adj
                return (S, out_i)
            xs = tuple((jnp.moveaxis(t, 2, 0) for t in (q, k, u, w)))
            S0 = jnp.zeros((b, h, dk, dv), q.dtype)
            S, outs = jax.lax.scan(step, S0, xs)
            out = jnp.moveaxis(outs, 0, 2).reshape(b, h, Lp, dv)[:, :, :L]
            return (out, S)
        key = jax.random.key(seed)
        ks = jax.random.split(key, 16)
        B, L, D, H = (2, 512, 128, 4)
        dk, dv = (D, D)
        dh = dv // H
        gate_in_dim = D + 16
        gate_hidden = D * 2 // 2
        s = 0.02
        f32 = jnp.float32
        return {'hidden_states': jax.random.normal(ks[0], (B, L, D), f32), 'q_proj_w': jax.random.normal(ks[1], (dk, D), f32) * s, 'k_proj_w': jax.random.normal(ks[2], (dk, D), f32) * s, 'v_proj_w': jax.random.normal(ks[3], (dv, D), f32) * s, 'b_proj_w': jax.random.normal(ks[4], (H, D), f32) * s, 'q_conv_w': jax.random.normal(ks[5], (dk, 4), f32) * 0.1, 'k_conv_w': jax.random.normal(ks[6], (dk, 4), f32) * 0.1, 'v_conv_w': jax.random.normal(ks[7], (dv, 4), f32) * 0.1, 'fir_short_w': jax.random.normal(ks[8], (H, dh, 5), f32) * 0.02, 'fir_long_w': jax.random.normal(ks[9], (H, dh, 64), f32) * 0.02, 'fuse_w1': jax.random.normal(ks[10], (gate_hidden, gate_in_dim), f32) * s, 'fuse_b1': jnp.zeros((gate_hidden,), f32), 'fuse_w2': jax.random.normal(ks[11], (4, gate_hidden), f32) * s, 'fuse_b2': jnp.array([-1.0, -1.0, 1.0, 3.0], f32), 'logit_temp': jnp.full((1,), math.log(math.expm1(0.7)), f32), 'res_scale_short': jnp.full((1,), 0.1, f32), 'res_scale_long': jnp.full((1,), 0.1, f32), 'o_norm_w': jnp.ones((dh,), f32), 'o_proj_w': jax.random.normal(ks[12], (D, dv), f32) * s}
    _L0_attn_in = _L0_attn_setup()

    def _L0_ffn_setup():
        import jax, jax.numpy as jnp
        import numpy as np
        B, S, H, FFN, E = (2, 256, 128, 512, 8)
        key = jax.random.key(seed)
        k0, k1, k2, k3 = jax.random.split(key, 4)
        return {'hidden_states': jax.random.normal(k0, (B, S, H), dtype=jnp.float32), 'Wr': jax.random.normal(k1, (H, E), dtype=jnp.float32) * 0.02, 'br': jnp.zeros((E,), dtype=jnp.float32), 'W1': jax.random.normal(k2, (E, H, FFN), dtype=jnp.float32) * 0.02, 'W2': jax.random.normal(k3, (E, FFN, H), dtype=jnp.float32) * 0.02}
    _L0_ffn_in = _L0_ffn_setup()

    def _L1_attn_setup():
        import jax, jax.numpy as jnp
        import numpy as np
        B, T, DIM = (2, 512, 128)
        DEPTH, HEADS = (4, 8)
        DH = DIM // HEADS
        NLOCAL, WINDOW, BUCKET = (4, 128, 64)
        MULT = 4

        def layer_norm(x, g, b, eps=1e-05):
            m = jnp.mean(x, -1, keepdims=True)
            v = jnp.mean(jnp.square(x - m), -1, keepdims=True)
            return (x - m) * jax.lax.rsqrt(v + eps) * g + b

        def causal_linear_attn(q, k, v):
            b, h, n, e = q.shape
            u = n // BUCKET
            q = jax.nn.softmax(q, axis=-1)
            k = jax.nn.elu(k) + 1.0
            bq = q.reshape(b, h, u, BUCKET, e)
            bk = k.reshape(b, h, u, BUCKET, e)
            bv = v.reshape(b, h, u, BUCKET, e)
            k_cum = jnp.cumsum(bk.sum(axis=-2), axis=-2)
            ctx = jnp.einsum('bhund,bhune->bhude', bk, bv)
            ctx = jnp.cumsum(ctx, axis=2)
            ctx = ctx / (k_cum[..., None] + 1e-06)
            ctx = jnp.pad(ctx, ((0, 0), (0, 0), (1, 0), (0, 0), (0, 0)))[:, :, :-1]
            out = jnp.einsum('bhund,bhude->bhune', bq, ctx)
            return out.reshape(b, h, n, e)

        def local_attn(q, k, v):
            b, lh, t, e = q.shape
            bh = b * lh
            nb = t // WINDOW
            bq = q.reshape(bh, nb, WINDOW, e)
            bk = k.reshape(bh, nb, WINDOW, e)
            bv = v.reshape(bh, nb, WINDOW, e)

            def look_around(x):
                padded = jnp.pad(x, ((0, 0), (1, 0), (0, 0), (0, 0)))
                return jnp.concatenate([padded[:, :-1], padded[:, 1:]], axis=2)
            bk2 = look_around(bk)
            bv2 = look_around(bv)
            tix = jnp.arange(t).reshape(1, nb, WINDOW)
            tpad = jnp.pad(tix, ((0, 0), (1, 0), (0, 0)), constant_values=-1)
            kix = jnp.concatenate([tpad[:, :-1], tpad[:, 1:]], axis=2)
            dots = jnp.einsum('bwie,bwje->bwij', bq, bk2) * e ** (-0.5)
            mask_value = -jnp.finfo(dots.dtype).max
            causal_mask = tix[:, :, :, None] < kix[:, :, None, :]
            pad_mask = (kix == -1)[:, :, None, :]
            dots = jnp.where(causal_mask | pad_mask, mask_value, dots)
            attn = jax.nn.softmax(dots, axis=-1)
            out = jnp.einsum('bwij,bwje->bwie', attn, bv2)
            return out.reshape(b, lh, t, e)

        def self_attention(x, Wq, Wk, Wv, Wo, bo):
            b, t, _ = x.shape
            mh = lambda z: z.reshape(b, t, HEADS, DH).transpose(0, 2, 1, 3)
            q, k, v = (mh(x @ Wq), mh(x @ Wk), mh(x @ Wv))
            lo = local_attn(q[:, :NLOCAL], k[:, :NLOCAL], v[:, :NLOCAL])
            go = causal_linear_attn(q[:, NLOCAL:], k[:, NLOCAL:], v[:, NLOCAL:])
            out = jnp.concatenate([lo, go], axis=1)
            out = out.transpose(0, 2, 1, 3).reshape(b, t, DIM)
            return out @ Wo + bo
        key = jax.random.key(seed)
        ks = jax.random.split(key, 8)
        s = 0.02
        rn = lambda k, shape: jax.random.normal(k, shape, dtype=jnp.float32) * s
        return {'x': jax.random.normal(ks[0], (B, T, DIM), dtype=jnp.float32), 'Wq': rn(ks[1], (DEPTH, DIM, DIM)), 'Wk': rn(ks[2], (DEPTH, DIM, DIM)), 'Wv': rn(ks[3], (DEPTH, DIM, DIM)), 'Wo': rn(ks[4], (DEPTH, DIM, DIM)), 'bo': jnp.zeros((DEPTH, DIM), jnp.float32), 'ln1_g': jnp.ones((DEPTH, DIM), jnp.float32), 'ln1_b': jnp.zeros((DEPTH, DIM), jnp.float32), 'W1': rn(ks[5], (DEPTH, DIM, DIM * MULT)), 'b1': jnp.zeros((DEPTH, DIM * MULT), jnp.float32), 'W2': rn(ks[6], (DEPTH, DIM * MULT, DIM)), 'b2': jnp.zeros((DEPTH, DIM), jnp.float32), 'ln2_g': jnp.ones((DEPTH, DIM), jnp.float32), 'ln2_b': jnp.zeros((DEPTH, DIM), jnp.float32)}
    _L1_attn_in = _L1_attn_setup()

    def _L1_ffn_setup():
        import jax, jax.numpy as jnp
        import numpy as np
        EMBED_DIM = 128
        MLP_RATIO = 4
        NUM_EXPERTS = 8
        CAPACITY = 1.0
        LN_EPS = 1e-05

        def _layernorm(y, gamma, beta):
            mu = jnp.mean(y, axis=-1, keepdims=True)
            var = jnp.mean(jnp.square(y - mu), axis=-1, keepdims=True)
            return (y - mu) * jax.lax.rsqrt(var + LN_EPS) * gamma + beta
        key = jax.random.key(seed)
        k0, k1, k2, k3, k4, k5 = jax.random.split(key, 6)
        d = EMBED_DIM
        dd = EMBED_DIM * MLP_RATIO
        n = NUM_EXPERTS
        x = jax.random.normal(k0, (4, 256, d), dtype=jnp.float32)
        gate_w = jax.random.normal(k1, (n, d), dtype=jnp.float32) * 0.02
        ln_gamma = jnp.ones((d,), dtype=jnp.float32)
        ln_beta = jnp.zeros((d,), dtype=jnp.float32)
        fc1s = jax.random.normal(k2, (n, dd, d), dtype=jnp.float32) * (1.0 / np.sqrt(d))
        b1s = jax.random.normal(k3, (n, dd), dtype=jnp.float32) * 0.02
        fc2s = jax.random.normal(k4, (n, d, dd), dtype=jnp.float32) * (1.0 / np.sqrt(dd))
        b2s = jax.random.normal(k5, (n, d), dtype=jnp.float32) * 0.02
        return {'x': x, 'gate_w': gate_w, 'ln_gamma': ln_gamma, 'ln_beta': ln_beta, 'fc1s': fc1s, 'b1s': b1s, 'fc2s': fc2s, 'b2s': b2s}
    _L1_ffn_in = _L1_ffn_setup()

    def _L2_attn_setup():
        import jax, jax.numpy as jnp
        import numpy as np
        B, T, D = (4, 256, 128)
        H, Kd = (4, 32)
        Vd = 64
        KEY_DIM, VAL_DIM = (H * Kd, H * Vd)
        CONV = 4
        EPS = 1e-06
        LN_EPS = 1e-05

        def _layernorm(x, g, b):
            m = jnp.mean(x, -1, keepdims=True)
            v = jnp.mean((x - m) ** 2, -1, keepdims=True)
            return (x - m) * jax.lax.rsqrt(v + LN_EPS) * g + b

        def _rmsnorm(x, w):
            return x * jax.lax.rsqrt(jnp.mean(x * x, -1, keepdims=True) + EPS) * w

        def _l2norm(x):
            return x * jax.lax.rsqrt(jnp.sum(x * x, -1, keepdims=True) + EPS)

        def _causal_conv_silu(x, w):
            t = x.shape[1]
            xp = jnp.pad(x, ((0, 0), (CONV - 1, 0), (0, 0)))
            y = xp[:, 0:t, :] * w[:, 0]
            for i in range(1, CONV):
                y = y + xp[:, i:i + t, :] * w[:, i]
            return jax.nn.silu(y)

        def _gated_delta_rule(q, k, v, g, beta):
            qT = jnp.moveaxis(q, 1, 0)
            kT = jnp.moveaxis(k, 1, 0)
            vT = jnp.moveaxis(v, 1, 0)
            gT = jnp.moveaxis(g, 1, 0)
            bT = jnp.moveaxis(beta, 1, 0)
            S0 = jnp.zeros((q.shape[0], H, Kd, Vd), q.dtype)

            def step(S, inp):
                q_t, k_t, v_t, g_t, b_t = inp
                S = S * jnp.exp(g_t)[..., None, None]
                kv = jnp.einsum('bhk,bhkv->bhv', k_t, S)
                delta = (v_t - kv) * b_t[..., None]
                S = S + k_t[..., :, None] * delta[..., None, :]
                o = jnp.einsum('bhk,bhkv->bhv', q_t, S)
                return (S, o)
            _, o = jax.lax.scan(step, S0, (qT, kT, vT, gT, bT))
            return jnp.moveaxis(o, 0, 1)

        def _forward(x, ln1_g, ln1_b, ln2_g, ln2_b, rms_in_w, Wq, Wk, Wv, conv_q_w, conv_k_w, conv_v_w, Wa, dt_bias, A_log, Wb, Wg, o_norm_w, Wo, W2, b2):
            b, t, _ = x.shape
            h = _layernorm(x, ln1_g, ln1_b)
            h = _rmsnorm(h, rms_in_w)
            q = _causal_conv_silu(h @ Wq, conv_q_w).reshape(b, t, H, Kd)
            k = _causal_conv_silu(h @ Wk, conv_k_w).reshape(b, t, H, Kd)
            v = _causal_conv_silu(h @ Wv, conv_v_w).reshape(b, t, H, Vd)
            q = _l2norm(q) * Kd ** (-0.5)
            k = _l2norm(k)
            g = -jnp.exp(A_log) * jax.nn.softplus(h @ Wa + dt_bias)
            beta = jax.nn.sigmoid(h @ Wb)
            o = _gated_delta_rule(q, k, v, g, beta)
            gate = (h @ Wg).reshape(b, t, H, Vd)
            o = _rmsnorm(o, o_norm_w) * jax.nn.silu(gate)
            enc = o.reshape(b, t, VAL_DIM) @ Wo
            x = x + enc
            h2 = _layernorm(x, ln2_g, ln2_b)
            x_out = jax.nn.gelu(h2 @ W2 + b2, approximate=False) + x
            return x_out
        key = jax.random.key(seed)
        ks = jax.random.split(key, 16)
        r = lambda k, shp, s=0.02: jax.random.normal(k, shp, dtype=jnp.float32) * s
        return {'x': jax.random.normal(ks[0], (B, T, D), dtype=jnp.float32), 'ln1_g': jnp.ones((D,), jnp.float32), 'ln1_b': jnp.zeros((D,), jnp.float32), 'ln2_g': jnp.ones((D,), jnp.float32), 'ln2_b': jnp.zeros((D,), jnp.float32), 'rms_in_w': jnp.ones((D,), jnp.float32), 'Wq': r(ks[1], (D, KEY_DIM)), 'Wk': r(ks[2], (D, KEY_DIM)), 'Wv': r(ks[3], (D, VAL_DIM)), 'conv_q_w': r(ks[4], (KEY_DIM, CONV), 0.3), 'conv_k_w': r(ks[5], (KEY_DIM, CONV), 0.3), 'conv_v_w': r(ks[6], (VAL_DIM, CONV), 0.3), 'Wa': r(ks[7], (D, H)), 'dt_bias': r(ks[8], (H,), 0.5), 'A_log': jnp.log(jax.random.uniform(ks[9], (H,), minval=1.0, maxval=16.0)), 'Wb': r(ks[10], (D, H)), 'Wg': r(ks[11], (D, VAL_DIM)), 'o_norm_w': jnp.ones((Vd,), jnp.float32), 'Wo': r(ks[12], (VAL_DIM, D)), 'W2': r(ks[13], (D, D)), 'b2': jnp.zeros((D,), jnp.float32)}
    _L2_attn_in = _L2_attn_setup()

    def _L2_ffn_setup():
        import jax, jax.numpy as jnp
        import numpy as np
        DIM = 128
        DEPTH = 2
        HEADS = 8
        DIM_HEAD = 64
        WINDOW = 64
        INNER = HEADS * DIM_HEAD
        HID = int(DIM * 4 * 2 / 3)
        B, N = (2, 1024)
        QK_SCALE = 8.0

        def shift_token(t):
            t1, t2 = jnp.split(t, 2, axis=-1)
            t2 = jnp.pad(t2, ((0, 0), (1, 0), (0, 0)))[:, :-1]
            return jnp.concatenate([t1, t2], axis=-1)

        def l2norm(t):
            return t / jnp.clip(jnp.linalg.norm(t, axis=-1, keepdims=True), 1e-12)

        def rotate_half(x):
            x1, x2 = jnp.split(x, 2, axis=-1)
            return jnp.concatenate([-x2, x1], axis=-1)

        def rotary_xpos(q, k):
            n = q.shape[-2]
            half_idx = jnp.arange(0, DIM_HEAD, 2, dtype=jnp.float32)
            inv_freq = 1.0 / 10000.0 ** (half_idx / DIM_HEAD)
            t = jnp.arange(n, dtype=jnp.float32)
            freqs = t[:, None] * inv_freq[None, :]
            freqs = jnp.concatenate([freqs, freqs], axis=-1)
            base = (half_idx + 0.4 * DIM_HEAD) / (1.4 * DIM_HEAD)
            power = (t - n // 2) / float(WINDOW // 2)
            scale = base[None, :] ** power[:, None]
            scale = jnp.concatenate([scale, scale], axis=-1)
            cos, sin = (jnp.cos(freqs), jnp.sin(freqs))
            q = q * cos * scale + rotate_half(q) * sin * scale
            k = k * cos / scale + rotate_half(k) * sin / scale
            return (q, k)

        def local_attention(q, k, v):
            b, h, n, d = q.shape
            w = n // WINDOW
            bq = q.reshape(b, h, w, WINDOW, d) * QK_SCALE
            bk = k.reshape(b, h, w, WINDOW, d)
            bv = v.reshape(b, h, w, WINDOW, d)

            def look_around(t):
                p = jnp.pad(t, ((0, 0), (0, 0), (1, 0), (0, 0), (0, 0)))
                return jnp.concatenate([p[:, :, :w], p[:, :, 1:]], axis=3)
            bk, bv = (look_around(bk), look_around(bv))
            bt = jnp.arange(n).reshape(w, WINDOW)
            btp = jnp.pad(bt, ((1, 0), (0, 0)), constant_values=-1)
            btk = jnp.concatenate([btp[:w], btp[1:]], axis=1)
            sim = jnp.einsum('bhwid,bhwjd->bhwij', bq, bk)
            i = bt[:, :, None]
            j = btk[:, None, :]
            mask = (i < j) | (i > j + WINDOW) | (j == -1)
            sim = jnp.where(mask, -jnp.finfo(sim.dtype).max, sim)
            attn = jax.nn.softmax(sim, axis=-1)
            out = jnp.einsum('bhwij,bhwjd->bhwid', attn, bv)
            return out.reshape(b, h, n, d)

        def _layer(x, wqkv, qs, ksc, wo, lg, lb, w1, b1, w2, b2):
            b, n, _ = x.shape
            h = shift_token(x)
            qkv = h @ wqkv
            q, k, v = jnp.split(qkv, 3, axis=-1)
            to_heads = lambda t: t.reshape(b, n, HEADS, DIM_HEAD).transpose(0, 2, 1, 3)
            q, k, v = (to_heads(q), to_heads(k), to_heads(v))
            q = l2norm(q) * qs
            k = l2norm(k) * ksc
            q, k = rotary_xpos(q, k)
            o = local_attention(q, k, v)
            o = o.transpose(0, 2, 1, 3).reshape(b, n, INNER)
            x = x + o @ wo
            h = shift_token(x)
            mu = h.mean(-1, keepdims=True)
            var = h.var(-1, keepdims=True)
            h = (h - mu) / jnp.sqrt(var + 1e-05) * lg + lb
            h = h @ w1 + b1
            a, g = jnp.split(h, 2, axis=-1)
            h = a * jax.nn.gelu(g, approximate=False)
            x = x + h @ w2 + b2
            return x
        key = jax.random.key(seed)
        ks = jax.random.split(key, 6)
        return {'x': jax.random.normal(ks[0], (B, N, DIM), jnp.float32), 'wqkv': jax.random.normal(ks[1], (DEPTH, DIM, 3 * INNER), jnp.float32) * 0.02, 'q_scale': jnp.ones((DEPTH, DIM_HEAD), jnp.float32), 'k_scale': jnp.ones((DEPTH, DIM_HEAD), jnp.float32), 'wo': jax.random.normal(ks[2], (DEPTH, INNER, DIM), jnp.float32) * 0.02, 'ln_g': jnp.ones((DEPTH, DIM), jnp.float32), 'ln_b': jnp.zeros((DEPTH, DIM), jnp.float32), 'w1': jax.random.normal(ks[3], (DEPTH, DIM, 2 * HID), jnp.float32) * 0.02, 'b1': jnp.zeros((DEPTH, 2 * HID), jnp.float32), 'w2': jax.random.normal(ks[4], (DEPTH, HID, DIM), jnp.float32) * 0.02, 'b2': jnp.zeros((DEPTH, DIM), jnp.float32)}
    _L2_ffn_in = _L2_ffn_setup()

    def _L3_attn_setup():
        import jax, jax.numpy as jnp
        import numpy as np
        B, T, D, C = (4, 512, 128, 64)
        key = jax.random.key(seed)
        k1, k2, k3 = jax.random.split(key, 3)
        scale = 1.0 / np.sqrt(D)
        return {'out': jax.random.normal(k1, (B, T, D), dtype=jnp.float32), 'W_write': jax.random.normal(k2, (D, D), dtype=jnp.float32) * scale, 'W_read': jax.random.normal(k3, (D, D), dtype=jnp.float32) * scale, 'decay': jnp.asarray(4.6, dtype=jnp.float32), 'log_alpha': jnp.asarray(np.log(0.03), dtype=jnp.float32)}
    _L3_attn_in = _L3_attn_setup()

    def _L3_ffn_setup():
        import jax, jax.numpy as jnp
        import numpy as np
        E, H, F, K = (8, 128, 256, 2)
        B, S = (2, 256)
        key = jax.random.key(seed)
        ks = jax.random.split(key, 8)

        def w(k, shape, fan_in):
            return jax.random.normal(k, shape, jnp.float32) / np.float32(np.sqrt(fan_in))
        return {'x': jax.random.normal(ks[0], (B, S, H), jnp.float32), 'Wgate': w(ks[1], (H, E), H), 'bgate': jnp.zeros((E,), jnp.float32), 'W1': w(ks[2], (E, H, F), H), 'b1': jnp.zeros((E, F), jnp.float32), 'W2': w(ks[3], (E, H, F), H), 'b2': jnp.zeros((E, F), jnp.float32), 'Wg': w(ks[4], (E, F, F), F), 'bg': jnp.zeros((E, F), jnp.float32), 'Wl': w(ks[5], (E, F, F), F), 'bl': jnp.zeros((E, F), jnp.float32), 'W3': w(ks[6], (E, F, H), F), 'b3': jnp.zeros((E, H), jnp.float32)}
    _L3_ffn_in = _L3_ffn_setup()
    _d = {'L0_attn_hidden_states': _L0_attn_in['hidden_states'], 'L0_attn_q_proj_w': _L0_attn_in['q_proj_w'], 'L0_attn_k_proj_w': _L0_attn_in['k_proj_w'], 'L0_attn_v_proj_w': _L0_attn_in['v_proj_w'], 'L0_attn_b_proj_w': _L0_attn_in['b_proj_w'], 'L0_attn_q_conv_w': _L0_attn_in['q_conv_w'], 'L0_attn_k_conv_w': _L0_attn_in['k_conv_w'], 'L0_attn_v_conv_w': _L0_attn_in['v_conv_w'], 'L0_attn_fir_short_w': _L0_attn_in['fir_short_w'], 'L0_attn_fir_long_w': _L0_attn_in['fir_long_w'], 'L0_attn_fuse_w1': _L0_attn_in['fuse_w1'], 'L0_attn_fuse_b1': _L0_attn_in['fuse_b1'], 'L0_attn_fuse_w2': _L0_attn_in['fuse_w2'], 'L0_attn_fuse_b2': _L0_attn_in['fuse_b2'], 'L0_attn_logit_temp': _L0_attn_in['logit_temp'], 'L0_attn_res_scale_short': _L0_attn_in['res_scale_short'], 'L0_attn_res_scale_long': _L0_attn_in['res_scale_long'], 'L0_attn_o_norm_w': _L0_attn_in['o_norm_w'], 'L0_attn_o_proj_w': _L0_attn_in['o_proj_w'], 'L0_ffn_Wr': _L0_ffn_in['Wr'], 'L0_ffn_br': _L0_ffn_in['br'], 'L0_ffn_W1': _L0_ffn_in['W1'], 'L0_ffn_W2': _L0_ffn_in['W2'], 'L1_attn_Wq': _L1_attn_in['Wq'], 'L1_attn_Wk': _L1_attn_in['Wk'], 'L1_attn_Wv': _L1_attn_in['Wv'], 'L1_attn_Wo': _L1_attn_in['Wo'], 'L1_attn_bo': _L1_attn_in['bo'], 'L1_attn_ln1_g': _L1_attn_in['ln1_g'], 'L1_attn_ln1_b': _L1_attn_in['ln1_b'], 'L1_attn_W1': _L1_attn_in['W1'], 'L1_attn_b1': _L1_attn_in['b1'], 'L1_attn_W2': _L1_attn_in['W2'], 'L1_attn_b2': _L1_attn_in['b2'], 'L1_attn_ln2_g': _L1_attn_in['ln2_g'], 'L1_attn_ln2_b': _L1_attn_in['ln2_b'], 'L1_ffn_gate_w': _L1_ffn_in['gate_w'], 'L1_ffn_ln_gamma': _L1_ffn_in['ln_gamma'], 'L1_ffn_ln_beta': _L1_ffn_in['ln_beta'], 'L1_ffn_fc1s': _L1_ffn_in['fc1s'], 'L1_ffn_b1s': _L1_ffn_in['b1s'], 'L1_ffn_fc2s': _L1_ffn_in['fc2s'], 'L1_ffn_b2s': _L1_ffn_in['b2s'], 'L2_attn_ln1_g': _L2_attn_in['ln1_g'], 'L2_attn_ln1_b': _L2_attn_in['ln1_b'], 'L2_attn_ln2_g': _L2_attn_in['ln2_g'], 'L2_attn_ln2_b': _L2_attn_in['ln2_b'], 'L2_attn_rms_in_w': _L2_attn_in['rms_in_w'], 'L2_attn_Wq': _L2_attn_in['Wq'], 'L2_attn_Wk': _L2_attn_in['Wk'], 'L2_attn_Wv': _L2_attn_in['Wv'], 'L2_attn_conv_q_w': _L2_attn_in['conv_q_w'], 'L2_attn_conv_k_w': _L2_attn_in['conv_k_w'], 'L2_attn_conv_v_w': _L2_attn_in['conv_v_w'], 'L2_attn_Wa': _L2_attn_in['Wa'], 'L2_attn_dt_bias': _L2_attn_in['dt_bias'], 'L2_attn_A_log': _L2_attn_in['A_log'], 'L2_attn_Wb': _L2_attn_in['Wb'], 'L2_attn_Wg': _L2_attn_in['Wg'], 'L2_attn_o_norm_w': _L2_attn_in['o_norm_w'], 'L2_attn_Wo': _L2_attn_in['Wo'], 'L2_attn_W2': _L2_attn_in['W2'], 'L2_attn_b2': _L2_attn_in['b2'], 'L2_ffn_wqkv': _L2_ffn_in['wqkv'], 'L2_ffn_q_scale': _L2_ffn_in['q_scale'], 'L2_ffn_k_scale': _L2_ffn_in['k_scale'], 'L2_ffn_wo': _L2_ffn_in['wo'], 'L2_ffn_ln_g': _L2_ffn_in['ln_g'], 'L2_ffn_ln_b': _L2_ffn_in['ln_b'], 'L2_ffn_w1': _L2_ffn_in['w1'], 'L2_ffn_b1': _L2_ffn_in['b1'], 'L2_ffn_w2': _L2_ffn_in['w2'], 'L2_ffn_b2': _L2_ffn_in['b2'], 'L3_attn_W_write': _L3_attn_in['W_write'], 'L3_attn_W_read': _L3_attn_in['W_read'], 'L3_attn_decay': _L3_attn_in['decay'], 'L3_attn_log_alpha': _L3_attn_in['log_alpha'], 'L3_ffn_Wgate': _L3_ffn_in['Wgate'], 'L3_ffn_bgate': _L3_ffn_in['bgate'], 'L3_ffn_W1': _L3_ffn_in['W1'], 'L3_ffn_b1': _L3_ffn_in['b1'], 'L3_ffn_W2': _L3_ffn_in['W2'], 'L3_ffn_b2': _L3_ffn_in['b2'], 'L3_ffn_Wg': _L3_ffn_in['Wg'], 'L3_ffn_bg': _L3_ffn_in['bg'], 'L3_ffn_Wl': _L3_ffn_in['Wl'], 'L3_ffn_bl': _L3_ffn_in['bl'], 'L3_ffn_W3': _L3_ffn_in['W3'], 'L3_ffn_b3': _L3_ffn_in['b3']}
    _x0 = _d['L0_attn_hidden_states']
    _d['L0_attn_hidden_states'] = jax.random.normal(jax.random.fold_in(jax.random.key(seed), 1), (8, 512, 128), dtype=_x0.dtype)
    del _x0
    return _d

def reference(L0_attn_hidden_states, L0_attn_q_proj_w, L0_attn_k_proj_w, L0_attn_v_proj_w, L0_attn_b_proj_w, L0_attn_q_conv_w, L0_attn_k_conv_w, L0_attn_v_conv_w, L0_attn_fir_short_w, L0_attn_fir_long_w, L0_attn_fuse_w1, L0_attn_fuse_b1, L0_attn_fuse_w2, L0_attn_fuse_b2, L0_attn_logit_temp, L0_attn_res_scale_short, L0_attn_res_scale_long, L0_attn_o_norm_w, L0_attn_o_proj_w, L0_ffn_Wr, L0_ffn_br, L0_ffn_W1, L0_ffn_W2, L1_attn_Wq, L1_attn_Wk, L1_attn_Wv, L1_attn_Wo, L1_attn_bo, L1_attn_ln1_g, L1_attn_ln1_b, L1_attn_W1, L1_attn_b1, L1_attn_W2, L1_attn_b2, L1_attn_ln2_g, L1_attn_ln2_b, L1_ffn_gate_w, L1_ffn_ln_gamma, L1_ffn_ln_beta, L1_ffn_fc1s, L1_ffn_b1s, L1_ffn_fc2s, L1_ffn_b2s, L2_attn_ln1_g, L2_attn_ln1_b, L2_attn_ln2_g, L2_attn_ln2_b, L2_attn_rms_in_w, L2_attn_Wq, L2_attn_Wk, L2_attn_Wv, L2_attn_conv_q_w, L2_attn_conv_k_w, L2_attn_conv_v_w, L2_attn_Wa, L2_attn_dt_bias, L2_attn_A_log, L2_attn_Wb, L2_attn_Wg, L2_attn_o_norm_w, L2_attn_Wo, L2_attn_W2, L2_attn_b2, L2_ffn_wqkv, L2_ffn_q_scale, L2_ffn_k_scale, L2_ffn_wo, L2_ffn_ln_g, L2_ffn_ln_b, L2_ffn_w1, L2_ffn_b1, L2_ffn_w2, L2_ffn_b2, L3_attn_W_write, L3_attn_W_read, L3_attn_decay, L3_attn_log_alpha, L3_ffn_Wgate, L3_ffn_bgate, L3_ffn_W1, L3_ffn_b1, L3_ffn_W2, L3_ffn_b2, L3_ffn_Wg, L3_ffn_bg, L3_ffn_Wl, L3_ffn_bl, L3_ffn_W3, L3_ffn_b3):

    def _L0_attn_ref(hidden_states, q_proj_w, k_proj_w, v_proj_w, b_proj_w, q_conv_w, k_conv_w, v_conv_w, fir_short_w, fir_long_w, fuse_w1, fuse_b1, fuse_w2, fuse_b2, logit_temp, res_scale_short, res_scale_long, o_norm_w, o_proj_w):
        import math
        import jax, jax.numpy as jnp
        import numpy as np
        CHUNK = 32
        EPS = 1e-05

        def l2norm(x):
            return x * jax.lax.rsqrt(jnp.sum(x * x, -1, keepdims=True))

        def causal_dwconv(x, w):
            C, K = w.shape
            return jax.lax.conv_general_dilated(x, w[:, None, :], (1,), [(K - 1, 0)], feature_group_count=C)

        def per_head_stats(x):
            mean = jnp.mean(x, -1, keepdims=True)
            var = jnp.mean(x * x, -1, keepdims=True) - mean * mean
            abs_mean = jnp.mean(jnp.abs(x), -1, keepdims=True)
            l2 = jnp.sqrt(jnp.sum(x * x, -1, keepdims=True))
            return jnp.concatenate([mean, var, abs_mean, l2], -1)

        def delta_rule_chunkwise(q, k, v, beta, chunk=CHUNK):
            b, h, L, dk = q.shape
            dv = v.shape[-1]
            pad = -L % chunk
            if pad:
                pc = ((0, 0), (0, 0), (0, pad), (0, 0))
                q, k, v = (jnp.pad(t, pc) for t in (q, k, v))
                beta = jnp.pad(beta, ((0, 0), (0, 0), (0, pad)))
            Lp = L + pad
            n = Lp // chunk
            q = l2norm(q)
            k = l2norm(k)
            v = v * beta[..., None]
            kb = k * beta[..., None]
            resh = lambda t: t.reshape(b, h, n, chunk, t.shape[-1])
            q, k, v, kb = map(resh, (q, k, v, kb))
            tri = jnp.triu(jnp.ones((chunk, chunk), bool))
            strict = jnp.triu(jnp.ones((chunk, chunk), bool), 1)
            A = jnp.where(tri, 0.0, -jnp.einsum('bhncd,bhned->bhnce', kb, k))
            for i in range(1, chunk):
                upd = jnp.einsum('...k,...kj->...j', A[..., i, :], A[..., :, :i])
                A = A.at[..., i, :i].add(upd)
            inv = A + jnp.eye(chunk, dtype=A.dtype)
            u = inv @ v
            w = inv @ kb

            def step(S, xs):
                qi, ki, ui, wi = xs
                attn = jnp.where(strict, 0.0, qi @ jnp.swapaxes(ki, -1, -2))
                u_adj = ui - wi @ S
                out_i = qi @ S + attn @ u_adj
                S = S + jnp.swapaxes(ki, -1, -2) @ u_adj
                return (S, out_i)
            xs = tuple((jnp.moveaxis(t, 2, 0) for t in (q, k, u, w)))
            S0 = jnp.zeros((b, h, dk, dv), q.dtype)
            S, outs = jax.lax.scan(step, S0, xs)
            out = jnp.moveaxis(outs, 0, 2).reshape(b, h, Lp, dv)[:, :, :L]
            return (out, S)
        B, L, D = hidden_states.shape
        H = fir_short_w.shape[0]

        def shortconv(x, w):
            y = causal_dwconv(jnp.swapaxes(x, 1, 2), w)
            return jax.nn.silu(jnp.swapaxes(y, 1, 2))
        q = shortconv(hidden_states @ q_proj_w.T, q_conv_w)
        k = shortconv(hidden_states @ k_proj_w.T, k_conv_w)
        v = shortconv(hidden_states @ v_proj_w.T, v_conv_w)
        q = q.reshape(B, L, H, -1)
        k = k.reshape(B, L, H, -1)
        v_direct = v.reshape(B, L, H, -1)
        beta = jax.nn.sigmoid(hidden_states @ b_proj_w.T)
        delta_out, _S = delta_rule_chunkwise(jnp.transpose(q, (0, 2, 1, 3)), jnp.transpose(k, (0, 2, 1, 3)), jnp.transpose(v_direct, (0, 2, 1, 3)), jnp.transpose(beta, (0, 2, 1)))
        delta_out = jnp.transpose(delta_out, (0, 2, 1, 3))

        def fir(x, filt):
            hh, dd, kk = filt.shape
            xf = jnp.swapaxes(x.reshape(B, L, hh * dd), 1, 2)
            y = causal_dwconv(xf, filt.reshape(hh * dd, kk))
            return jnp.swapaxes(y, 1, 2).reshape(B, L, hh, dd)
        local_short = fir(v_direct, fir_short_w)
        local_long = fir(v_direct, fir_long_w)
        stats = jnp.concatenate([per_head_stats(t) for t in (local_short, local_long, delta_out, v_direct)], -1)
        hs_exp = jnp.broadcast_to(hidden_states[:, :, None, :], (B, L, H, D))
        gate_in = jnp.concatenate([hs_exp, stats], -1)
        hdn = jax.nn.gelu(gate_in @ fuse_w1.T + fuse_b1, approximate=False)
        logits = hdn @ fuse_w2.T + fuse_b2
        temp = jax.nn.softplus(logit_temp) + 0.0001
        fw = jax.nn.softmax(logits / temp, -1)
        o = fw[..., 0:1] * local_short + fw[..., 1:2] * local_long + fw[..., 2:3] * delta_out + fw[..., 3:4] * v_direct
        o = o + res_scale_short * local_short + res_scale_long * local_long
        o = o * jax.lax.rsqrt(jnp.mean(o * o, -1, keepdims=True) + EPS) * o_norm_w
        return o.reshape(B, L, -1) @ o_proj_w.T

    def _L0_ffn_ref(hidden_states, Wr, br, W1, W2):
        import jax, jax.numpy as jnp
        import numpy as np
        B, S, H, FFN, E = (2, 256, 128, 512, 8)
        b, s, h = hidden_states.shape
        x = hidden_states.reshape(-1, h)
        route = jax.nn.sigmoid(x @ Wr + br)
        max_prob = jnp.max(route, axis=1, keepdims=True)
        max_ind = jnp.argmax(route, axis=1)
        out = jnp.zeros_like(x)
        n_experts = Wr.shape[1]
        for e in range(n_experts):
            mask = (max_ind == e)[:, None].astype(x.dtype)
            y = jax.nn.gelu(x @ W1[e], approximate=False) @ W2[e]
            out = out + mask * y
        out = out * max_prob
        return out.reshape(b, s, h)

    def _L1_attn_ref(x, Wq, Wk, Wv, Wo, bo, ln1_g, ln1_b, W1, b1, W2, b2, ln2_g, ln2_b):
        import jax, jax.numpy as jnp
        import numpy as np
        B, T, DIM = (2, 512, 128)
        DEPTH, HEADS = (4, 8)
        DH = DIM // HEADS
        NLOCAL, WINDOW, BUCKET = (4, 128, 64)
        MULT = 4

        def layer_norm(x, g, b, eps=1e-05):
            m = jnp.mean(x, -1, keepdims=True)
            v = jnp.mean(jnp.square(x - m), -1, keepdims=True)
            return (x - m) * jax.lax.rsqrt(v + eps) * g + b

        def causal_linear_attn(q, k, v):
            b, h, n, e = q.shape
            u = n // BUCKET
            q = jax.nn.softmax(q, axis=-1)
            k = jax.nn.elu(k) + 1.0
            bq = q.reshape(b, h, u, BUCKET, e)
            bk = k.reshape(b, h, u, BUCKET, e)
            bv = v.reshape(b, h, u, BUCKET, e)
            k_cum = jnp.cumsum(bk.sum(axis=-2), axis=-2)
            ctx = jnp.einsum('bhund,bhune->bhude', bk, bv)
            ctx = jnp.cumsum(ctx, axis=2)
            ctx = ctx / (k_cum[..., None] + 1e-06)
            ctx = jnp.pad(ctx, ((0, 0), (0, 0), (1, 0), (0, 0), (0, 0)))[:, :, :-1]
            out = jnp.einsum('bhund,bhude->bhune', bq, ctx)
            return out.reshape(b, h, n, e)

        def local_attn(q, k, v):
            b, lh, t, e = q.shape
            bh = b * lh
            nb = t // WINDOW
            bq = q.reshape(bh, nb, WINDOW, e)
            bk = k.reshape(bh, nb, WINDOW, e)
            bv = v.reshape(bh, nb, WINDOW, e)

            def look_around(x):
                padded = jnp.pad(x, ((0, 0), (1, 0), (0, 0), (0, 0)))
                return jnp.concatenate([padded[:, :-1], padded[:, 1:]], axis=2)
            bk2 = look_around(bk)
            bv2 = look_around(bv)
            tix = jnp.arange(t).reshape(1, nb, WINDOW)
            tpad = jnp.pad(tix, ((0, 0), (1, 0), (0, 0)), constant_values=-1)
            kix = jnp.concatenate([tpad[:, :-1], tpad[:, 1:]], axis=2)
            dots = jnp.einsum('bwie,bwje->bwij', bq, bk2) * e ** (-0.5)
            mask_value = -jnp.finfo(dots.dtype).max
            causal_mask = tix[:, :, :, None] < kix[:, :, None, :]
            pad_mask = (kix == -1)[:, :, None, :]
            dots = jnp.where(causal_mask | pad_mask, mask_value, dots)
            attn = jax.nn.softmax(dots, axis=-1)
            out = jnp.einsum('bwij,bwje->bwie', attn, bv2)
            return out.reshape(b, lh, t, e)

        def self_attention(x, Wq, Wk, Wv, Wo, bo):
            b, t, _ = x.shape
            mh = lambda z: z.reshape(b, t, HEADS, DH).transpose(0, 2, 1, 3)
            q, k, v = (mh(x @ Wq), mh(x @ Wk), mh(x @ Wv))
            lo = local_attn(q[:, :NLOCAL], k[:, :NLOCAL], v[:, :NLOCAL])
            go = causal_linear_attn(q[:, NLOCAL:], k[:, NLOCAL:], v[:, NLOCAL:])
            out = jnp.concatenate([lo, go], axis=1)
            out = out.transpose(0, 2, 1, 3).reshape(b, t, DIM)
            return out @ Wo + bo
        for i in range(DEPTH):
            x = x + self_attention(layer_norm(x, ln1_g[i], ln1_b[i]), Wq[i], Wk[i], Wv[i], Wo[i], bo[i])
            h = layer_norm(x, ln2_g[i], ln2_b[i])
            x = x + (jax.nn.gelu(h @ W1[i] + b1[i], approximate=False) @ W2[i] + b2[i])
        return x

    def _L1_ffn_ref(x, gate_w, ln_gamma, ln_beta, fc1s, b1s, fc2s, b2s):
        import jax, jax.numpy as jnp
        import numpy as np
        EMBED_DIM = 128
        MLP_RATIO = 4
        NUM_EXPERTS = 8
        CAPACITY = 1.0
        LN_EPS = 1e-05

        def _layernorm(y, gamma, beta):
            mu = jnp.mean(y, axis=-1, keepdims=True)
            var = jnp.mean(jnp.square(y - mu), axis=-1, keepdims=True)
            return (y - mu) * jax.lax.rsqrt(var + LN_EPS) * gamma + beta
        og_shape = x.shape
        d = og_shape[-1]
        xf = x.reshape(-1, d)
        bs = xf.shape[0]
        n = gate_w.shape[0]
        k = int(bs * CAPACITY) // n
        scores = xf @ gate_w.T
        scores = (jnp.tanh(scores) + 1.0) * 0.5
        vals, idx = jax.lax.top_k(scores.T, k)
        kept_w = vals.T
        flat_idx = idx.T.reshape(-1)
        y = xf[flat_idx].reshape(k, n, d)
        y = _layernorm(y, ln_gamma, ln_beta)
        h = jnp.einsum('knd,nfd->knf', y, fc1s) + b1s
        h = jax.nn.gelu(h, approximate=True)
        o = jnp.einsum('knf,ndf->knd', h, fc2s) + b2s
        o = o * kept_w[:, :, None]
        out = xf.at[flat_idx].add(o.reshape(k * n, d))
        return out.reshape(og_shape)

    def _L2_attn_ref(x, ln1_g, ln1_b, ln2_g, ln2_b, rms_in_w, Wq, Wk, Wv, conv_q_w, conv_k_w, conv_v_w, Wa, dt_bias, A_log, Wb, Wg, o_norm_w, Wo, W2, b2):
        import jax, jax.numpy as jnp
        import numpy as np
        B, T, D = (4, 256, 128)
        H, Kd = (4, 32)
        Vd = 64
        KEY_DIM, VAL_DIM = (H * Kd, H * Vd)
        CONV = 4
        EPS = 1e-06
        LN_EPS = 1e-05

        def _layernorm(x, g, b):
            m = jnp.mean(x, -1, keepdims=True)
            v = jnp.mean((x - m) ** 2, -1, keepdims=True)
            return (x - m) * jax.lax.rsqrt(v + LN_EPS) * g + b

        def _rmsnorm(x, w):
            return x * jax.lax.rsqrt(jnp.mean(x * x, -1, keepdims=True) + EPS) * w

        def _l2norm(x):
            return x * jax.lax.rsqrt(jnp.sum(x * x, -1, keepdims=True) + EPS)

        def _causal_conv_silu(x, w):
            t = x.shape[1]
            xp = jnp.pad(x, ((0, 0), (CONV - 1, 0), (0, 0)))
            y = xp[:, 0:t, :] * w[:, 0]
            for i in range(1, CONV):
                y = y + xp[:, i:i + t, :] * w[:, i]
            return jax.nn.silu(y)

        def _gated_delta_rule(q, k, v, g, beta):
            qT = jnp.moveaxis(q, 1, 0)
            kT = jnp.moveaxis(k, 1, 0)
            vT = jnp.moveaxis(v, 1, 0)
            gT = jnp.moveaxis(g, 1, 0)
            bT = jnp.moveaxis(beta, 1, 0)
            S0 = jnp.zeros((q.shape[0], H, Kd, Vd), q.dtype)

            def step(S, inp):
                q_t, k_t, v_t, g_t, b_t = inp
                S = S * jnp.exp(g_t)[..., None, None]
                kv = jnp.einsum('bhk,bhkv->bhv', k_t, S)
                delta = (v_t - kv) * b_t[..., None]
                S = S + k_t[..., :, None] * delta[..., None, :]
                o = jnp.einsum('bhk,bhkv->bhv', q_t, S)
                return (S, o)
            _, o = jax.lax.scan(step, S0, (qT, kT, vT, gT, bT))
            return jnp.moveaxis(o, 0, 1)

        def _forward(x, ln1_g, ln1_b, ln2_g, ln2_b, rms_in_w, Wq, Wk, Wv, conv_q_w, conv_k_w, conv_v_w, Wa, dt_bias, A_log, Wb, Wg, o_norm_w, Wo, W2, b2):
            b, t, _ = x.shape
            h = _layernorm(x, ln1_g, ln1_b)
            h = _rmsnorm(h, rms_in_w)
            q = _causal_conv_silu(h @ Wq, conv_q_w).reshape(b, t, H, Kd)
            k = _causal_conv_silu(h @ Wk, conv_k_w).reshape(b, t, H, Kd)
            v = _causal_conv_silu(h @ Wv, conv_v_w).reshape(b, t, H, Vd)
            q = _l2norm(q) * Kd ** (-0.5)
            k = _l2norm(k)
            g = -jnp.exp(A_log) * jax.nn.softplus(h @ Wa + dt_bias)
            beta = jax.nn.sigmoid(h @ Wb)
            o = _gated_delta_rule(q, k, v, g, beta)
            gate = (h @ Wg).reshape(b, t, H, Vd)
            o = _rmsnorm(o, o_norm_w) * jax.nn.silu(gate)
            enc = o.reshape(b, t, VAL_DIM) @ Wo
            x = x + enc
            h2 = _layernorm(x, ln2_g, ln2_b)
            x_out = jax.nn.gelu(h2 @ W2 + b2, approximate=False) + x
            return x_out
        return _forward(x, ln1_g, ln1_b, ln2_g, ln2_b, rms_in_w, Wq, Wk, Wv, conv_q_w, conv_k_w, conv_v_w, Wa, dt_bias, A_log, Wb, Wg, o_norm_w, Wo, W2, b2)

    def _L2_ffn_ref(x, wqkv, q_scale, k_scale, wo, ln_g, ln_b, w1, b1, w2, b2):
        import jax, jax.numpy as jnp
        import numpy as np
        DIM = 128
        DEPTH = 2
        HEADS = 8
        DIM_HEAD = 64
        WINDOW = 64
        INNER = HEADS * DIM_HEAD
        HID = int(DIM * 4 * 2 / 3)
        B, N = (2, 1024)
        QK_SCALE = 8.0

        def shift_token(t):
            t1, t2 = jnp.split(t, 2, axis=-1)
            t2 = jnp.pad(t2, ((0, 0), (1, 0), (0, 0)))[:, :-1]
            return jnp.concatenate([t1, t2], axis=-1)

        def l2norm(t):
            return t / jnp.clip(jnp.linalg.norm(t, axis=-1, keepdims=True), 1e-12)

        def rotate_half(x):
            x1, x2 = jnp.split(x, 2, axis=-1)
            return jnp.concatenate([-x2, x1], axis=-1)

        def rotary_xpos(q, k):
            n = q.shape[-2]
            half_idx = jnp.arange(0, DIM_HEAD, 2, dtype=jnp.float32)
            inv_freq = 1.0 / 10000.0 ** (half_idx / DIM_HEAD)
            t = jnp.arange(n, dtype=jnp.float32)
            freqs = t[:, None] * inv_freq[None, :]
            freqs = jnp.concatenate([freqs, freqs], axis=-1)
            base = (half_idx + 0.4 * DIM_HEAD) / (1.4 * DIM_HEAD)
            power = (t - n // 2) / float(WINDOW // 2)
            scale = base[None, :] ** power[:, None]
            scale = jnp.concatenate([scale, scale], axis=-1)
            cos, sin = (jnp.cos(freqs), jnp.sin(freqs))
            q = q * cos * scale + rotate_half(q) * sin * scale
            k = k * cos / scale + rotate_half(k) * sin / scale
            return (q, k)

        def local_attention(q, k, v):
            b, h, n, d = q.shape
            w = n // WINDOW
            bq = q.reshape(b, h, w, WINDOW, d) * QK_SCALE
            bk = k.reshape(b, h, w, WINDOW, d)
            bv = v.reshape(b, h, w, WINDOW, d)

            def look_around(t):
                p = jnp.pad(t, ((0, 0), (0, 0), (1, 0), (0, 0), (0, 0)))
                return jnp.concatenate([p[:, :, :w], p[:, :, 1:]], axis=3)
            bk, bv = (look_around(bk), look_around(bv))
            bt = jnp.arange(n).reshape(w, WINDOW)
            btp = jnp.pad(bt, ((1, 0), (0, 0)), constant_values=-1)
            btk = jnp.concatenate([btp[:w], btp[1:]], axis=1)
            sim = jnp.einsum('bhwid,bhwjd->bhwij', bq, bk)
            i = bt[:, :, None]
            j = btk[:, None, :]
            mask = (i < j) | (i > j + WINDOW) | (j == -1)
            sim = jnp.where(mask, -jnp.finfo(sim.dtype).max, sim)
            attn = jax.nn.softmax(sim, axis=-1)
            out = jnp.einsum('bhwij,bhwjd->bhwid', attn, bv)
            return out.reshape(b, h, n, d)

        def _layer(x, wqkv, qs, ksc, wo, lg, lb, w1, b1, w2, b2):
            b, n, _ = x.shape
            h = shift_token(x)
            qkv = h @ wqkv
            q, k, v = jnp.split(qkv, 3, axis=-1)
            to_heads = lambda t: t.reshape(b, n, HEADS, DIM_HEAD).transpose(0, 2, 1, 3)
            q, k, v = (to_heads(q), to_heads(k), to_heads(v))
            q = l2norm(q) * qs
            k = l2norm(k) * ksc
            q, k = rotary_xpos(q, k)
            o = local_attention(q, k, v)
            o = o.transpose(0, 2, 1, 3).reshape(b, n, INNER)
            x = x + o @ wo
            h = shift_token(x)
            mu = h.mean(-1, keepdims=True)
            var = h.var(-1, keepdims=True)
            h = (h - mu) / jnp.sqrt(var + 1e-05) * lg + lb
            h = h @ w1 + b1
            a, g = jnp.split(h, 2, axis=-1)
            h = a * jax.nn.gelu(g, approximate=False)
            x = x + h @ w2 + b2
            return x
        for l in range(DEPTH):
            x = _layer(x, wqkv[l], q_scale[l], k_scale[l], wo[l], ln_g[l], ln_b[l], w1[l], b1[l], w2[l], b2[l])
        return x

    def _L3_attn_ref(out, W_write, W_read, decay, log_alpha):
        import jax, jax.numpy as jnp
        import numpy as np
        B, T, D, C = (4, 512, 128, 64)
        Bq, Tq, Dq = out.shape
        n_chunks = Tq // C
        out32 = out.astype(jnp.float32)
        gamma = jax.nn.sigmoid(decay)
        log_gamma = jnp.log(gamma)
        v = jnp.einsum('btd,ed->bte', out32, W_write)
        wk = jnp.pad(out32[:, :-1], ((0, 0), (1, 0), (0, 0)))
        rk = out32

        def to_chunks(x):
            return x.reshape(Bq, n_chunks, C, Dq).transpose(1, 0, 2, 3)
        rk_ch, wk_ch, v_ch = (to_chunks(rk), to_chunks(wk), to_chunks(v))
        p = jnp.arange(C)
        diffs = jnp.clip(p[:, None] - 1 - p[None, :], 0)
        causal = p[:, None] > p[None, :]
        M = jnp.exp(diffs.astype(jnp.float32) * log_gamma) * causal
        gp = gamma ** p
        gw = gamma ** (C - 1 - p)
        gC = gamma ** C

        def step(W, xs):
            rk_c, wk_c, v_c = xs
            inter = jnp.einsum('bij,bcj->bci', W, rk_c) * gp[None, :, None]
            S = jnp.einsum('bcd,bkd->bck', rk_c, wk_c)
            intra = jnp.einsum('bck,bkd->bcd', S * M, v_c)
            reads = inter + intra
            W = gC * W + jnp.einsum('bcd,bce->bde', v_c * gw[None, :, None], wk_c)
            return (W, reads)
        W0 = jnp.zeros((Bq, Dq, Dq), dtype=jnp.float32)
        _, reads = jax.lax.scan(step, W0, (rk_ch, wk_ch, v_ch))
        reads = reads.transpose(1, 0, 2, 3).reshape(Bq, Tq, Dq)
        alpha = jnp.exp(log_alpha)
        read_out = jnp.einsum('btd,ed->bte', reads, W_read)
        return out + alpha * read_out.astype(out.dtype)

    def _L3_ffn_ref(x, Wgate, bgate, W1, b1, W2, b2, Wg, bg, Wl, bl, W3, b3):
        import jax, jax.numpy as jnp
        import numpy as np
        E, H, F, K = (8, 128, 256, 2)
        B, S = (2, 256)
        gout = x @ Wgate + bgate
        topv, topi = jax.lax.top_k(gout, K)
        topw = jax.nn.softmax(topv, axis=-1)
        combine = jnp.sum(jax.nn.one_hot(topi, E, dtype=x.dtype) * topw[..., None], axis=-2)
        x1 = jnp.einsum('bsh,ehf->bsef', x, W1) + b1
        x2 = jnp.einsum('bsh,ehf->bsef', x, W2) + b2
        z = x1 * x2
        g = jnp.einsum('bsef,efg->bseg', z, Wg) + bg
        o = g * jax.nn.sigmoid(g) * (jnp.einsum('bsef,efg->bseg', z, Wl) + bl)
        y = jnp.einsum('bsef,efh->bseh', o, W3) + b3
        return jnp.einsum('bse,bseh->bsh', combine, y)
    x = L0_attn_hidden_states
    x = x + _L0_attn_ref(_layernorm(x, axis=-1), L0_attn_q_proj_w, L0_attn_k_proj_w, L0_attn_v_proj_w, L0_attn_b_proj_w, L0_attn_q_conv_w, L0_attn_k_conv_w, L0_attn_v_conv_w, L0_attn_fir_short_w, L0_attn_fir_long_w, L0_attn_fuse_w1, L0_attn_fuse_b1, L0_attn_fuse_w2, L0_attn_fuse_b2, L0_attn_logit_temp, L0_attn_res_scale_short, L0_attn_res_scale_long, L0_attn_o_norm_w, L0_attn_o_proj_w)
    x = x + _L0_ffn_ref(_layernorm(x, axis=-1), L0_ffn_Wr, L0_ffn_br, L0_ffn_W1, L0_ffn_W2)
    x = x + _L1_attn_ref(_layernorm(x, axis=-1), L1_attn_Wq, L1_attn_Wk, L1_attn_Wv, L1_attn_Wo, L1_attn_bo, L1_attn_ln1_g, L1_attn_ln1_b, L1_attn_W1, L1_attn_b1, L1_attn_W2, L1_attn_b2, L1_attn_ln2_g, L1_attn_ln2_b)
    x = x + _L1_ffn_ref(_layernorm(x, axis=-1), L1_ffn_gate_w, L1_ffn_ln_gamma, L1_ffn_ln_beta, L1_ffn_fc1s, L1_ffn_b1s, L1_ffn_fc2s, L1_ffn_b2s)
    x = x + _L2_attn_ref(_layernorm(x, axis=-1), L2_attn_ln1_g, L2_attn_ln1_b, L2_attn_ln2_g, L2_attn_ln2_b, L2_attn_rms_in_w, L2_attn_Wq, L2_attn_Wk, L2_attn_Wv, L2_attn_conv_q_w, L2_attn_conv_k_w, L2_attn_conv_v_w, L2_attn_Wa, L2_attn_dt_bias, L2_attn_A_log, L2_attn_Wb, L2_attn_Wg, L2_attn_o_norm_w, L2_attn_Wo, L2_attn_W2, L2_attn_b2)
    x = x + _L2_ffn_ref(_layernorm(x, axis=-1), L2_ffn_wqkv, L2_ffn_q_scale, L2_ffn_k_scale, L2_ffn_wo, L2_ffn_ln_g, L2_ffn_ln_b, L2_ffn_w1, L2_ffn_b1, L2_ffn_w2, L2_ffn_b2)
    x = x + _L3_attn_ref(_layernorm(x, axis=-1), L3_attn_W_write, L3_attn_W_read, L3_attn_decay, L3_attn_log_alpha)
    x = x + _L3_ffn_ref(_layernorm(x, axis=-1), L3_ffn_Wgate, L3_ffn_bgate, L3_ffn_W1, L3_ffn_b1, L3_ffn_W2, L3_ffn_b2, L3_ffn_Wg, L3_ffn_bg, L3_ffn_Wl, L3_ffn_bl, L3_ffn_W3, L3_ffn_b3)
    return x

_drawn_inputs = setup_inputs


def setup_inputs(seed=0):
    import zlib

    import numpy as np

    out = dict(_drawn_inputs(seed))
    spreads = {'L0_attn_fuse_b1': (0.0, 0.8),
     'L0_attn_o_norm_w': (1.0, 0.2),
     'L0_ffn_br': (0.0, 0.1),
     'L1_attn_bo': (0.0, 0.1),
     'L1_attn_ln1_g': (1.0, 0.6),
     'L1_attn_ln1_b': (0.0, 0.656),
     'L1_attn_b1': (0.0, 0.1),
     'L1_attn_b2': (0.0, 0.1),
     'L1_attn_ln2_g': (1.0, 0.6),
     'L1_attn_ln2_b': (0.0, 0.519),
     'L1_ffn_ln_gamma': (1.0, 0.2),
     'L1_ffn_ln_beta': (0.0, 0.439),
     'L2_attn_ln1_g': (1.0, 0.6),
     'L2_attn_ln1_b': (0.0, 0.8),
     'L2_attn_ln2_g': (1.0, 0.6),
     'L2_attn_ln2_b': (0.0, 0.8),
     'L2_attn_rms_in_w': (1.0, 0.6),
     'L2_attn_o_norm_w': (1.0, 0.6),
     'L2_attn_b2': (0.0, 0.321),
     'L2_ffn_q_scale': (1.0, 0.6),
     'L2_ffn_k_scale': (1.0, 0.6),
     'L2_ffn_ln_g': (1.0, 0.6),
     'L2_ffn_ln_b': (0.0, 0.8),
     'L2_ffn_b1': (0.0, 0.8),
     'L2_ffn_b2': (0.0, 0.1),
     'L3_ffn_bgate': (0.0, 0.494),
     'L3_ffn_b1': (0.0, 0.8),
     'L3_ffn_b2': (0.0, 0.8),
     'L3_ffn_bg': (0.0, 0.8),
     'L3_ffn_bl': (0.0, 0.8),
     'L3_ffn_b3': (0.0, 0.7)}
    factors = {'L0_attn_q_proj_w': 3.161,
     'L0_attn_k_proj_w': 3.213,
     'L0_attn_b_proj_w': 7.679,
     'L0_attn_q_conv_w': 3.351,
     'L0_attn_k_conv_w': 3.194,
     'L0_attn_fir_short_w': 8.0,
     'L0_attn_fir_long_w': 5.637,
     'L0_attn_fuse_w1': 8.0,
     'L0_attn_fuse_w2': 8.0,
     'L1_attn_Wq': 8.0,
     'L1_attn_Wk': 8.0,
     'L1_attn_Wv': 2.966,
     'L1_ffn_b1s': 8.0,
     'L1_ffn_b2s': 8.0,
     'L2_attn_Wq': 7.44,
     'L2_attn_Wk': 7.612,
     'L2_attn_Wv': 7.461,
     'L2_attn_conv_q_w': 7.443,
     'L2_attn_conv_k_w': 7.339,
     'L2_attn_conv_v_w': 7.44,
     'L2_attn_Wa': 8.0,
     'L2_attn_dt_bias': 8.0,
     'L2_attn_A_log': 8.0,
     'L2_attn_Wb': 8.0,
     'L2_attn_Wg': 7.474,
     'L2_attn_Wo': 7.426,
     'L2_ffn_wqkv': 5.082,
     'L2_ffn_wo': 4.864,
     'L2_ffn_w1': 8.0,
     'L2_ffn_w2': 8.0}
    for name, (base, spread) in spreads.items():
        noise = np.random.default_rng([zlib.crc32(name.encode()), seed]).standard_normal(out[name].shape)
        drawn = base * np.exp(spread * noise) if base else spread * noise
        out[name] = jnp.asarray(drawn.astype(out[name].dtype))
    for name, factor in factors.items():
        out[name] = (out[name] * factor).astype(out[name].dtype)
    return out
```

```python
from contextlib import ExitStack



import numpy as np
import concourse.bass as bass
from concourse import mybir

F32 = mybir.dt.float32
ALU = mybir.AluOpType
ACT = mybir.ActivationFunctionType
AX = mybir.AxisListType.X
ds = bass.ds

P = 128
BATCH, SEQ, DIM = 8, 512, 128
TILES = SEQ // P
BANK = 512
LN_EPS = 1e-5


class At:

    def __init__(self, view):
        self.view = view


class Token:

    def __init__(self, producer, k):
        self.producer, self.k = producer, k


class Program:

    CHANNELS = 3

    def __init__(self, nc, ctx):
        self.nc = nc
        self.handle = {"PE": nc.tensor, "DVE": nc.vector, "ACT": nc.scalar, "POOL": nc.gpsimd, "SP": nc.sync}
        self.producers = ["PE", "DVE", "ACT", "POOL"] + [f"DMA{c}" for c in range(self.CHANNELS)]
        self.sem = {p: ctx.enter_context(nc.semaphore(f"done_{p}")) for p in self.producers}
        self.unit = {p: 16 if p.startswith("DMA") else 1 for p in self.producers}
        self.base = {p: 0 for p in self.producers}
        self.weights_sem = [ctx.enter_context(nc.semaphore(f"weights_landed_{side}")) for side in range(2)]
        self.loads = 0
        self.banks = [ctx.enter_context(nc.psum_tensor(f"bank{b}", [P, BANK], F32)) for b in range(8)]


    def prefetch(self, dst, src):
        for p in self.producers:
            self.nc.sync.wait_ge(self.sem[p], self.base[p] * self.unit[p])
        self.nc.sync.dma_start(dst, src).then_inc(self.weights_sem[self.loads % 2], 16)
        self.loads += 1

    def weights_landed(self):
        for engine in ("PE", "DVE", "ACT", "POOL"):
            self.handle[engine].wait_ge(self.weights_sem[(self.loads - 1) % 2], 16 * ((self.loads + 1) // 2))


class Section:

    def __init__(self, program, name):
        self.pr, self.name = program, name
        self.queue = {e: [] for e in program.handle}
        self.count = {p: 0 for p in program.producers}

    def _put(self, issuer, producer, fn, args, kw, after, link, signal):
        waits = [t for t in after if t is not None]
        if link and self.count[producer]:
            waits = waits + [Token(producer, self.count[producer])]
        if signal:
            self.count[producer] += 1
        self.queue[issuer].append((waits, fn, args, kw, producer if signal else None))
        return Token(producer, self.count[producer]) if signal else None

    def dve(self, fn, *args, after=(), link=True, **kw):
        return self._put("DVE", "DVE", fn, args, kw, after, link, True)

    def act(self, fn, *args, after=(), link=False, **kw):
        return self._put("ACT", "ACT", fn, args, kw, after, link, True)

    def pool(self, fn, *args, after=(), link=True, **kw):
        return self._put("POOL", "POOL", fn, args, kw, after, link, True)

    def mm(self, out, lhsT, rhs, start=True, stop=True, after=(), signal=True):
        return self._put("PE", "PE", self.pr.nc.tensor.matmul, (out, lhsT, rhs), dict(start=start, stop=stop),
                         after, False, signal)

    def tr(self, out, in_, ident, after=(), signal=True):
        return self._put("PE", "PE", self.pr.nc.tensor.transpose, (out, in_, ident), {}, after, False, signal)

    def dma(self, channel, out, in_, after=()):
        return self._put("SP", f"DMA{channel}", self.pr.nc.sync.dma_start, (out, in_), {}, after, False, True)

    def emit(self, outer=1, inner=1):
        pr, nc = self.pr, self.pr.nc
        engine_types = {"PE": mybir.EngineType.PE, "DVE": mybir.EngineType.DVE, "ACT": mybir.EngineType.Activation,
                        "POOL": mybir.EngineType.Pool, "SP": mybir.EngineType.SP}

        def run(o, i):
            turn = o * inner + i

            def value(producer, k):
                n = self.count[producer]
                v = pr.base[producer] + k
                return (v + turn * n) * pr.unit[producer] if n else v * pr.unit[producer]

            for issuer, items in self.queue.items():
                if not items:
                    continue
                handle = pr.handle[issuer]
                for p in pr.producers:
                    if pr.base[p] or self.count[p]:
                        handle.wait_ge(pr.sem[p], value(p, 0))
                waited = {}
                for waits, fn, args, kw, producer in items:
                    for t in waits:
                        if waited.get(t.producer, 0) < t.k:
                            handle.wait_ge(pr.sem[t.producer], value(t.producer, t.k))
                            waited[t.producer] = t.k
                    put = [a.view(o, i) if isinstance(a, At) else a for a in args]
                    ins = fn(*put, **kw)
                    if producer:
                        ins.then_inc(pr.sem[producer], pr.unit[producer])

        engines = tuple(engine_types[e] for e in self.queue if self.queue[e])
        if outer == 1 and inner == 1:
            run(0, 0)
        elif outer == 1:
            with nc.Fori(0, inner, engines=engines) as i:
                run(0, i)
        else:
            with nc.Fori(0, outer, engines=engines) as o:
                with nc.Fori(0, inner, engines=engines) as i:
                    run(o, i)
        for p in pr.producers:
            pr.base[p] += self.count[p] * outer * inner


class Ring:

    def __init__(self, items):
        self.items, self.free, self.n, self.held = items, [()] * len(items), 0, set()

    def take(self):
        k = self.n % len(self.items)
        self.n += 1
        assert k not in self.held, "taken again before it was given back"
        self.held.add(k)
        return self.items[k], self.free[k], k

    def give(self, k, *readers):
        self.free[k] = readers
        self.held.discard(k)


class Arena:

    def __init__(self, tensor, columns):
        self.tensor, self.columns, self.at = tensor, columns, 0

    def take(self, *shape):
        n = int(np.prod(shape))
        assert self.at + n <= self.columns, (self.at + n, self.columns)
        v = self.tensor[:, self.at:self.at + n]
        self.at += n
        if len(shape) > 1:
            names = "abcd"[:len(shape)]
            v = v.rearrange(f"p ({' '.join(names)}) -> p {' '.join(names)}", **{x: s for x, s in zip(names, shape)})
        return v


def pack(parts):
    where, cols, at = {}, [], 0
    for name, a in parts:
        a = np.asarray(a, np.float32)
        full = np.zeros((P, a.shape[1]), np.float32)
        full[:a.shape[0]] = a
        cols.append(full)
        where[name] = (at, a.shape[0], a.shape[1])
        at += a.shape[1]
    return np.ascontiguousarray(np.concatenate(cols, axis=1)), where


class Weights:

    def __init__(self, tensor, where, at=0):
        self.tensor, self.where, self.at = tensor, where, at

    def __call__(self, name, rows=None, cols=None):
        at, r, c = self.where[name]
        lo, hi = cols or (0, c)
        rlo, rhi = rows or (0, r)
        return self.tensor[rlo:rhi, self.at + at + lo:self.at + at + hi]





def constants():
    i = np.arange(P)
    parts = [("ident", np.eye(P)), ("neghalf", np.full((P, 64), -0.5)), ("ones", np.ones((P, P))),
             ("scratch", np.zeros((P, 1))), ("tri_incl", (i[:, None] <= i[None, :]) * 1.0),
             ("tri_strict", (i[:, None] < i[None, :]) * 1.0), ("after", (i[:, None] > i[None, :]) * 1.0)]
    parts += [("causal", np.where(i[None, :] <= i[:, None], 0.0, -1e30)), ("heads16", np.kron(np.eye(4), np.ones((16, 16))))]
    for n in range(7):
        b = i >> n
        m = ((b[:, None] >> 1) == (b[None, :] >> 1)) & (b[:, None] % 2 == 1) & (b[None, :] % 2 == 0)
        parts += [(f"level{n}", m.T if n == 0 else m)]
    parts += [("blocks32", np.kron(np.eye(4), np.ones((32, 32)))), ("blocks64", np.kron(np.eye(4), np.ones((32, 64))))]
    c = np.arange(192)
    band = np.where((c[None, :] >= i[:, None]) & (c[None, :] <= i[:, None] + 64), 0.0, -1e30)
    parts += [("band", band)] + rotary_tables()
    parts += [("lag", np.maximum(i[None, :] - 1 - i[:, None], 0)), ("place", np.broadcast_to(i[None, :], (P, P))),
              ("left", (P - 1 - i)[:, None])]
    return parts


def rotary_tables():
    hd, window, n = 64, 64, SEQ
    half = np.arange(0, hd, 2, dtype=np.float32)
    inv_freq = (1.0 / np.float32(10000.0) ** (half / np.float32(hd))).astype(np.float32)
    t = np.arange(n, dtype=np.float32)
    freqs = (t[:, None] * inv_freq[None, :]).astype(np.float32).astype(np.float64)
    base = (half + 0.4 * hd) / (1.4 * hd)
    scale = base[None, :].astype(np.float64) ** ((t - n // 2) / float(window // 2))[:, None]
    out = []
    for side, m in (("q", scale), ("k", 1.0 / scale)):
        cos, sin = np.cos(freqs) * m, np.sin(freqs) * m
        for name, a in (("cos", np.concatenate([cos, cos], axis=1)), ("sin", np.concatenate([-sin, sin], axis=1))):
            out.append((f"{name}_{side}", a.reshape(TILES, P, hd).transpose(1, 0, 2).reshape(P, TILES * hd)))
    return out





class Kit:

    def __init__(self, pr, consts, X):
        self.pr, self.nc, self.c, self.X = pr, pr.nc, consts, X
        self.ident = consts("ident")


def over(view, n):
    m = view.shape[1]
    return view.unsqueeze(2).broadcast_to([view.shape[0], m, n])


def settle(kit, s):
    s.dve(kit.nc.vector.memset, kit.c("scratch"), 0.0)


def norm_rows(kit, s, src, dst, mv, stats, rstd, eps, after=()):
    nc, tiles = kit.nc, src.shape[1]
    for t in range(tiles):
        s.dve(nc.vector.bn_stats, stats[:, t, :], src[:, t, :], after=after if t == 0 else (), link=(t == 0))
    settle(kit, s)
    for t in range(tiles):
        moments = s.dve(nc.vector.bn_aggr, mv[:, t, :], stats[:, t, :], link=False)
    shifted = s.dve(nc.vector.tensor_scalar, rstd, mv[:, :, 1], eps, None, ALU.add)
    root = s.pool(nc.gpsimd.tensor_tensor, rstd, rstd, kit.c("neghalf", cols=(0, tiles)), ALU.pow, after=[shifted])
    for t in range(tiles):
        done = s.dve(nc.vector.tensor_scalar, dst[:, t, :], src[:, t, :], mv[:, t, 0:1], rstd[:, t:t + 1],
                     ALU.subtract, ALU.mult, after=[root, moments] if t == 0 else (), link=False)
    return done


def to_features(kit, s, ring, blocks, dst, after, scale=None, bias=None, engine="ACT", width=P, rows=P):
    nc = kit.nc
    bank, free, k = ring.take()
    n = len(blocks)
    if rows < P:
        hold(kit, s, bank, [*after, *free])
        after = free = ()
    for t, block in enumerate(blocks):
        turned = s.tr(bank[0:rows, t * P:(t + 1) * P], block, kit.ident,
                      after=[*after, *free] if t == 0 else (), signal=(t == n - 1))
    src = bank[0:rows, 0:n * P]
    if engine == "ACT":
        if scale is None and bias is None:
            done = s.act(nc.scalar.copy, dst, src, after=[turned])
        else:
            done = s.act(nc.scalar.activation, dst, src, ACT.Identity, bias=bias if bias is not None else 0.0,
                         scale=scale if scale is not None else 1.0, after=[turned])
    else:
        done = s.dve(nc.vector.tensor_copy, dst, src, after=[turned], link=False)
    ring.give(k, done)
    return done


def log1p(kit, s, e, u, rest, out, after=()):
    nc = kit.nc
    one_more = s.dve(nc.vector.tensor_scalar, u, e, 1.0, None, ALU.add, after=after)
    s.dve(nc.vector.tensor_scalar, rest, u, -1.0, None, ALU.add)
    s.dve(nc.vector.tensor_tensor, rest, e, rest, ALU.subtract)
    log = s.act(nc.scalar.activation, out, u, ACT.Ln, after=[one_more])
    return s.dve(nc.vector.tensor_tensor, out, out, rest, ALU.add, after=[log])


def hold(kit, s, bank, after):
    s.mm(bank[:, 0:1], kit.ident, kit.c("ident", cols=(0, 1)), after=after, signal=False)




EXPERTS = 8


def prefix_exclusive(kit, s, eq, pre, n):
    nc = kit.nc
    a, b = pre
    s.dve(nc.vector.memset, a[:, :, 0:1], 0.0)
    s.dve(nc.vector.tensor_copy, a[:, :, 1:n], eq[:, :, 0:n - 1], link=False)
    step = 1
    while step < n:
        s.dve(nc.vector.tensor_copy, b[:, :, 0:step], a[:, :, 0:step])
        s.dve(nc.vector.tensor_tensor, b[:, :, step:n], a[:, :, step:n], a[:, :, 0:n - step], ALU.add, link=False)
        a, b = b, a
        step *= 2
    return a


def weighted_experts(kit, s, hidden_all, weight_of, acc, fc2, ff_tiles, hid, y_rings, started):
    nc = kit.nc

    def down(e, hT, k, last):
        bank, yfree, yk = y_rings.take()
        for t in range(TILES):
            for f in range(ff_tiles):
                y = s.mm(bank[:, t * P:(t + 1) * P], hT[:, f, t * P:(t + 1) * P], fc2(e, f),
                         start=(f == 0), stop=(f == ff_tiles - 1), after=[last, *yfree] if t == 0 and f == 0 else (),
                         signal=(t == TILES - 1 and f == ff_tiles - 1))
        hid.give(k, y)
        return bank, yk, y

    def add(e, bank, yk, y):
        for t in range(TILES):
            part, first = bank[:, t * P:(t + 1) * P], t == 0
            if e == 0:
                done = s.dve(nc.vector.tensor_scalar, acc[:, t, :], part, weight_of(e, t), None, ALU.mult,
                             after=[y] if first else (), link=first)
            else:
                done = s.dve(nc.vector.scalar_tensor_tensor, acc[:, t, :], part, weight_of(e, t), acc[:, t, :],
                             ALU.mult, ALU.add, after=[y] if first else (), link=first)
        y_rings.give(yk, done)
        return done

    previous, pending, done = None, None, None
    for e in range(EXPERTS):
        current = (e, *hidden_all(e, started if e == 0 else ()))
        if previous:
            pending = (previous[0], *down(*previous))
            done = add(*pending)
        previous = current
    return add(previous[0], *down(*previous))




HEADS, DK = 4, 32
LEVELS = 7


class Delta:

    def __init__(self, kit, arena, dv, out_scaled):
        self.kit, self.dv = kit, dv
        self.NT, self.AT, self.X, self.XT, self.T1 = (arena.take(2, HEADS, P) for _ in range(5))
        self.WT = Ring([arena.take(P) for _ in range(2)])
        self.U = Ring([arena.take(HEADS, dv) for _ in range(2)])
        self.S = arena.take(HEADS * dv)
        self.gain = arena.take(HEADS * dv)
        self.own = kit.c(f"blocks{dv}")
        self.qS = arena.take(HEADS, dv) if out_scaled else None

    def start(self, s):
        return s.dve(self.kit.nc.vector.memset, self.S, 0.0, link=False)

    def invert(self, s, ring, chunks, kT, kbq, gt, after, gt_masked=None, filler=None):
        kit, nc = self.kit, self.kit.nc
        banks = []
        for hh in range(HEADS):
            bank, free, k = ring.take()
            part = slice(DK * hh, DK * hh + DK)
            for j, c in enumerate(chunks):
                made = s.mm(bank[:, j * 2 * P:(j + 1) * 2 * P], kT(c)[part, :], kbq(c)[part, :],
                            after=[*after, *free] if j == 0 else (), signal=j == 1)
            banks.append((bank, k, made))
        for hh, (bank, k, made) in enumerate(banks):
            both = bank[:, :].rearrange("p (c a n) -> p c a n", c=2, a=2)
            if gt is None:
                a = s.act(nc.scalar.copy, self.NT[:, :, hh, :], both[:, :, 0, :], after=[made])
                b = s.dve(nc.vector.tensor_tensor, self.AT[:, :, hh, :], both[:, :, 1, :],
                          kit.c("tri_incl").unsqueeze(1).broadcast_to([P, 2, P]), ALU.mult, after=[made, a],
                          link=False)
            else:
                a = s.dve(nc.vector.tensor_tensor, self.NT[:, :, hh, :], both[:, :, 0, :], gt[:, :, hh, :], ALU.mult,
                          after=[made], link=False)
                b = s.dve(nc.vector.tensor_tensor, self.AT[:, :, hh, :], both[:, :, 1, :], gt_masked[:, :, hh, :],
                          ALU.mult, link=False)
            ring.give(k, b)
        flat = lambda m, j: m[:, j].rearrange("p h n -> p (h n)")
        bc = lambda name: kit.c(name).unsqueeze(1).broadcast_to([P, HEADS, P])
        xt = [None, None]
        for j in range(2):
            s.dve(nc.vector.tensor_tensor, self.T1[:, j], self.NT[:, j], bc("level0"), ALU.mult, after=[a])
            xt[j] = s.dve(nc.vector.tensor_tensor, self.XT[:, j], bc("ident"), self.T1[:, j], ALU.subtract)
        for n in range(1, LEVELS):
            x = [None, None]
            for j in range(2):
                bank, free, k = ring.take()
                for hh in range(HEADS):
                    made = s.tr(bank[:, hh * P:(hh + 1) * P], self.XT[:, j, hh, :], kit.ident,
                                after=[xt[j], *free] if hh == 0 else (), signal=hh == HEADS - 1)
                x[j] = s.act(nc.scalar.copy, flat(self.X, j), bank[:, :], after=[made])
                ring.give(k, x[j])
            t1 = [None, None]
            for j in range(2):
                bank, free, k = ring.take()
                for hh in range(HEADS):
                    made = s.mm(bank[:, hh * P:(hh + 1) * P], self.NT[:, j, hh, :], self.X[:, j, hh, :],
                                after=[x[j], a, *free] if hh == 0 else (), signal=hh == HEADS - 1)
                t1[j] = s.dve(nc.vector.tensor_tensor, self.T1[:, j],
                              bank[:, :].rearrange("p (h n) -> p h n", h=HEADS), bc(f"level{n}"), ALU.mult,
                              after=[made], link=False)
                ring.give(k, t1[j])
            for j in range(2):
                bank, free, k = ring.take()
                for hh in range(HEADS):
                    made = s.mm(bank[:, hh * P:(hh + 1) * P], self.T1[:, j, hh, :], self.XT[:, j, hh, :],
                                after=[t1[j], *free] if hh == 0 else (), signal=hh == HEADS - 1)
                xt[j] = s.dve(nc.vector.tensor_tensor, flat(self.XT, j), flat(self.XT, j), bank[:, :], ALU.subtract,
                              after=[made], link=False)
                ring.give(k, xt[j])
            if filler:
                filler()
        return xt, [a, b]

    def advance(self, s, ring, j, state, ready, qT, vb, kbe, kd, out, out_scale=None, chunk_decay=None):
        kit, nc, dv = self.kit, self.kit.nc, self.dv
        wt, wfree, wk = self.WT.take()
        bank, free, k = ring.take()
        for hh in range(HEADS):
            made = s.mm(bank[DK * hh:DK * hh + DK, 0:P], kbe[:, hh, :], self.XT[:, j, hh, :],
                        after=[*ready, *free] if hh == 0 else (), signal=hh == HEADS - 1)
        turned = s.act(nc.scalar.mul, wt, bank[:, 0:P], -1.0, after=[made, *wfree])
        ring.give(k, turned)
        u, ufree, uk = self.U.take()
        flat_u = u.rearrange("p h d -> p (h d)")
        width = HEADS * dv
        bank, free, k = ring.take()
        s.mm(bank[:, 0:width], wt, self.S, stop=False, after=[turned, state, *free], signal=False)
        for hh in range(HEADS):
            made = s.mm(bank[:, hh * dv:(hh + 1) * dv], self.XT[:, j, hh, :], vb[:, hh, :], start=False, stop=hh == HEADS - 1,
                        signal=hh == HEADS - 1)
        self.WT.give(wk, made)
        values = s.act(nc.scalar.copy, flat_u, bank[:, 0:width], after=[made, *ufree])
        ring.give(k, values)
        bank, free, k = ring.take()
        by_head = lambda v: v[:, 0:width].rearrange("p (h d) -> p h d", d=dv)
        if out_scale is None:
            s.mm(bank[:, 0:width], qT, self.S, stop=False, after=free, signal=False)
            for hh in range(HEADS):
                made = s.mm(bank[:, hh * dv:(hh + 1) * dv], self.AT[:, j, hh, :], u[:, hh, :], start=False, stop=hh == HEADS - 1,
                            after=[values] if hh == 0 else (), signal=hh == HEADS - 1)
            got = s.act(nc.scalar.copy, out, by_head(bank), after=[made])
        else:
            bank2, free2, k2 = ring.take()
            carried = s.mm(bank2[:, 0:width], qT, self.S, after=[*free, *free2])
            scaled = s.dve(nc.vector.tensor_tensor, self.qS, by_head(bank2), over(out_scale, dv), ALU.mult,
                           after=[carried])
            ring.give(k2, scaled)
            for hh in range(HEADS):
                made = s.mm(bank[:, hh * dv:(hh + 1) * dv], self.AT[:, j, hh, :], u[:, hh, :],
                            after=[values] if hh == 0 else (), signal=hh == HEADS - 1)
            got = s.dve(nc.vector.tensor_tensor, out, self.qS, by_head(bank), ALU.add, after=[made])
        ring.give(k, got)
        bank, free, k = ring.take()
        added = s.mm(bank[:, 0:width], kd, flat_u, after=free)
        self.U.give(uk, added)
        gained = s.dve(nc.vector.tensor_tensor, self.gain, bank[:, 0:width], self.own, ALU.mult, after=[added])
        ring.give(k, gained)
        if chunk_decay is None:
            state = s.dve(nc.vector.tensor_tensor, self.S, self.S, self.gain, ALU.add)
        else:
            state = s.dve(nc.vector.scalar_tensor_tensor, self.S, self.S, chunk_decay, self.gain, ALU.mult, ALU.add)
        return state, got




L0_ATTN_SHORT, L0_ATTN_LONG, L0_ATTN_CONV = 5, 64, 4
L0_ATTN_PAD = L0_ATTN_LONG - 1
L0_ATTN_STATS = 16
L0_ATTN_GROUPS = TILES * HEADS


def layout_l0_attn(w):
    bc = lambda v: np.broadcast_to(np.reshape(v, (1, -1)), (P, np.size(v)))
    stat_w = np.zeros((HEADS, 32, P), np.float32)
    stat_w[:, :L0_ATTN_STATS, :] = w["fuse_w1"][:, DIM:].T[None]
    return [("q", w["q_proj_w"].T), ("k", w["k_proj_w"].T), ("v", w["v_proj_w"].T), ("beta", w["b_proj_w"].T),
            ("q_conv", w["q_conv_w"]), ("k_conv", w["k_conv_w"]), ("v_conv", w["v_conv_w"]),
            ("short", w["fir_short_w"].reshape(P, L0_ATTN_SHORT)), ("long", w["fir_long_w"].reshape(P, L0_ATTN_LONG)),
            ("fuse_hidden", w["fuse_w1"][:, :DIM].T), ("fuse_stats", stat_w.reshape(P, P)),
            ("fuse_b1", w["fuse_b1"][:, None]), ("fuse_w2", w["fuse_w2"].T), ("fuse_b2", bc(w["fuse_b2"])),
            ("temp", bc(w["logit_temp"])), ("res", bc(np.concatenate([w["res_scale_short"], w["res_scale_long"]]))),
            ("o_norm", np.tile(w["o_norm_w"], HEADS)[:, None]), ("o", w["o_proj_w"].T)]


def depthwise(kit, s, dst, src, taps, first, n, after=()):
    nc = kit.nc
    for j in range(n):
        view = src[:, first + j:first + j + SEQ]
        if j == 0:
            done = s.dve(nc.vector.tensor_scalar, dst, view, taps[:, 0:1], None, ALU.mult, after=after)
        else:
            done = s.dve(nc.vector.scalar_tensor_tensor, dst, view, taps[:, j:j + 1], dst, ALU.mult, ALU.add)
    return done


def stage_l0_attn(kit, w, arena):
    nc, X, banks = kit.nc, kit.X, kit.pr.banks
    before = [arena.take(L0_ATTN_CONV - 1 + SEQ) for _ in range(3)]
    vT = arena.take(L0_ATTN_PAD + SEQ)
    stat_rows = arena.take(TILES, HEADS, 32)
    u1, u2, u3, temp_inv = (arena.take(1) for _ in range(4))
    s = Section(kit.pr, "l0_start")
    for b in before:
        s.dve(nc.vector.memset, b[:, 0:L0_ATTN_CONV - 1], 0.0, link=False)
    s.dve(nc.vector.memset, vT[:, 0:L0_ATTN_PAD], 0.0, link=False)
    s.dve(nc.vector.memset, stat_rows, 0.0, link=False)
    s.dve(nc.vector.tensor_scalar, u1, w("temp"), -1.0, None, ALU.mult)
    low = s.dve(nc.vector.tensor_tensor, u1, u1, w("temp"), ALU.min)
    ex = s.act(nc.scalar.activation, u1, u1, ACT.Exp, after=[low])
    log1p(kit, s, u1, u2, u3, temp_inv, after=[ex])
    s.dve(nc.vector.tensor_scalar, u1, w("temp"), 0.0, 1e-4, ALU.max, ALU.add)
    s.dve(nc.vector.tensor_tensor, temp_inv, temp_inv, u1, ALU.add)
    s.dve(nc.vector.reciprocal, temp_inv, temp_inv)
    s.emit()

    s = Section(kit.pr, "l0_attn")
    xr, z, zT = arena.take(TILES, P), arena.take(TILES, P), arena.take(SEQ)
    stats, mv, rstd = arena.take(TILES, 6), arena.take(TILES, 2), arena.take(TILES)
    qrow, krow, vrow = (arena.take(TILES, P) for _ in range(3))
    vb, kb = arena.take(TILES, P), arena.take(TILES, P)
    kT, kbq = arena.take(TILES, P), arena.take(TILES, 2, P)
    beta, ss, rn = arena.take(TILES, HEADS), arena.take(2, L0_ATTN_GROUPS), arena.take(2, L0_ATTN_GROUPS)
    drow = arena.take(TILES, P)
    delta = Delta(kit, arena, DK, False)
    hid = arena.take(HEADS, SEQ) if False else None
    shortT, longT = arena.take(SEQ), arena.take(SEQ)
    logits, lmax = arena.take(L0_ATTN_GROUPS, 4), arena.take(L0_ATTN_GROUPS)
    ring = Ring(banks)
    heads = lambda v: v.rearrange("p t (h d) -> p (t h) d", d=DK)

    loaded = s.dve(nc.vector.tensor_copy, xr, At(lambda o, i: X[:, ds(i * TILES, TILES), :]))
    rows = norm_rows(kit, s, xr, z, mv, stats, rstd, LN_EPS, after=[loaded])
    feats = to_features(kit, s, ring, [z[:, t, :] for t in range(TILES)], zT, [rows])
    shaped = []
    for name, src, dst in (("v", before[2], vT[:, L0_ATTN_PAD:]), ("k", before[1], longT), ("q", before[0], shortT)):
        bank, free, k = ring.take()
        made = s.mm(bank[:, :], w(name), zT, after=[feats, *free])
        moved = s.act(nc.scalar.copy, src[:, L0_ATTN_CONV - 1:], bank[:, :], after=[made])
        ring.give(k, moved)
        conv = depthwise(kit, s, kT.rearrange("p t n -> p (t n)") if name == "k" else
                         drow.rearrange("p t n -> p (t n)") if name == "v" else
                         kb.rearrange("p t n -> p (t n)"), src, w(f"{name}_conv"), 0, L0_ATTN_CONV, after=[moved])
        source = {"k": kT, "v": drow, "q": kb}[name].rearrange("p t n -> p (t n)")
        shaped.append(s.act(nc.scalar.activation, dst, source, ACT.Silu, after=[conv]))
    values_T, keys_T, queries_T = shaped
    bank, free, k = ring.take()
    for t in range(TILES):
        made = s.mm(bank[:, t * HEADS:(t + 1) * HEADS], zT[:, t * P:(t + 1) * P], w("beta"),
                    after=free if t == 0 else (), signal=t == TILES - 1)
    betas = s.act(nc.scalar.activation, beta, bank[:, 0:L0_ATTN_GROUPS].rearrange("p (t h) -> p t h", h=HEADS), ACT.Sigmoid,
                  after=[made])
    ring.give(k, betas)
    blocks = lambda v, first=0: [v[:, first + t * P:first + (t + 1) * P] for t in range(TILES)]
    flat = lambda v: v.rearrange("p t n -> p (t n)")
    vals = to_features(kit, s, ring, blocks(vT, L0_ATTN_PAD), flat(vrow), [values_T])
    for n, (src, dst, made) in enumerate(((longT, krow, keys_T), (shortT, qrow, queries_T))):
        raw = to_features(kit, s, ring, blocks(src), flat(dst), [made])
        sq = s.act(nc.scalar.activation, flat(vb), flat(dst), ACT.Square, after=[raw, Token("DVE", s.count["DVE"])],
                   link=True)
        total = s.dve(nc.vector.tensor_reduce, ss[:, n, :], heads(vb), AX, ALU.add, after=[sq])
        root = s.pool(nc.gpsimd.tensor_tensor, rn[:, n, :], ss[:, n, :], kit.c("neghalf", cols=(0, L0_ATTN_GROUPS)), ALU.pow,
                      after=[total])
        unit = s.dve(nc.vector.tensor_tensor, heads(dst), heads(dst), over(rn[:, n, :], DK), ALU.mult, after=[root])
    by_beta = over(beta.rearrange("p t h -> p (t h)"), DK)
    s.dve(nc.vector.tensor_tensor, heads(vb), heads(vrow), by_beta, ALU.mult, after=[vals, betas])
    ready = s.dve(nc.vector.tensor_tensor, heads(kb), heads(krow), by_beta, ALU.mult)
    tok = lambda v: [v[:, t, :] for t in range(TILES)]
    turned = [to_features(kit, s, ring, tok(krow), flat(kT), [ready])]
    for n, src in enumerate((kb, qrow)):
        bank, free, k = ring.take()
        for t in range(TILES):
            made = s.tr(bank[:, t * P:(t + 1) * P], src[:, t, :], kit.ident, after=[ready, *free] if t == 0 else (),
                        signal=t == TILES - 1)
        turned.append(s.act(nc.scalar.copy, kbq[:, :, n, :], bank[:, :].rearrange("p (t n) -> p t n", n=P),
                            after=[made]))
        ring.give(k, turned[-1])

    taps = [("short", shortT, L0_ATTN_SHORT, j) for j in range(L0_ATTN_SHORT)] + [("long", longT, L0_ATTN_LONG, j) for j in range(L0_ATTN_LONG)]
    filters = [None]

    def filler(count=6):
        for _ in range(count):
            if not taps:
                return
            name, dst, n, j = taps.pop(0)
            view = vT[:, L0_ATTN_PAD - (n - 1) + j:L0_ATTN_PAD - (n - 1) + j + SEQ]
            if j == 0:
                filters[0] = s.dve(nc.vector.tensor_scalar, dst, view, w(name, cols=(0, 1)), None, ALU.mult,
                                   after=[values_T, *turned])
            else:
                filters[0] = s.dve(nc.vector.scalar_tensor_tensor, dst, view, w(name, cols=(j, j + 1)), dst,
                                   ALU.mult, ALU.add)

    state = delta.start(s)
    chunk_heads = lambda v, c: v[:, c, :].rearrange("p (h d) -> p h d", d=DK)
    for pair in range(2):
        chunks = (2 * pair, 2 * pair + 1)
        xt, scored = delta.invert(s, ring, chunks, lambda c: kT[:, c, :], lambda c: kbq[:, c].rearrange("p a n -> p (a n)"),
                                  None, turned, filler=filler)
        for j, c in enumerate(chunks):
            state, got = delta.advance(s, ring, j, state, [*xt, *scored], kbq[:, c, 1, :], chunk_heads(vb, c),
                                       chunk_heads(kb, c), krow[:, c, :], chunk_heads(drow, c))
    while taps:
        filler()
    srow, lrow = qrow, krow
    outs = [to_features(kit, s, ring, blocks(shortT), flat(srow), [filters[0], got, state]),
            to_features(kit, s, ring, blocks(longT), flat(lrow), [filters[0], got, state])]
    tmp, m1, m2, m3 = vb, ss[:, 0, :], ss[:, 1, :], rn[:, 0, :]
    st4 = stat_rows.rearrange("p t h c -> p (t h) c")
    for n, src in enumerate((srow, lrow, drow, vrow)):
        col = lambda c: st4[:, :, 4 * n + c]
        s.dve(nc.vector.tensor_reduce, m1, heads(src), AX, ALU.add, after=[*outs, got])
        sq = s.act(nc.scalar.activation, flat(tmp), flat(src), ACT.Square, after=[*outs, Token("DVE", s.count["DVE"])])
        s.dve(nc.vector.tensor_scalar, col(0), m1, 1.0 / DK, None, ALU.mult)
        s.dve(nc.vector.tensor_reduce, m3, heads(src), AX, ALU.add, apply_absolute_value=True)
        s.dve(nc.vector.tensor_scalar, col(2), m3, 1.0 / DK, None, ALU.mult)
        s.dve(nc.vector.tensor_reduce, m2, heads(tmp), AX, ALU.add, after=[sq])
        s.dve(nc.vector.tensor_tensor, m1, col(0), col(0), ALU.mult)
        s.dve(nc.vector.scalar_tensor_tensor, col(1), m2, 1.0 / DK, m1, ALU.mult, ALU.subtract)
        length = s.dve(nc.vector.tensor_copy, col(3), m2)
    lengths = s.act(nc.scalar.activation, stat_rows.rearrange("p t h (n c) -> p (t h) n c", c=4)[:, :, 0:4, 3],
                    stat_rows.rearrange("p t h (n c) -> p (t h) n c", c=4)[:, :, 0:4, 3], ACT.Sqrt, after=[length])
    statT = shortT
    stat_feats = to_features(kit, s, ring, [stat_rows[:, t].rearrange("p h c -> p (h c)") for t in range(TILES)],
                             statT, [lengths])
    hidT = delta.X.rearrange("p a h n -> p (a h n)").rearrange("p (b n) -> p b n", n=SEQ)
    hids = Ring([hidT[:, 0, :], hidT[:, 1, :]])
    lbank, lfree, lk = ring.take()
    hold_ring = []
    for hh in range(HEADS):
        bank, free, k = ring.take()
        s.mm(bank[:, :], w("fuse_hidden"), zT, stop=False, after=[stat_feats, got, *free], signal=False)
        part = (DK * hh, DK * hh + DK)
        made = s.mm(bank[:, :], w("fuse_stats", rows=part), statT[part[0]:part[1], :], start=False)
        dst, hfree, hk = hids.take()
        act = s.act(nc.scalar.activation, dst, bank[:, :], ACT.Gelu, bias=w("fuse_b1"), after=[made, *hfree])
        ring.give(k, act)
        for t in range(TILES):
            at = (t * HEADS + hh) * 4
            made = s.mm(lbank[:, at:at + 4], dst[:, t * P:(t + 1) * P], w("fuse_w2"),
                        after=[act, *lfree] if t == 0 else (), signal=t == TILES - 1)
        hids.give(hk, made)
    s.dve(nc.vector.tensor_tensor, logits, lbank[:, 0:L0_ATTN_GROUPS * 4].rearrange("p (g c) -> p g c", c=4),
          w("fuse_b2").unsqueeze(1).broadcast_to([P, L0_ATTN_GROUPS, 4]), ALU.add, after=[made])
    s.dve(nc.vector.tensor_reduce, lmax, logits, AX, ALU.max)
    centred = s.dve(nc.vector.tensor_tensor, logits, logits, over(lmax, 4), ALU.subtract)
    ring.give(lk, centred)
    exps = s.act(nc.scalar.activation, logits, logits, ACT.Exp, scale=temp_inv, after=[centred])
    s.dve(nc.vector.tensor_reduce, lmax, logits, AX, ALU.add, after=[exps])
    s.dve(nc.vector.reciprocal, lmax, lmax)
    s.dve(nc.vector.tensor_tensor, logits, logits, over(lmax, 4), ALU.mult)
    for n in range(2):
        s.dve(nc.vector.tensor_scalar, logits[:, :, n], logits[:, :, n], w("res", cols=(n, n + 1)), None, ALU.add)
    for n, src in enumerate((srow, lrow, drow, vrow)):
        s.dve(nc.vector.tensor_tensor, heads(src), heads(src), over(logits[:, :, n], DK), ALU.mult)
    s.dve(nc.vector.tensor_tensor, srow, srow, lrow, ALU.add)
    s.dve(nc.vector.tensor_tensor, drow, drow, vrow, ALU.add)
    mixed = s.dve(nc.vector.tensor_tensor, srow, srow, drow, ALU.add)
    sq = s.act(nc.scalar.activation, flat(tmp), flat(srow), ACT.Square, after=[mixed])
    s.dve(nc.vector.tensor_reduce, m1, heads(tmp), AX, ALU.add, after=[sq])
    shifted = s.dve(nc.vector.tensor_scalar, m1, m1, 1.0 / DK, 1e-5, ALU.mult, ALU.add)
    root = s.pool(nc.gpsimd.tensor_tensor, m2, m1, kit.c("neghalf", cols=(0, L0_ATTN_GROUPS)), ALU.pow, after=[shifted])
    normed = s.dve(nc.vector.tensor_tensor, heads(srow), heads(srow), over(m2, DK), ALU.mult, after=[root])
    oT = longT
    turned_o = to_features(kit, s, ring, tok(srow), oT, [normed], scale=w("o_norm"))
    bank, free, k = ring.take()
    for t in range(TILES):
        made = s.mm(bank[:, t * P:(t + 1) * P], oT[:, t * P:(t + 1) * P], w("o"),
                    after=[turned_o, *free] if t == 0 else (), signal=t == TILES - 1)
    s.dve(nc.vector.tensor_tensor, At(lambda o, i: X[:, ds(i * TILES, TILES), :]), xr,
          bank[:, :].rearrange("p (t d) -> p t d", d=P), ALU.add, after=[made])
    s.emit(1, BATCH)




L0_FFN_FF_TILES = 4


def layout_l0_ffn(w):
    parts = [("router", w["Wr"]), ("router_bias", np.broadcast_to(w["br"][None, :], (P, EXPERTS)))]
    for e in range(EXPERTS):
        parts.append((f"up{e}", w["W1"][e]))
        for f in range(4):
            parts.append((f"down{e}_{f}", w["W2"][e][f * P:(f + 1) * P]))
    return parts


def stage_l0_ffn(kit, w, arena):
    nc, X = kit.nc, kit.X
    s = Section(kit.pr, "l0_ffn")
    xr, h, xT = arena.take(TILES, P), arena.take(TILES, P), arena.take(SEQ)
    acc, hid0, hid1 = arena.take(TILES, P), arena.take(4, SEQ), arena.take(4, SEQ)
    stats, mv, rstd = arena.take(TILES, 6), arena.take(TILES, 2), arena.take(TILES)
    route, eq, pa, pb = (arena.take(TILES, EXPERTS) for _ in range(4))
    top, weight = arena.take(TILES), arena.take(TILES, EXPERTS)
    banks = kit.pr.banks
    ring, yring, hid = Ring(banks[0:4]), Ring(banks[4:6]), Ring([hid0, hid1])

    loaded = s.dve(nc.vector.tensor_copy, xr, At(lambda o, i: X[:, ds(i * TILES, TILES), :]))
    rows = norm_rows(kit, s, xr, h, mv, stats, rstd, LN_EPS, after=[loaded])
    feats = to_features(kit, s, ring, [h[:, t, :] for t in range(TILES)], xT, [rows])
    for t in range(TILES):
        logits = s.mm(banks[6][:, t * EXPERTS:(t + 1) * EXPERTS], xT[:, t * P:(t + 1) * P], w("router"),
                      after=[feats] if t == 0 else (), signal=(t == TILES - 1))
    s.dve(nc.vector.tensor_tensor, route, banks[6][:, 0:TILES * EXPERTS].rearrange("p (t e) -> p t e", e=EXPERTS),
          w("router_bias").unsqueeze(1).broadcast_to([P, TILES, EXPERTS]), ALU.add, after=[logits])
    biased = Token("DVE", s.count["DVE"])
    prob = s.act(nc.scalar.activation, route, route, ACT.Sigmoid, after=[biased])
    s.dve(nc.vector.tensor_reduce, top, route, AX, ALU.max, after=[prob])
    s.dve(nc.vector.tensor_tensor, eq, route, over(top, EXPERTS), ALU.is_equal)
    pre = prefix_exclusive(kit, s, eq, (pa, pb), EXPERTS)
    s.dve(nc.vector.tensor_scalar, pre, pre, 0.5, None, ALU.is_lt)
    s.dve(nc.vector.tensor_tensor, eq, eq, pre, ALU.mult)
    weights = s.dve(nc.vector.tensor_tensor, weight, eq, over(top, EXPERTS), ALU.mult)

    def hidden_all(e, started):
        hT, free, hk = hid.take()
        for f in range(L0_FFN_FF_TILES):
            bank, bfree, k = ring.take()
            up = s.mm(bank[:, :], w(f"up{e}", cols=(f * P, (f + 1) * P)), xT, after=[*bfree, *started])
            act = s.act(nc.scalar.activation, hT[:, f, :], bank[:, :], ACT.Gelu,
                        after=[up, *(free if f == 0 else ())])
            ring.give(k, act)
        return hT, hk, act

    done = weighted_experts(kit, s, hidden_all, lambda e, t: weight[:, t, e:e + 1], acc,
                            lambda e, f: w(f"down{e}_{f}"), L0_FFN_FF_TILES, hid, yring, [feats])
    s.dve(nc.vector.tensor_tensor, At(lambda o, i: X[:, ds(i * TILES, TILES), :]), xr, acc, ALU.add, after=[done])
    s.emit(1, BATCH)




L1_ATTN_LAYERS, L1_ATTN_HEADS, L1_ATTN_HD = 4, 8, 16
L1_ATTN_LOCAL = 4
L1_ATTN_HALF = L1_ATTN_LOCAL * L1_ATTN_HD
L1_ATTN_BUCKET = 64
L1_ATTN_BUCKETS = SEQ // L1_ATTN_BUCKET
L1_ATTN_FF = 4


def layout_l1_attn(w):
    parts = []
    for n in range(L1_ATTN_LAYERS):
        def padded(m):
            out = np.zeros((P, L1_ATTN_LOCAL, 32), np.float32)
            out[:, :, :L1_ATTN_HD] = m[:, :L1_ATTN_HALF].reshape(P, L1_ATTN_LOCAL, L1_ATTN_HD)
            return out.reshape(P, P)
        bc = lambda v: np.broadcast_to(v[None, :], (P, P))
        one = [("q", padded(w["Wq"][n])), ("k", padded(w["Wk"][n])),
               ("qkv", np.concatenate([w["Wq"][n][:, L1_ATTN_HALF:], w["Wk"][n][:, L1_ATTN_HALF:], w["Wv"][n]], axis=1)),
               ("o", w["Wo"][n]), ("up", w["W1"][n])]
        one += [(f"down{f}", w["W2"][n][f * P:(f + 1) * P]) for f in range(L1_ATTN_FF)]
        one += [("bo", bc(w["bo"][n])), ("b2", bc(w["b2"][n])), ("b1", w["b1"][n].reshape(L1_ATTN_FF, P).T)]
        one += [(c, w[c][n][:, None]) for c in ("ln1_g", "ln1_b", "ln2_g", "ln2_b")]
        parts += [(name if n == 0 else f"{name}@{n}", a) for name, a in one]
    return parts


def stage_l1_attn(kit, w, arena):
    nc, X, banks = kit.nc, kit.X, kit.pr.banks
    layer_cols = w.where["q@1"][0] - w.where["q"][0]
    Yall = arena.take(BATCH * TILES, P)
    static = arena.take(layer_cols)
    wl = Weights(static, w.where)
    xr = arena.take(TILES, P)
    stats, mv, rstd = arena.take(TILES, 6), arena.take(TILES, 2), arena.take(TILES)
    tiles_of = lambda A: At(lambda o, i: A[:, ds(i * TILES, TILES), :])

    s = Section(kit.pr, "l1_enter")
    y = arena.take(TILES, P)
    v = arena.take(TILES, P + 1)
    loaded = s.dve(nc.vector.tensor_copy, xr, tiles_of(X))
    rows = norm_rows(kit, s, xr, y, mv, stats, rstd, LN_EPS, after=[loaded])
    s.dve(nc.vector.tensor_copy, tiles_of(Yall), y)
    s.dve(nc.vector.memset, v[:, :, P:P + 1], 1.0, link=False)
    s.emit(1, BATCH)

    s = Section(kit.pr, "l1_layers")
    h, hT, qT, kT, oT = arena.take(TILES, P), arena.take(SEQ), arena.take(SEQ), arena.take(SEQ), arena.take(SEQ)
    qg, kg, kpos = arena.take(TILES, L1_ATTN_HALF), arena.take(TILES, L1_ATTN_HALF), arena.take(TILES, L1_ATTN_HALF)
    gmax = arena.take(TILES * L1_ATTN_LOCAL)
    ff = arena.take(L1_ATTN_FF, SEQ)
    probs = Ring([ff[:, 2 * n:2 * n + 2, :].rearrange("p a (h c) -> p (a h) c", c=2 * P) for n in range(2)])
    turned = Ring([arena.take(2 * L1_ATTN_LOCAL, P) for _ in range(2)])
    top, sums, inv = arena.take(L1_ATTN_LOCAL, TILES), arena.take(TILES, L1_ATTN_LOCAL), arena.take(TILES, L1_ATTN_LOCAL)
    orow = arena.take(TILES, L1_ATTN_HALF)
    qgT = arena.take(SEQ)
    cum = [arena.take(L1_ATTN_BUCKETS - 1, L1_ATTN_HALF + 1) for _ in range(2)]
    ctx_inv, ctx_n = arena.take(L1_ATTN_BUCKETS - 1), arena.take(L1_ATTN_BUCKETS - 1, L1_ATTN_HALF)
    ybo, y2, yb2 = arena.take(TILES, P), arena.take(TILES, P), arena.take(TILES, P)
    ring = Ring(banks[0:8])

    weights = s.pool(nc.gpsimd.tensor_copy, static, At(lambda o, i: w.tensor[:, ds(o * layer_cols + w.at, layer_cols)]))
    loaded = s.dve(nc.vector.tensor_copy, y, tiles_of(Yall))
    with_bo = s.pool(nc.gpsimd.tensor_tensor, ybo, y, wl("bo").unsqueeze(1).broadcast_to([P, TILES, P]), ALU.add,
                     after=[loaded])
    rows = norm_rows(kit, s, y, h, mv, stats, rstd, LN_EPS, after=[loaded])
    feats = to_features(kit, s, ring, [h[:, t, :] for t in range(TILES)], hT, [rows, weights],
                        scale=wl("ln1_g"), bias=wl("ln1_b"))
    qk = []
    for name, dst in (("q", qT), ("k", kT)):
        bank, free, k = ring.take()
        made = s.mm(bank[:, :], wl(name), hT, after=[feats, *free])
        qk.append(s.act(nc.scalar.copy, dst, bank[:, :], after=[made]))
        ring.give(k, qk[-1])
    wide = 2 * L1_ATTN_HALF + P
    for pair in range(TILES // 2):
        bank, free, k = ring.take()
        for j in range(2):
            t = 2 * pair + j
            made = s.mm(bank[:, j * wide:(j + 1) * wide], hT[:, t * P:(t + 1) * P], wl("qkv"),
                        after=free if j == 0 else (), signal=j == 1)
        both = bank[:, :].rearrange("p (t d) -> p t d", t=2)
        at = slice(2 * pair, 2 * pair + 2)
        a = s.dve(nc.vector.tensor_copy, qg[:, at, :], both[:, :, 0:L1_ATTN_HALF], after=[made], link=False)
        b = s.dve(nc.vector.tensor_scalar, kg[:, at, :], both[:, :, L1_ATTN_HALF:2 * L1_ATTN_HALF], 0.0, None, ALU.min, link=False)
        c = s.dve(nc.vector.tensor_scalar, kpos[:, at, :], both[:, :, L1_ATTN_HALF:2 * L1_ATTN_HALF], 0.0, None, ALU.max, link=False)
        values = s.act(nc.scalar.copy, v[:, at, 0:P], both[:, :, 2 * L1_ATTN_HALF:wide], after=[c])
        ring.give(k, values)
    q16 = qg.rearrange("p t (h d) -> p (t h) d", d=L1_ATTN_HD)
    s.dve(nc.vector.tensor_reduce, gmax, q16, AX, ALU.max)
    centred = s.dve(nc.vector.tensor_tensor, q16, q16, over(gmax, L1_ATTN_HD), ALU.subtract)
    kexp = s.act(nc.scalar.activation, kg, kg, ACT.Exp, after=[centred])
    qexp = s.act(nc.scalar.activation, qg, qg, ACT.Exp)
    keys = s.dve(nc.vector.tensor_tensor, kg, kg, kpos, ALU.add, after=[kexp])
    s.dve(nc.vector.tensor_reduce, gmax, q16, AX, ALU.add, after=[qexp])
    s.dve(nc.vector.reciprocal, gmax, gmax)
    queries = s.dve(nc.vector.tensor_tensor, q16, q16, over(gmax, L1_ATTN_HD), ALU.mult)
    even, efree, ek = ring.take()
    odd, ofree, ok = ring.take()
    cw = L1_ATTN_HALF + 1
    hold(kit, s, even, [keys, values, *efree, *ofree])
    for u in range(L1_ATTN_BUCKETS - 1):
        t, lo = u // 2, (u % 2) * L1_ATTN_BUCKET
        into = odd if u % 2 else even
        made = s.mm(into[0:L1_ATTN_HALF, (u // 2) * cw:(u // 2 + 1) * cw], kg[lo:lo + L1_ATTN_BUCKET, t, :],
                    v[lo:lo + L1_ATTN_BUCKET, t, L1_ATTN_HALF:P + 1],
                    signal=u == L1_ATTN_BUCKETS - 2)
    n_even = L1_ATTN_BUCKETS // 2
    s.dve(nc.vector.tensor_copy, cum[0][0:L1_ATTN_HALF, 0:L1_ATTN_BUCKETS - 1:2, :],
          even[0:L1_ATTN_HALF, 0:n_even * cw].rearrange("p (u d) -> p u d", d=cw), after=[made])
    a0 = s.dve(nc.vector.tensor_copy, cum[0][0:L1_ATTN_HALF, 1:L1_ATTN_BUCKETS - 1:2, :],
               odd[0:L1_ATTN_HALF, 0:(n_even - 1) * cw].rearrange("p (u d) -> p u d", d=cw), link=False)
    ring.give(ek, a0)
    ring.give(ok, a0)
    a, b, n = cum[0], cum[1], 1
    while n < L1_ATTN_BUCKETS - 1:
        s.dve(nc.vector.tensor_copy, b[0:L1_ATTN_HALF, 0:n, :], a[0:L1_ATTN_HALF, 0:n, :])
        s.dve(nc.vector.tensor_tensor, b[0:L1_ATTN_HALF, n:L1_ATTN_BUCKETS - 1, :], a[0:L1_ATTN_HALF, n:L1_ATTN_BUCKETS - 1, :],
              a[0:L1_ATTN_HALF, 0:L1_ATTN_BUCKETS - 1 - n, :], ALU.add, link=False)
        a, b, n = b, a, 2 * n
    s.dve(nc.vector.tensor_scalar, ctx_inv[0:L1_ATTN_HALF, :], a[0:L1_ATTN_HALF, :, L1_ATTN_HALF], 1e-6, None, ALU.add)
    s.dve(nc.vector.reciprocal, ctx_inv[0:L1_ATTN_HALF, :], ctx_inv[0:L1_ATTN_HALF, :])
    s.dve(nc.vector.tensor_tensor, ctx_n[0:L1_ATTN_HALF, :, :], a[0:L1_ATTN_HALF, :, 0:L1_ATTN_HALF], over(ctx_inv[0:L1_ATTN_HALF, :], L1_ATTN_HALF), ALU.mult)
    contexts = s.dve(nc.vector.tensor_tensor, ctx_n[0:L1_ATTN_HALF, :, :], ctx_n[0:L1_ATTN_HALF, :, :],
                     kit.c("heads16").unsqueeze(1).broadcast_to([L1_ATTN_HALF, L1_ATTN_BUCKETS - 1, L1_ATTN_HALF]), ALU.mult)
    gqueries = to_features(kit, s, ring, [qg[:, t, :] for t in range(TILES)], qgT[0:L1_ATTN_HALF, :], [queries], rows=L1_ATTN_HALF)
    first = s.dve(nc.vector.memset, oT[L1_ATTN_HALF:P, 0:L1_ATTN_BUCKET], 0.0, link=False)
    bank, free, k = ring.take()
    hold(kit, s, bank, [contexts, gqueries, *free])
    for u in range(1, L1_ATTN_BUCKETS):
        made = s.mm(bank[L1_ATTN_HALF:P, u * L1_ATTN_BUCKET:(u + 1) * L1_ATTN_BUCKET], ctx_n[0:L1_ATTN_HALF, u - 1, :],
                    qgT[0:L1_ATTN_HALF, u * L1_ATTN_BUCKET:(u + 1) * L1_ATTN_BUCKET], signal=u == L1_ATTN_BUCKETS - 1)
    linear_out = s.act(nc.scalar.copy, oT[L1_ATTN_HALF:P, L1_ATTN_BUCKET:SEQ], bank[L1_ATTN_HALF:P, L1_ATTN_BUCKET:SEQ], after=[made, first])
    ring.give(k, linear_out)

    scale = L1_ATTN_HD ** -0.5

    def scores(first):
        out = []
        for hh in range(L1_ATTN_LOCAL):
            bank, free, k = ring.take()
            part = slice(32 * hh, 32 * hh + 32)
            for j in range(2):
                t, base = first + j, j * 2 * P
                lhs = qT[part, t * P:(t + 1) * P]
                s.mm(bank[:, base + P:base + 2 * P], kit.ident, kit.c("causal"), stop=False,
                     after=[*qk, *free] if j == 0 else (), signal=False)
                made = s.mm(bank[:, base + P:base + 2 * P], lhs, kT[part, t * P:(t + 1) * P], start=False,
                            signal=j == 1 and t == 0)
                if t:
                    made = s.mm(bank[:, base:base + P], lhs, kT[part, (t - 1) * P:t * P], signal=j == 1)
            out.append((bank, k, made))
        return out

    def maxima(first, got):
        for hh, (bank, k, made) in enumerate(got):
            if first:
                s.dve(nc.vector.tensor_reduce, top[:, hh, first:first + 2],
                      bank[:, :].rearrange("p (t c) -> p t c", t=2), AX, ALU.max, after=[made], link=False)
            else:
                for t, lo in ((0, P), (1, 2 * P)):
                    s.dve(nc.vector.tensor_reduce, top[:, hh, t:t + 1], bank[:, lo:2 * P * (t + 1)], AX, ALU.max,
                          after=[made], link=False)
        return s.dve(nc.vector.tensor_scalar, top[:, :, first:first + 2], top[:, :, first:first + 2], -scale, None,
                     ALU.mult)

    def softmax(t, got, neg):
        lo, base = (0 if t else P), (t % 2) * 2 * P
        pr, pfree, pk = probs.take()
        for hh, (bank, k, made) in enumerate(got):
            done = s.act(nc.scalar.activation, pr[:, hh, lo:2 * P], bank[:, base + lo:base + 2 * P],
                         ACT.Exp, scale=scale, bias=top[:, hh, t:t + 1], accum_out=sums[:, t, hh:hh + 1],
                         after=[neg, *(pfree if hh == 0 else ())])
            ring.give(k, done)
        return pr, pk, done

    def turn(t, pr, pk, done):
        sides = (0, 1) if t else (1,)
        dst, dfree, dk = turned.take()
        for side in sides:
            bank, free, k = ring.take()
            for hh in range(L1_ATTN_LOCAL):
                made = s.tr(bank[:, hh * P:(hh + 1) * P], pr[:, hh, side * P:(side + 1) * P], kit.ident,
                            after=[done, *free] if hh == 0 else (), signal=hh == L1_ATTN_LOCAL - 1)
            to = dst[:, side * L1_ATTN_LOCAL:(side + 1) * L1_ATTN_LOCAL, :].rearrange("p h q -> p (h q)")
            if side:
                last = moved = s.act(nc.scalar.copy, to, bank[:, :], after=[made, *dfree])
            else:
                before = moved = s.dve(nc.vector.tensor_copy, to, bank[:, :], after=[made, *dfree], link=False)
            ring.give(k, moved)
        probs.give(pk, made)
        return dst, dk, [last, before] if t else [last]

    def values_of(t, dst, dk, ready):
        bank, free, k = ring.take()
        sides = (0, 1) if t else (1,)
        for hh in range(L1_ATTN_LOCAL):
            for side in sides:
                made = s.mm(bank[:, hh * L1_ATTN_HD:(hh + 1) * L1_ATTN_HD], dst[:, side * L1_ATTN_LOCAL + hh, :],
                            v[:, t - 1 + side, hh * L1_ATTN_HD:(hh + 1) * L1_ATTN_HD], start=side == sides[0], stop=side == 1,
                            after=[*ready, *free, values] if hh == 0 and side == sides[0] else (),
                            signal=hh == L1_ATTN_LOCAL - 1 and side == 1)
        turned.give(dk, made)
        s.dve(nc.vector.reciprocal, inv[:, t, :], sums[:, t, :], after=[made])
        done = s.dve(nc.vector.tensor_tensor, orow[:, t, :].rearrange("p (h d) -> p h d", d=L1_ATTN_HD),
                     bank[:, 0:L1_ATTN_HALF].rearrange("p (h d) -> p h d", d=L1_ATTN_HD), over(inv[:, t, :], L1_ATTN_HD), ALU.mult)
        ring.give(k, done)
        return done

    for first in range(0, TILES, 2):
        got = scores(first)
        neg = maxima(first, got)
        for t in (first, first + 1):
            local = values_of(t, *turn(t, *softmax(t, got, neg)))
    local_out = to_features(kit, s, ring, [orow[:, t, :] for t in range(TILES)], oT[0:L1_ATTN_HALF, :], [local], rows=L1_ATTN_HALF)
    bank, free, k = ring.take()
    for t in range(TILES):
        made = s.mm(bank[:, t * P:(t + 1) * P], oT[:, t * P:(t + 1) * P], wl("o"),
                    after=[local_out, linear_out, *free] if t == 0 else (), signal=t == TILES - 1)
    attended = s.dve(nc.vector.tensor_tensor, y2, ybo, bank[:, :].rearrange("p (t d) -> p t d", d=P), ALU.add,
                     after=[made, with_bo])
    ring.give(k, attended)
    with_b2 = s.pool(nc.gpsimd.tensor_tensor, yb2, y2, wl("b2").unsqueeze(1).broadcast_to([P, TILES, P]), ALU.add,
                     after=[attended])
    rows = norm_rows(kit, s, y2, h, mv, stats, rstd, LN_EPS, after=[attended])
    feats = to_features(kit, s, ring, [h[:, t, :] for t in range(TILES)], hT, [rows],
                        scale=wl("ln2_g"), bias=wl("ln2_b"))
    for f in range(L1_ATTN_FF):
        bank, free, k = ring.take()
        made = s.mm(bank[:, :], wl("up", cols=(f * P, (f + 1) * P)), hT, after=[feats, *free])
        act = s.act(nc.scalar.activation, ff[:, f, :], bank[:, :], ACT.Gelu, bias=wl("b1", cols=(f, f + 1)),
                    after=[made])
        ring.give(k, act)
    bank, free, k = ring.take()
    for t in range(TILES):
        for f in range(L1_ATTN_FF):
            made = s.mm(bank[:, t * P:(t + 1) * P], ff[:, f, t * P:(t + 1) * P], wl(f"down{f}"), start=f == 0,
                        stop=f == L1_ATTN_FF - 1, after=[act, *free] if t == 0 and f == 0 else (),
                        signal=t == TILES - 1 and f == L1_ATTN_FF - 1)
    s.dve(nc.vector.tensor_tensor, tiles_of(Yall), yb2, bank[:, :].rearrange("p (t d) -> p t d", d=P), ALU.add,
          after=[made, with_b2])
    s.emit(L1_ATTN_LAYERS, BATCH)

    s = Section(kit.pr, "l1_leave")
    s.dve(nc.vector.tensor_tensor, X, X, Yall, ALU.add)
    s.emit()




L1_FFN_FF1 = 4
L1_FFN_ALL = BATCH * TILES
L1_FFN_PLACES = BATCH * SEQ // EXPERTS
L1_FFN_SCORE_BITS = 26


def layout_l1_ffn(w):
    parts = [("gate", w["gate_w"].T), ("gamma", w["ln_gamma"][:, None]), ("beta", w["ln_beta"][:, None]),
             ("b1", w["b1s"].reshape(EXPERTS * L1_FFN_FF1, P).T), ("b2", w["b2s"])]
    for e in range(EXPERTS):
        parts.append((f"up{e}", w["fc1s"][e].T))
        for f in range(L1_FFN_FF1):
            parts.append((f"down{e}_{f}", w["fc2s"][e][:, f * P:(f + 1) * P].T))
    return parts


def stage_l1_ffn(kit, w, arena):
    nc, X, E = kit.nc, kit.X, EXPERTS
    banks = kit.pr.banks
    scores = arena.take(L1_FFN_ALL, E)
    taken = arena.take(L1_FFN_ALL, E)
    xr, z, zT, y = arena.take(TILES, P), arena.take(TILES, P), arena.take(SEQ), arena.take(TILES, P)
    stats, mv, rstd = arena.take(TILES, 6), arena.take(TILES, 2), arena.take(TILES)

    s = Section(kit.pr, "l1_scores")
    ring = Ring(banks[0:4])
    loaded = s.dve(nc.vector.tensor_copy, xr, At(lambda o, i: X[:, ds(i * TILES, TILES), :]))
    rows = norm_rows(kit, s, xr, z, mv, stats, rstd, LN_EPS, after=[loaded])
    feats = to_features(kit, s, ring, [z[:, t, :] for t in range(TILES)], zT, [rows])
    for t in range(TILES):
        logits = s.mm(banks[7][:, t * E:(t + 1) * E], zT[:, t * P:(t + 1) * P], w("gate"),
                      after=[feats] if t == 0 else (), signal=(t == TILES - 1))
    part = y[:, 0, 0:TILES * E].rearrange("p (t e) -> p t e", e=E)
    tanh = s.act(nc.scalar.activation, part, banks[7][:, 0:TILES * E].rearrange("p (t e) -> p t e", e=E), ACT.Tanh,
                 after=[logits])
    s.dve(nc.vector.tensor_scalar, At(lambda o, i: scores[:, ds(i * TILES, TILES), :]), part, 1.0, 0.5,
          ALU.add, ALU.mult, after=[tanh])
    s.emit(1, BATCH)

    s = Section(kit.pr, "l1_threshold_start")
    cand, thr, step, keep, part8 = (arena.take(E) for _ in range(5))
    flags = arena.take(L1_FFN_ALL, E)
    s.dve(nc.vector.memset, thr, 0.0)
    s.dve(nc.vector.memset, step, 1.0, link=False)
    s.emit()
    s = Section(kit.pr, "l1_threshold")
    everyone = kit.c("ones")

    def count_flags():
        own = s.dve(nc.vector.tensor_reduce, part8, flags.rearrange("p t e -> p e t"), AX, ALU.add)
        return s.mm(banks[6][:, 0:E], everyone, part8, after=[own])

    s.dve(nc.vector.tensor_tensor, cand, thr, step, ALU.add)
    s.dve(nc.vector.tensor_tensor, flags, scores, cand.unsqueeze(1).broadcast_to([P, L1_FFN_ALL, E]), ALU.is_ge)
    total = count_flags()
    s.dve(nc.vector.tensor_scalar, keep, banks[6][:, 0:E], L1_FFN_PLACES - 0.5, None, ALU.is_gt, after=[total])
    s.dve(nc.vector.tensor_tensor, keep, keep, step, ALU.mult)
    s.dve(nc.vector.tensor_tensor, thr, thr, keep, ALU.add)
    s.dve(nc.vector.tensor_scalar, step, step, 0.5, None, ALU.mult)
    s.emit(1, L1_FFN_SCORE_BITS)

    s = Section(kit.pr, "l1_taken")
    need, pre0, pre1, sums = arena.take(E), arena.take(L1_FFN_ALL, E), arena.take(L1_FFN_ALL, E), arena.take(L1_FFN_ALL, E)
    bound = thr.unsqueeze(1).broadcast_to([P, L1_FFN_ALL, E])
    s.dve(nc.vector.tensor_tensor, flags, scores, bound, ALU.is_gt)
    total = count_flags()
    s.dve(nc.vector.tensor_scalar, need, banks[6][:, 0:E], -1.0, float(L1_FFN_PLACES), ALU.mult, ALU.add, after=[total])
    above = s.dve(nc.vector.tensor_copy, taken, flags)
    equal = s.dve(nc.vector.tensor_tensor, flags, scores, bound, ALU.is_equal)
    width = L1_FFN_ALL * E
    flat = flags.rearrange("p t e -> p (t e)")
    within = s.mm(banks[5][:, 0:width], kit.c("tri_strict"), flat, after=[equal])
    tile_sums = s.mm(banks[4][:, 0:width], everyone, flat)
    s.dve(nc.vector.tensor_copy, sums, banks[4][:, 0:width].rearrange("p (t e) -> p t e", e=E), after=[tile_sums])
    s.dve(nc.vector.memset, pre0[:, 0:1, :], 0.0)
    s.dve(nc.vector.tensor_copy, pre0[:, 1:L1_FFN_ALL, :], sums[:, 0:L1_FFN_ALL - 1, :])
    a, b, n = pre0, pre1, 1
    while n < L1_FFN_ALL:
        s.dve(nc.vector.tensor_copy, b[:, 0:n, :], a[:, 0:n, :])
        s.dve(nc.vector.tensor_tensor, b[:, n:L1_FFN_ALL, :], a[:, n:L1_FFN_ALL, :], a[:, 0:L1_FFN_ALL - n, :], ALU.add, link=False)
        a, b, n = b, a, n * 2
    s.dve(nc.vector.tensor_tensor, a, a, banks[5][:, 0:width].rearrange("p (t e) -> p t e", e=E), ALU.add,
          after=[within])
    s.dve(nc.vector.tensor_tensor, a, a, need.unsqueeze(1).broadcast_to([P, L1_FFN_ALL, E]), ALU.is_lt)
    s.dve(nc.vector.tensor_tensor, a, a, flags, ALU.mult)
    s.dve(nc.vector.tensor_tensor, taken, taken, a, ALU.add)
    s.dve(nc.vector.tensor_tensor, taken, taken, scores, ALU.mult)
    s.emit()

    s = Section(kit.pr, "l1_experts")
    acc, yT, shareT = arena.take(TILES, P), arena.take(SEQ), arena.take(SEQ)
    share = arena.take(TILES, E)
    hid = Ring([arena.take(L1_FFN_FF1, SEQ), arena.take(L1_FFN_FF1, SEQ)])
    ring, yring = Ring(banks[0:4]), Ring(banks[4:6])
    loaded = s.dve(nc.vector.tensor_copy, xr, At(lambda o, i: X[:, ds(i * TILES, TILES), :]))
    weights = s.dve(nc.vector.tensor_copy, share, At(lambda o, i: taken[:, ds(i * TILES, TILES), :]))
    rows = norm_rows(kit, s, xr, z, mv, stats, rstd, LN_EPS, after=[loaded])
    settle(kit, s)
    rows = norm_rows(kit, s, z, y, mv, stats, rstd, LN_EPS, after=[rows])
    feats = to_features(kit, s, ring, [y[:, t, :] for t in range(TILES)], yT, [rows], scale=w("gamma"), bias=w("beta"))
    shares = to_features(kit, s, ring, [share[:, t, :] for t in range(TILES)], shareT[0:E, :], [weights], rows=E)

    def hidden_all(e, started):
        hT, free, hk = hid.take()
        for f in range(L1_FFN_FF1):
            bank, bfree, k = ring.take()
            up = s.mm(bank[:, :], w(f"up{e}", cols=(f * P, (f + 1) * P)), yT, after=[*bfree, *started])
            c = e * L1_FFN_FF1 + f
            act = s.act(nc.scalar.activation, hT[:, f, :], bank[:, :], ACT.Gelu_apprx_tanh,
                        bias=w("b1", cols=(c, c + 1)), after=[up, *(free if f == 0 else ())])
            ring.give(k, act)
        return hT, hk, act

    done = weighted_experts(kit, s, hidden_all, lambda e, t: share[:, t, e:e + 1], acc,
                            lambda e, f: w(f"down{e}_{f}"), L1_FFN_FF1, hid, yring, [feats])
    bank, free, k = yring.take()
    for t in range(TILES):
        biases = s.mm(bank[:, t * P:(t + 1) * P], shareT[0:E, t * P:(t + 1) * P], w("b2"),
                      after=[shares, *free] if t == 0 else (), signal=(t == TILES - 1))
    s.dve(nc.vector.tensor_tensor, acc, acc, bank[:, :].rearrange("p (t d) -> p t d", d=P), ALU.add,
          after=[biases, done])
    s.dve(nc.vector.tensor_tensor, acc, acc, z, ALU.add)
    s.dve(nc.vector.tensor_tensor, At(lambda o, i: X[:, ds(i * TILES, TILES), :]), xr, acc, ALU.add)
    s.emit(1, BATCH)




L2_ATTN_CONV, L2_ATTN_DV = 4, 64
L2_ATTN_VAL = HEADS * L2_ATTN_DV
L2_ATTN_GROUPS = TILES * HEADS


def layout_l2_attn(w):
    bc = lambda v: np.broadcast_to(np.reshape(v, (1, -1)), (P, np.size(v)))
    parts = [("q", w["Wq"]), ("k", w["Wk"]), ("v", w["Wv"]), ("ab", np.concatenate([w["Wa"], w["Wb"]], axis=1)),
             ("gate", w["Wg"]), ("q_conv", w["conv_q_w"]), ("k_conv", w["conv_k_w"]),
             ("v_conv0", w["conv_v_w"][:P]), ("v_conv1", w["conv_v_w"][P:]), ("o0", w["Wo"][:P]), ("o1", w["Wo"][P:]),
             ("w2", w["W2"]), ("b2", bc(w["b2"])), ("ln1_g", bc(w["ln1_g"])), ("ln1_b", bc(w["ln1_b"])),
             ("dt", bc(w["dt_bias"])), ("A", bc(w["A_log"])), ("o_norm", np.tile(w["o_norm_w"], 2)[:, None])]
    return parts + [(c, w[c][:, None]) for c in ("rms_in_w", "ln2_g", "ln2_b")]


def stage_l2_attn(kit, w, arena):
    nc, X, banks = kit.nc, kit.X, kit.pr.banks
    before = [arena.take(L2_ATTN_CONV - 1 + SEQ) for _ in range(4)]
    rate = arena.take(HEADS)
    s = Section(kit.pr, "l2_start")
    for b in before:
        s.dve(nc.vector.memset, b[:, 0:L2_ATTN_CONV - 1], 0.0, link=False)
    grown = s.act(nc.scalar.activation, rate, w("A"), ACT.Exp)
    s.dve(nc.vector.tensor_scalar, rate, rate, -1.0, None, ALU.mult, after=[grown])
    s.emit()

    s = Section(kit.pr, "l2_attn")
    xr, z, a, hT = arena.take(TILES, P), arena.take(TILES, P), arena.take(TILES, P), arena.take(SEQ)
    stats, mv, rstd = arena.take(TILES, 6), arena.take(TILES, 2), arena.take(TILES)
    qrow, krow, kb = (arena.take(TILES, P) for _ in range(3))
    vrow, gates, orow = (arena.take(TILES, L2_ATTN_VAL) for _ in range(3))
    kT, kbq = arena.take(TILES, P), arena.take(TILES, 2, P)
    gt = arena.take(2, HEADS, P)
    gtm = arena.take(2, HEADS, P)
    conv = [gt[:, 0], gt[:, 1], gtm[:, 0], gtm[:, 1]]
    conv = [c.rearrange("p h n -> p (h n)") for c in conv]
    gtri = a
    beta, g, spread = arena.take(TILES, HEADS), arena.take(TILES, HEADS), arena.take(TILES, HEADS)
    t1, t2, t3 = (arena.take(TILES, HEADS) for _ in range(3))
    dec = arena.take(2 * L2_ATTN_GROUPS + TILES)
    ss, rn = arena.take(2, L2_ATTN_GROUPS), arena.take(2, L2_ATTN_GROUPS)
    delta = Delta(kit, arena, L2_ATTN_DV, True)
    ring = Ring(banks)
    flat = lambda v: v.rearrange("p t n -> p (t n)")
    heads = lambda v, d=DK: v.rearrange("p t (h d) -> p (t h) d", d=d)
    tok = lambda v: [v[:, t, :] for t in range(TILES)]
    blocks = lambda v: [v[:, t * P:(t + 1) * P] for t in range(TILES)]
    rows_of = lambda name: w(name).unsqueeze(1).broadcast_to([P, TILES, P])

    def inverse_root(dst, src, scale, eps, width, after):
        shifted = s.dve(nc.vector.tensor_scalar, src, src, scale, eps, ALU.mult, ALU.add, after=after)
        return s.pool(nc.gpsimd.tensor_tensor, dst, src, kit.c("neghalf", cols=(0, width)), ALU.pow, after=[shifted])

    loaded = s.dve(nc.vector.tensor_copy, xr, At(lambda o, i: X[:, ds(i * TILES, TILES), :]))
    rows = norm_rows(kit, s, xr, z, mv, stats, rstd, LN_EPS, after=[loaded])
    settle(kit, s)
    norm_rows(kit, s, z, a, mv, stats, rstd, LN_EPS, after=[rows])
    s.dve(nc.vector.tensor_tensor, a, a, rows_of("ln1_g"), ALU.mult)
    affine = s.dve(nc.vector.tensor_tensor, a, a, rows_of("ln1_b"), ALU.add)
    sq = s.act(nc.scalar.activation, kb, a, ACT.Square, after=[affine])
    s.dve(nc.vector.tensor_reduce, rstd, kb, AX, ALU.add, after=[sq])
    root = inverse_root(mv[:, :, 0], rstd, 1.0 / P, 1e-6, TILES, ())
    scaled = s.dve(nc.vector.tensor_tensor, a, a, over(mv[:, :, 0], P), ALU.mult, after=[root])
    feats = to_features(kit, s, ring, tok(a), hT, [scaled], scale=w("rms_in_w"))
    bank, free, k = ring.take()
    for t in range(TILES):
        made = s.mm(bank[:, t * 8:(t + 1) * 8], hT[:, t * P:(t + 1) * P], w("ab"), after=[feats, *free] if t == 0 else (),
                    signal=t == TILES - 1)
    ab = bank[:, 0:TILES * 8].rearrange("p (t c) -> p t c", c=8)
    betas = s.act(nc.scalar.activation, beta, ab[:, :, HEADS:8], ACT.Sigmoid, after=[made])
    s.dve(nc.vector.tensor_tensor, g, ab[:, :, 0:HEADS], w("dt").unsqueeze(1).broadcast_to([P, TILES, HEADS]), ALU.add,
          after=[made, betas])
    given = s.dve(nc.vector.tensor_scalar, t1, g, -1.0, None, ALU.mult)
    ring.give(k, given)
    low = s.dve(nc.vector.tensor_tensor, t1, t1, g, ALU.min)
    ex = s.act(nc.scalar.activation, t1, t1, ACT.Exp, after=[low])
    log1p(kit, s, t1, t2, t3, spread, after=[ex])
    s.dve(nc.vector.tensor_scalar, g, g, 0.0, None, ALU.max)
    s.dve(nc.vector.tensor_tensor, g, g, spread, ALU.add)
    logs = s.dve(nc.vector.tensor_tensor, g, g, rate.unsqueeze(1).broadcast_to([P, TILES, HEADS]), ALU.mult)
    gflat = g.rearrange("p t h -> p (t h)")
    wide = s.dve(nc.vector.tensor_copy, heads(orow[:, 0:2, :].rearrange("p a b -> p (a b)").rearrange(
        "p (t n) -> p t n", t=TILES)), over(gflat, DK))
    bank, free, k = ring.take()
    s.mm(bank[:, 0:L2_ATTN_GROUPS], kit.c("tri_incl"), gflat, after=[logs, wide, *free], signal=False)
    s.mm(bank[:, L2_ATTN_GROUPS:2 * L2_ATTN_GROUPS], kit.c("after"), gflat, signal=False)
    wide_rows = orow[:, 0:2, :].rearrange("p a b -> p (a b)")
    for t in range(TILES):
        made = s.mm(bank[:, 2 * L2_ATTN_GROUPS + t:2 * L2_ATTN_GROUPS + t + 1], wide_rows[:, t * P:(t + 1) * P],
                    kit.c("ones", cols=(0, 1)), signal=t == TILES - 1)
    decayed = s.act(nc.scalar.activation, dec, bank[:, 0:2 * L2_ATTN_GROUPS + TILES], ACT.Exp, after=[made])
    ring.give(k, decayed)
    from_start, to_end, whole = dec[:, 0:L2_ATTN_GROUPS], dec[:, L2_ATTN_GROUPS:2 * L2_ATTN_GROUPS], dec[:, 2 * L2_ATTN_GROUPS:]
    shaped = []
    for n, (name, cols, taps) in enumerate((("q", (0, P), "q_conv"), ("k", (0, P), "k_conv"),
                                            ("v", (0, P), "v_conv0"), ("v", (P, 2 * P), "v_conv1"))):
        bank, free, k = ring.take()
        made = s.mm(bank[:, :], w(name, cols=cols), hT, after=[feats, *free])
        moved = s.act(nc.scalar.copy, before[n][:, L2_ATTN_CONV - 1:], bank[:, :], after=[made])
        ring.give(k, moved)
        for j in range(L2_ATTN_CONV):
            view = before[n][:, j:j + SEQ]
            if j == 0:
                done = s.dve(nc.vector.tensor_scalar, conv[n], view, w(taps, cols=(0, 1)), None, ALU.mult,
                             after=[moved])
            else:
                done = s.dve(nc.vector.scalar_tensor_tensor, conv[n], view, w(taps, cols=(j, j + 1)), conv[n],
                             ALU.mult, ALU.add)
        shaped.append(s.act(nc.scalar.activation, conv[n], conv[n], ACT.Silu, after=[done]))
    for pair in range(2):
        bank, free, k = ring.take()
        for j in range(2):
            t = 2 * pair + j
            made = s.mm(bank[:, j * L2_ATTN_VAL:(j + 1) * L2_ATTN_VAL], hT[:, t * P:(t + 1) * P], w("gate"),
                        after=free if j == 0 else (), signal=j == 1)
        gated = s.act(nc.scalar.activation, gates[:, 2 * pair:2 * pair + 2, :],
                      bank[:, :].rearrange("p (t n) -> p t n", n=L2_ATTN_VAL), ACT.Silu, after=[made])
        ring.give(k, gated)
    turned = [to_features(kit, s, ring, blocks(conv[2 + n]), vrow[:, :, n * P:(n + 1) * P], [shaped[2 + n]])
              for n in range(2)]
    for n, dst in enumerate((qrow, krow)):
        raw = to_features(kit, s, ring, blocks(conv[n]), flat(dst), [shaped[n]])
        turned.append(raw)
        sq = s.act(nc.scalar.activation, kb, dst, ACT.Square, after=[raw, Token("DVE", s.count["DVE"])], link=True)
        s.dve(nc.vector.tensor_reduce, ss[:, n, :], heads(kb), AX, ALU.add, after=[sq])
        factor = float(DK) if n == 0 else 1.0
        root = inverse_root(rn[:, n, :], ss[:, n, :], factor, factor * 1e-6, L2_ATTN_GROUPS, ())
        unit = s.dve(nc.vector.tensor_tensor, heads(dst), heads(dst), over(rn[:, n, :], DK), ALU.mult, after=[root])
    by_beta = beta.rearrange("p t h -> p (t h)")
    s.dve(nc.vector.tensor_tensor, heads(kb), heads(krow), over(by_beta, DK), ALU.mult, after=[betas])
    ready = s.dve(nc.vector.tensor_tensor, heads(vrow, L2_ATTN_DV), heads(vrow, L2_ATTN_DV), over(by_beta, L2_ATTN_DV), ALU.mult,
                  after=turned)
    keyed = [to_features(kit, s, ring, tok(krow), flat(kT), [ready])]
    for n, src in enumerate((kb, qrow)):
        bank, free, k = ring.take()
        for t in range(TILES):
            made = s.tr(bank[:, t * P:(t + 1) * P], src[:, t, :], kit.ident, after=[ready, *free] if t == 0 else (),
                        signal=t == TILES - 1)
        keyed.append(s.act(nc.scalar.copy, kbq[:, :, n, :], bank[:, :].rearrange("p (t n) -> p t n", n=P),
                           after=[made]))
        ring.give(k, keyed[-1])
    s.dve(nc.vector.tensor_tensor, heads(kb), heads(kb), over(from_start, DK), ALU.mult, after=[decayed, *keyed])
    weighed = s.dve(nc.vector.tensor_tensor, heads(krow), heads(krow), over(to_end, DK), ALU.mult)

    state = delta.start(s)
    chunk_heads = lambda v, c, d=DK: v[:, c, :].rearrange("p (h d) -> p h d", d=d)
    for pair in range(2):
        chunks = (2 * pair, 2 * pair + 1)
        for j, c in enumerate(chunks):
            steps = s.dve(nc.vector.tensor_tensor, gtri, kit.c("tri_incl").unsqueeze(1).broadcast_to([P, HEADS, P]),
                          over(g[:, c, :], P), ALU.mult, after=[weighed, feats])
            bank, free, k = ring.take()
            made = s.mm(bank[:, :], kit.c("after"), flat(gtri), after=[steps, *free])
            pairwise = s.act(nc.scalar.activation, gt[:, j].rearrange("p h n -> p (h n)"), bank[:, :], ACT.Exp,
                             after=[made, Token("DVE", s.count["DVE"])])
            ring.give(k, pairwise)
            s.dve(nc.vector.tensor_tensor, gtm[:, j], gt[:, j],
                  kit.c("tri_incl").unsqueeze(1).broadcast_to([P, HEADS, P]), ALU.mult, after=[pairwise])
        settle(kit, s)
        xt, scored = delta.invert(s, ring, chunks, lambda c: kT[:, c, :],
                                  lambda c: kbq[:, c].rearrange("p a n -> p (a n)"), gt, keyed, gt_masked=gtm)
        for j, c in enumerate(chunks):
            state, got = delta.advance(s, ring, j, state, [*xt, *scored, weighed], kbq[:, c, 1, :],
                                       chunk_heads(vrow, c, L2_ATTN_DV), chunk_heads(kb, c), krow[:, c, :],
                                       chunk_heads(orow, c, L2_ATTN_DV), out_scale=from_start[:, c * HEADS:(c + 1) * HEADS],
                                       chunk_decay=whole[:, c:c + 1])
    sq = s.act(nc.scalar.activation, vrow, orow, ACT.Square, after=[got, state])
    s.dve(nc.vector.tensor_reduce, ss[:, 0, :], heads(vrow, L2_ATTN_DV), AX, ALU.add, after=[sq])
    root = inverse_root(rn[:, 0, :], ss[:, 0, :], 1.0 / L2_ATTN_DV, 1e-6, L2_ATTN_GROUPS, ())
    s.dve(nc.vector.tensor_tensor, orow, orow, gates, ALU.mult, after=[gated])
    ready = s.dve(nc.vector.tensor_tensor, heads(orow, L2_ATTN_DV), heads(orow, L2_ATTN_DV), over(rn[:, 0, :], L2_ATTN_DV), ALU.mult,
                  after=[root])
    oT = [conv[0], conv[1]]
    out_feats = [to_features(kit, s, ring, [orow[:, t, n * P:(n + 1) * P] for t in range(TILES)], oT[n], [ready],
                             scale=w("o_norm")) for n in range(2)]
    bank, free, k = ring.take()
    for t in range(TILES):
        for n in range(2):
            made = s.mm(bank[:, t * P:(t + 1) * P], oT[n][:, t * P:(t + 1) * P], w(f"o{n}"), start=n == 0,
                        stop=n == 1, after=[*out_feats, *free] if t == 0 and n == 0 else (),
                        signal=t == TILES - 1 and n == 1)
    by_tile = lambda bank: bank[:, :].rearrange("p (t d) -> p t d", d=P)
    added = s.dve(nc.vector.tensor_tensor, z, z, by_tile(bank), ALU.add, after=[made])
    ring.give(k, added)
    rows = norm_rows(kit, s, z, a, mv, stats, rstd, LN_EPS, after=[added])
    feats = to_features(kit, s, ring, tok(a), hT, [rows], scale=w("ln2_g"), bias=w("ln2_b"))
    bank, free, k = ring.take()
    for t in range(TILES):
        made = s.mm(bank[:, t * P:(t + 1) * P], hT[:, t * P:(t + 1) * P], w("w2"),
                    after=[feats, *free] if t == 0 else (), signal=t == TILES - 1)
    biased = s.dve(nc.vector.tensor_tensor, a, by_tile(bank), rows_of("b2"), ALU.add, after=[made])
    gelu = s.act(nc.scalar.activation, a, a, ACT.Gelu, after=[biased])
    s.dve(nc.vector.tensor_tensor, z, z, a, ALU.add, after=[gelu])
    s.dve(nc.vector.tensor_tensor, At(lambda o, i: X[:, ds(i * TILES, TILES), :]), xr, z, ALU.add)
    s.emit(1, BATCH)




L2_FFN_DEPTH, L2_FFN_HEADS, L2_FFN_HD = 2, 8, 64
L2_FFN_PAIRS = L2_FFN_HEADS // 2
L2_FFN_BACK = 64
L2_FFN_SPAN = L2_FFN_BACK + P
L2_FFN_HID = 341
L2_FFN_FF = 3
L2_FFN_WIDTH = [P, P, L2_FFN_HID - 2 * P]
L2_FFN_QK_SCALE = 8.0


def layout_l2_ffn(w):
    parts = []
    for n in range(L2_FFN_DEPTH):
        bc = lambda v: np.broadcast_to(v[None, :], (P, v.shape[0]))
        one = [("qkv", w["wqkv"][n]), ("up", w["w1"][n]), ("b2", bc(w["b2"][n]))]
        one += [(f"o{j}", w["wo"][n][j * P:(j + 1) * P]) for j in range(L2_FFN_PAIRS)]
        one += [(f"down{f}", w["w2"][n][f * P:f * P + L2_FFN_WIDTH[f]]) for f in range(L2_FFN_FF)]
        for half in range(2):
            one += [(f"b1_{half}_{f}", w["b1"][n][half * L2_FFN_HID + f * P:half * L2_FFN_HID + f * P + L2_FFN_WIDTH[f], None])
                    for f in range(L2_FFN_FF)]
        one += [(c, w[c][n][:, None]) for c in ("ln_g", "ln_b")]
        one += [(c, bc(w[c][n])) for c in ("q_scale", "k_scale")]
        parts += [(name if n == 0 else f"{name}@{n}", a) for name, a in one]
    return parts


def stage_l2_ffn(kit, w, arena):
    nc, X, banks = kit.nc, kit.X, kit.pr.banks
    layer_cols = w.where["qkv@1"][0] - w.where["qkv"][0]
    Yall = arena.take(BATCH * TILES, P)
    static = arena.take(layer_cols)
    wl = Weights(static, w.where)
    y = arena.take(TILES, P)
    stats, mv, rstd = arena.take(TILES, 6), arena.take(TILES, 2), arena.take(TILES)
    tiles_of = lambda A: At(lambda o, i: A[:, ds(i * TILES, TILES), :])
    h = arena.take(TILES, P)
    shifted = arena.take(SEQ + 1)
    probs = Ring([arena.take(4, 2 * P) for _ in range(2)])

    s = Section(kit.pr, "l2f_enter")
    loaded = s.dve(nc.vector.tensor_copy, h, tiles_of(X))
    rows = norm_rows(kit, s, h, y, mv, stats, rstd, LN_EPS, after=[loaded])
    s.dve(nc.vector.tensor_copy, tiles_of(Yall), y)
    s.emit(1, BATCH)
    s = Section(kit.pr, "l2f_zero")
    s.dve(nc.vector.memset, shifted[:, 0:1], 0.0)
    for pr in probs.items:
        s.dve(nc.vector.memset, pr[:, :, 0:L2_FFN_BACK], 0.0, link=False)
    s.emit()

    s = Section(kit.pr, "l2f_layers")
    rope = {n: arena.take(TILES, L2_FFN_HD) for n in ("cos_q", "sin_q", "cos_k", "sin_k")}
    qT = Ring([arena.take(L2_FFN_PAIRS, P) for _ in range(2)])
    kT = arena.take(L2_FFN_PAIRS, SEQ)
    v = arena.take(TILES, L2_FFN_HEADS * L2_FFN_HD)
    scratch = arena.take(4, L2_FFN_HEADS * L2_FFN_HD)
    cos_part, sin_part = scratch[:, 0], scratch[:, 1]
    square = sin_part
    orow = Ring([scratch[:, 2]])
    oT = Ring([scratch[:, 3]])
    turned = Ring([arena.take(8, P) for _ in range(1)])
    ss, rn = arena.take(L2_FFN_HEADS), arena.take(2, L2_FFN_HEADS)
    top, sums, inv = arena.take(L2_FFN_HEADS), arena.take(L2_FFN_HEADS), arena.take(L2_FFN_HEADS)
    ff = kT.rearrange("p a b -> p (a b)")[:, 0:L2_FFN_FF * SEQ].rearrange("p (f c) -> p f c", f=L2_FFN_FF)
    gel = Ring([scratch[:, 0], scratch[:, 1]])
    ring, oring = Ring(banks[0:7]), Ring([banks[7]])

    weights = s.pool(nc.gpsimd.tensor_copy, static, At(lambda o, i: w.tensor[:, ds(o * layer_cols + w.at, layer_cols)]))
    loaded = s.dve(nc.vector.tensor_copy, y, tiles_of(Yall))

    def shift(rows, after):
        bank, free, k = ring.take()
        for t in range(TILES):
            made = s.tr(bank[:, t * P:(t + 1) * P], rows[:, t, :], kit.ident,
                        after=[*after, *free] if t == 0 else (), signal=t == TILES - 1)
        s.act(nc.scalar.copy, shifted[0:64, 0:SEQ], bank[0:64, :], after=[made])
        done = s.act(nc.scalar.copy, shifted[64:P, 1:SEQ + 1], bank[64:P, :])
        ring.give(k, done)
        return done

    feats = shift(y, [loaded])
    xT = shifted[:, 0:SEQ]
    for side in "qk":
        sc = wl(f"{side}_scale")
        for name, lo, hi, frm in ((f"cos_{side}", 0, L2_FFN_HD, 0), (f"sin_{side}", 0, L2_FFN_HD // 2, L2_FFN_HD // 2),
                                  (f"sin_{side}", L2_FFN_HD // 2, L2_FFN_HD, 0)):
            tab = kit.c(name).rearrange("p (t d) -> p t d", d=L2_FFN_HD)
            tables = s.dve(nc.vector.tensor_tensor, rope[name][:, :, lo:hi], tab[:, :, lo:hi],
                           sc[:, frm:frm + hi - lo].unsqueeze(1).broadcast_to([P, TILES, hi - lo]), ALU.mult,
                           after=[weights], link=False)
    settle(kit, s)

    def heads3(view):
        return view.rearrange("p (h d) -> p h d", d=L2_FFN_HD)

    def project(t):
        made = []
        for part in range(3):
            bank, free, k = ring.take()
            made.append((bank, k, s.mm(bank[:, :], xT[:, t * P:(t + 1) * P],
                                       wl("qkv", cols=(part * 512, (part + 1) * 512)),
                                       after=[feats, weights, *free])))
        q_dst, qfree, qk = qT.take()
        moved = []
        for part, side in enumerate("qk"):
            bank, k, got = made[part]
            sq = s.act(nc.scalar.activation, square, bank[:, :], ACT.Square,
                       after=[got, Token("DVE", s.count["DVE"])])
            s.dve(nc.vector.tensor_reduce, ss, heads3(square), AX, ALU.add, after=[sq])
            floor = s.dve(nc.vector.tensor_scalar, ss, ss, 1e-24, None, ALU.max)
            root = s.pool(nc.gpsimd.tensor_tensor, rn[:, part, :], ss, kit.c("neghalf", cols=(0, L2_FFN_HEADS)), ALU.pow,
                          after=[floor])
            cos, sin = rope[f"cos_{side}"][:, t, :], rope[f"sin_{side}"][:, t, :]
            src = heads3(bank[:, :])
            free_before = moved[-1:] if moved else []
            s.dve(nc.vector.tensor_tensor, heads3(cos_part), src,
                  cos.unsqueeze(1).broadcast_to([P, L2_FFN_HEADS, L2_FFN_HD]), ALU.mult, after=free_before)
            for lo, frm in ((0, L2_FFN_HD // 2), (L2_FFN_HD // 2, 0)):
                last = s.dve(nc.vector.tensor_tensor, heads3(sin_part)[:, :, lo:lo + L2_FFN_HD // 2],
                             src[:, :, frm:frm + L2_FFN_HD // 2],
                             sin[:, lo:lo + L2_FFN_HD // 2].unsqueeze(1).broadcast_to([P, L2_FFN_HEADS, L2_FFN_HD // 2]), ALU.mult,
                             link=False)
            ring.give(k, last)
            s.dve(nc.vector.tensor_tensor, cos_part, cos_part, sin_part, ALU.add)
            done = s.dve(nc.vector.tensor_tensor, heads3(cos_part), heads3(cos_part), over(rn[:, part, :], L2_FFN_HD),
                         ALU.mult, after=[root])
            bank, free, k = ring.take()
            for j in range(L2_FFN_PAIRS):
                flipped = s.tr(bank[:, j * P:(j + 1) * P], cos_part[:, j * P:(j + 1) * P], kit.ident,
                               after=[done, *free] if j == 0 else (), signal=j == L2_FFN_PAIRS - 1)
            dst = q_dst if side == "q" else kT[:, :, t * P:(t + 1) * P]
            moved.append(s.act(nc.scalar.copy, dst, bank[:, :].rearrange("p (j c) -> p j c", j=L2_FFN_PAIRS),
                               after=[flipped, *(qfree if side == "q" else ())]))
            ring.give(k, moved[-1])
        bank, k, got = made[2]
        values = s.act(nc.scalar.copy, v[:, t, :], bank[:, :], after=[got])
        ring.give(k, values)
        return q_dst, qk, [*moved, values]

    def attend(t, q_src, qk, ready):
        keys_at = slice(max(t * P - L2_FFN_BACK, 0), (t + 1) * P)
        lo = 0 if t else L2_FFN_BACK
        n = L2_FFN_SPAN - lo
        obank, ofree, okk = oring.take()
        for group in range(2):
            got = []
            for side in range(2):
                bank, free, k = ring.take()
                part = slice(64 * side, 64 * side + 64)
                for j in range(2):
                    out = bank[:, j * L2_FFN_SPAN:j * L2_FFN_SPAN + n]
                    s.mm(out, kit.ident, kit.c("band", cols=(lo, L2_FFN_SPAN)), stop=False,
                         after=[*ready, *free] if j == 0 else (), signal=False)
                    made = s.mm(out, q_src[part, 2 * group + j, :], kT[part, 2 * group + j, keys_at], start=False,
                                signal=j == 1)
                got.append((bank, k, made))
            pr, pfree, pk = probs.take()
            for side, (bank, k, made) in enumerate(got):
                for j in range(2):
                    c = 4 * group + 2 * j + side
                    s.dve(nc.vector.tensor_reduce, top[:, c:c + 1], bank[:, j * L2_FFN_SPAN:j * L2_FFN_SPAN + n], AX, ALU.max,
                          after=[made], link=False)
            these = slice(4 * group, 4 * group + 4)
            neg = s.dve(nc.vector.tensor_scalar, top[:, these], top[:, these], -L2_FFN_QK_SCALE, None, ALU.mult)
            for side, (bank, k, made) in enumerate(got):
                for j in range(2):
                    hh = 2 * j + side
                    c = 4 * group + hh
                    done = s.act(nc.scalar.activation, pr[:, hh, L2_FFN_BACK + lo:2 * P], bank[:, j * L2_FFN_SPAN:j * L2_FFN_SPAN + n],
                                 ACT.Exp, scale=L2_FFN_QK_SCALE, bias=top[:, c:c + 1], accum_out=sums[:, c:c + 1],
                                 after=[neg, *pfree])
                    pfree = ()
                ring.give(k, done)
            dst, dfree, dk = turned.take()
            flips = []
            for side in ((0, 1) if t else (1,)):
                bank, free, k = ring.take()
                for hh in range(4):
                    made = s.tr(bank[:, hh * P:(hh + 1) * P], pr[:, hh, side * P:(side + 1) * P], kit.ident,
                                after=[done, *free] if hh == 0 else (), signal=hh == 3)
                to = dst[:, 4 * side:4 * side + 4, :].rearrange("p h q -> p (h q)")
                if side:
                    flips.append(s.act(nc.scalar.copy, to, bank[:, :], after=[made, *dfree]))
                else:
                    flips.append(s.dve(nc.vector.tensor_copy, to, bank[:, :], after=[made, *dfree], link=False))
                ring.give(k, flips[-1])
            probs.give(pk, made)
            for hh in range(4):
                c = 4 * group + hh
                cols = slice(c * L2_FFN_HD, (c + 1) * L2_FFN_HD)
                for side in ((0, 1) if t else (1,)):
                    out = s.mm(obank[:, cols], dst[:, 4 * side + hh, :], v[:, t - 1 + side, cols],
                               start=side == 1 and t == 0 or side == 0, stop=side == 1,
                               after=[*flips, *ofree] if hh == 0 else (), signal=hh == 3 and side == 1)
            turned.give(dk, out)
        qT.give(qk, out)
        s.dve(nc.vector.reciprocal, inv, sums, after=[out])
        row, rfree, rk = orow.take()
        normed = s.dve(nc.vector.tensor_tensor, heads3(row), heads3(obank[:, :]), over(inv, L2_FFN_HD), ALU.mult,
                       after=rfree)
        oring.give(okk, normed)
        oT_, tfree, tk = oT.take()
        flipped = to_features(kit, s, ring, [row[:, j * P:(j + 1) * P] for j in range(L2_FFN_PAIRS)], oT_, [normed, *tfree])
        orow.give(rk, flipped)
        bank, free, k = ring.take()
        for j in range(L2_FFN_PAIRS):
            made = s.mm(bank[:, 0:P], oT_[:, j * P:(j + 1) * P], wl(f"o{j}"), start=j == 0, stop=j == L2_FFN_PAIRS - 1,
                        after=[flipped, *free] if j == 0 else (), signal=j == L2_FFN_PAIRS - 1)
        oT.give(tk, made)
        done = s.dve(nc.vector.tensor_tensor, y[:, t, :], y[:, t, :], bank[:, 0:P], ALU.add, after=[made])
        ring.give(k, done)
        return done

    for t in range(TILES):
        attended = attend(t, *project(t))

    with_b2 = s.pool(nc.gpsimd.tensor_tensor, h, y, wl("b2").unsqueeze(1).broadcast_to([P, TILES, P]), ALU.add,
                     after=[attended])
    feats = shift(y, [attended])
    bank, free, k = ring.take()
    for t in range(TILES):
        made = s.tr(bank[:, t * P:(t + 1) * P], xT[:, t * P:(t + 1) * P], kit.ident,
                    after=[feats, *free] if t == 0 else (), signal=t == TILES - 1)
    normed = norm_rows(kit, s, bank[:, :].rearrange("p (t d) -> p t d", d=P), y, mv, stats, rstd, LN_EPS,
                       after=[made, feats, with_b2])
    ring.give(k, normed)
    hT = v[:, 0, :]
    feats = to_features(kit, s, ring, [y[:, t, :] for t in range(TILES)], hT, [normed],
                        scale=wl("ln_g"), bias=wl("ln_b"))
    for f in range(L2_FFN_FF):
        n = L2_FFN_WIDTH[f]
        parts = []
        for half in range(2):
            bank, free, k = ring.take()
            at = half * L2_FFN_HID + f * P
            parts.append((bank, k, s.mm(bank[0:n, :], wl("up", cols=(at, at + n)), hT, after=[feats, *free])))
        g, gfree, gk = gel.take()
        bank, k, made = parts[1]
        gelu = s.act(nc.scalar.activation, g[0:n, :], bank[0:n, :], ACT.Gelu, bias=wl(f"b1_1_{f}"),
                     after=[made, *gfree])
        ring.give(k, gelu)
        bank, k, made = parts[0]
        gated = s.dve(nc.vector.scalar_tensor_tensor, ff[0:n, f, :], bank[0:n, :], wl(f"b1_0_{f}"), g[0:n, :],
                      ALU.add, ALU.mult, after=[made, gelu], link=False)
        ring.give(k, gated)
        gel.give(gk, gated)
    bank, free, k = ring.take()
    for t in range(TILES):
        for f in range(L2_FFN_FF):
            made = s.mm(bank[:, t * P:(t + 1) * P], ff[0:L2_FFN_WIDTH[f], f, t * P:(t + 1) * P], wl(f"down{f}"),
                        start=f == 0, stop=f == L2_FFN_FF - 1, after=[gated, *free] if t == 0 and f == 0 else (),
                        signal=t == TILES - 1 and f == L2_FFN_FF - 1)
    s.dve(nc.vector.tensor_tensor, tiles_of(Yall), h, bank[:, :].rearrange("p (t d) -> p t d", d=P), ALU.add,
          after=[made])
    s.emit(L2_FFN_DEPTH, BATCH)

    s = Section(kit.pr, "l2f_leave")
    s.dve(nc.vector.tensor_tensor, X, X, Yall, ALU.add)
    s.emit()





def layout_l3_attn(w):
    col = lambda a: np.broadcast_to(np.reshape(a, (1, 1)), (P, 1))
    return [("write", w["W_write"].T), ("read", w["W_read"].T), ("decay", col(w["decay"])),
            ("log_alpha", col(w["log_alpha"]))]


def stage_l3_attn(kit, w, arena):
    nc, X, banks = kit.nc, kit.X, kit.pr.banks
    s = Section(kit.pr, "l3_powers")
    e, u, rest, lg, chunk_decay, alpha = (arena.take(1) for _ in range(6))
    decay_to, from_start, to_end, read = arena.take(P), arena.take(P), arena.take(1), arena.take(P)
    ex = s.act(nc.scalar.activation, e, w("decay"), ACT.Exp, scale=-1.0)
    log = log1p(kit, s, e, u, rest, lg, after=[ex])
    neg = s.dve(nc.vector.tensor_scalar, lg, lg, -1.0, None, ALU.mult)
    p1 = s.act(nc.scalar.activation, decay_to, kit.c("lag"), ACT.Exp, scale=lg, after=[neg])
    s.act(nc.scalar.activation, from_start, kit.c("place"), ACT.Exp, scale=lg)
    s.act(nc.scalar.activation, to_end, kit.c("left"), ACT.Exp, scale=lg)
    s.act(nc.scalar.activation, chunk_decay, lg, ACT.Exp, scale=float(P))
    p2 = s.act(nc.scalar.activation, alpha, w("log_alpha"), ACT.Exp)
    s.dve(nc.vector.tensor_tensor, decay_to, decay_to, kit.c("tri_strict"), ALU.mult, after=[p1])
    s.dve(nc.vector.tensor_scalar, read, w("read"), alpha, None, ALU.mult, after=[p2])
    s.emit()

    s = Section(kit.pr, "l3_attn")
    xr, z, zT, vT = arena.take(TILES, P), arena.take(TILES, P), arena.take(SEQ + 1), arena.take(TILES, P)
    stats, mv, rstd = arena.take(TILES, 6), arena.take(TILES, 2), arena.take(TILES)
    v, vg, wk, st, qd = (arena.take(TILES, P) for _ in range(5))
    reads = arena.take(SEQ)
    Wm = Ring([arena.take(P), arena.take(P)])
    ring = Ring(banks)
    loaded = s.dve(nc.vector.tensor_copy, xr, At(lambda o, i: X[:, ds(i * TILES, TILES), :]))
    rows = norm_rows(kit, s, xr, z, mv, stats, rstd, LN_EPS, after=[loaded])
    cleared = s.dve(nc.vector.memset, zT[:, 0:1], 0.0, link=False)
    key, query = zT[:, 0:SEQ], zT[:, 1:SEQ + 1]
    feats = to_features(kit, s, ring, [z[:, t, :] for t in range(TILES)], query, [rows])
    bank, free, k = ring.take()
    for t in range(TILES):
        values = s.mm(bank[:, t * P:(t + 1) * P], query[:, t * P:(t + 1) * P], w("write"),
                      after=[feats, *free] if t == 0 else (), signal=t == TILES - 1)
    bank4 = bank[:, :].rearrange("p (t d) -> p t d", d=P)
    vals = s.act(nc.scalar.copy, v, bank4, after=[values])
    vals_end = s.dve(nc.vector.tensor_scalar, vg, bank4, to_end, None, ALU.mult, after=[values, vals])
    ring.give(k, vals, vals_end)
    keys = to_features(kit, s, ring, [key[:, t * P:(t + 1) * P] for t in range(TILES)],
                       wk.rearrange("p t d -> p (t d)"), [feats, cleared])
    decayed = s.dve(nc.vector.tensor_tensor, qd, query.rearrange("p (t d) -> p t d", d=P),
                    from_start.unsqueeze(1).broadcast_to([P, TILES, P]), ALU.mult, after=[feats])
    bank, free, k = ring.take()
    for t in range(TILES):
        cols = slice(t * P, (t + 1) * P)
        pairs = s.mm(bank[:, cols], key[:, cols], query[:, cols], after=free if t == 0 else (), signal=t == TILES - 1)
    weighed = s.dve(nc.vector.tensor_tensor, st, bank[:, :].rearrange("p (t d) -> p t d", d=P),
                    decay_to.unsqueeze(1).broadcast_to([P, TILES, P]), ALU.mult, after=[pairs])
    ring.give(k, weighed)
    memory, ready = None, None
    rbank, rfree, rk = ring.take()
    for t in range(TILES):
        cols = slice(t * P, (t + 1) * P)
        out = s.mm(rbank[:, cols], v[:, t, :], st[:, t, :], stop=(t == 0), after=[vals, weighed, *rfree],
                   signal=(t == 0))
        if t > 0:
            out = s.mm(rbank[:, cols], memory, qd[:, t, :], start=False, after=[ready, decayed])
        if t < TILES - 1:
            mbank, mfree, mk = ring.take()
            added = s.mm(mbank[:, 0:P], wk[:, t, :], vg[:, t, :], after=[keys, vals_end, *mfree])
            new, nfree, nk = Wm.take()
            if t == 0:
                ready = s.dve(nc.vector.tensor_copy, new, mbank[:, 0:P], after=[added])
            else:
                ready = s.dve(nc.vector.scalar_tensor_tensor, new, memory, chunk_decay, mbank[:, 0:P], ALU.mult,
                              ALU.add, after=[added, *nfree])
            ring.give(mk, ready)
            if t > 0:
                Wm.give((nk + 1) % 2, out)
            memory = new
    copied = s.act(nc.scalar.copy, reads, rbank[:, :], after=[out])
    ring.give(rk, copied)
    bank, free, k = ring.take()
    for t in range(TILES):
        back = s.mm(bank[:, t * P:(t + 1) * P], reads[:, t * P:(t + 1) * P], read,
                    after=[copied, *free] if t == 0 else (), signal=t == TILES - 1)
    s.dve(nc.vector.tensor_tensor, z, z, bank[:, :].rearrange("p (t d) -> p t d", d=P), ALU.add, after=[back])
    s.dve(nc.vector.tensor_tensor, At(lambda o, i: X[:, ds(i * TILES, TILES), :]), xr, z, ALU.add)
    s.emit(1, BATCH)




L3_FFN_GLU = 256
L3_FFN_HALVES = L3_FFN_GLU // P


def layout_l3_ffn(w):
    parts = [("router", w["Wgate"]), ("router_bias", np.broadcast_to(w["bgate"][None, :], (P, EXPERTS))),
             ("out_bias", w["b3"])]
    for n in ("b1", "b2", "bg", "bl"):
        parts.append((n, w[n].reshape(EXPERTS * L3_FFN_HALVES, P).T))
    for e in range(EXPERTS):
        parts += [(f"one{e}", w["W1"][e]), (f"two{e}", w["W2"][e])]
        for f in range(L3_FFN_HALVES):
            rows = slice(f * P, (f + 1) * P)
            parts += [(f"gate{e}_{f}", w["Wg"][e][rows]), (f"lin{e}_{f}", w["Wl"][e][rows]),
                      (f"down{e}_{f}", w["W3"][e][rows])]
    return parts


def stage_l3_ffn(kit, w, arena):
    nc, X = kit.nc, kit.X
    s = Section(kit.pr, "l3_ffn")
    xr, h, xT = arena.take(TILES, P), arena.take(TILES, P), arena.take(SEQ)
    acc, hid0, hid1 = arena.take(TILES, P), arena.take(L3_FFN_HALVES, SEQ), arena.take(L3_FFN_HALVES, SEQ)
    z, z2 = Ring([arena.take(L3_FFN_HALVES, SEQ) for _ in range(2)]), Ring([arena.take(SEQ) for _ in range(2)])
    sg, gg = Ring([arena.take(SEQ) for _ in range(2)]), Ring([arena.take(SEQ) for _ in range(2)])
    stats, mv, rstd = arena.take(TILES, 6), arena.take(TILES, 2), arena.take(TILES)
    logit, above, equal, pa, pb, share = (arena.take(TILES, EXPERTS) for _ in range(6))
    best, count, need = arena.take(TILES, 8), arena.take(TILES), arena.take(TILES)
    shareT = arena.take(SEQ)
    banks = kit.pr.banks
    ring, yring, hid = Ring(banks[0:5]), Ring(banks[5:7]), Ring([hid0, hid1])
    E = EXPERTS

    loaded = s.dve(nc.vector.tensor_copy, xr, At(lambda o, i: X[:, ds(i * TILES, TILES), :]))
    rows = norm_rows(kit, s, xr, h, mv, stats, rstd, LN_EPS, after=[loaded])
    feats = to_features(kit, s, ring, [h[:, t, :] for t in range(TILES)], xT, [rows])
    for t in range(TILES):
        logits = s.mm(banks[7][:, t * E:(t + 1) * E], xT[:, t * P:(t + 1) * P], w("router"),
                      after=[feats] if t == 0 else (), signal=(t == TILES - 1))
    s.dve(nc.vector.tensor_tensor, logit, banks[7][:, 0:TILES * E].rearrange("p (t e) -> p t e", e=E),
          w("router_bias").unsqueeze(1).broadcast_to([P, TILES, E]), ALU.add, after=[logits])
    settle(kit, s)
    for t in range(TILES):
        s.dve(nc.vector.max, best[:, t, :], logit[:, t, :], link=False)
    s.dve(nc.vector.tensor_tensor, above, logit, over(best[:, :, 1], E), ALU.is_gt)
    s.dve(nc.vector.tensor_tensor, equal, logit, over(best[:, :, 1], E), ALU.is_equal, link=False)
    s.dve(nc.vector.tensor_reduce, count, above, AX, ALU.add)
    s.dve(nc.vector.tensor_scalar, need, count, -1.0, 2.0, ALU.mult, ALU.add)
    pre = prefix_exclusive(kit, s, equal, (pa, pb), E)
    s.dve(nc.vector.tensor_tensor, pre, pre, over(need, E), ALU.is_lt)
    s.dve(nc.vector.tensor_tensor, equal, equal, pre, ALU.mult)
    s.dve(nc.vector.tensor_tensor, above, above, equal, ALU.add)
    centred = s.dve(nc.vector.tensor_tensor, logit, logit, over(best[:, :, 0], E), ALU.subtract)
    powers = s.act(nc.scalar.activation, logit, logit, ACT.Exp, after=[centred])
    s.dve(nc.vector.tensor_tensor, share, logit, above, ALU.mult, after=[powers])
    s.dve(nc.vector.tensor_reduce, count, share, AX, ALU.add)
    s.dve(nc.vector.reciprocal, count, count)
    weights = s.dve(nc.vector.tensor_tensor, share, share, over(count, E), ALU.mult)
    shares = to_features(kit, s, ring, [share[:, t, :] for t in range(TILES)], shareT[0:E, :], [weights], rows=E)

    def hidden_all(e, started):
        zt, zfree, zk = z.take()
        for f in range(L3_FFN_HALVES):
            b1, free1, k1 = ring.take()
            one = s.mm(b1[:, :], w(f"one{e}", cols=(f * P, (f + 1) * P)), xT, after=[*free1, *started])
            b2, free2, k2 = ring.take()
            two = s.mm(b2[:, :], w(f"two{e}", cols=(f * P, (f + 1) * P)), xT, after=free2)
            c = e * L3_FFN_HALVES + f
            t2, tfree, tk = z2.take()
            second = s.act(nc.scalar.activation, t2, b2[:, :], ACT.Identity, bias=w("b2", cols=(c, c + 1)),
                           after=[two, *tfree])
            ring.give(k2, second)
            both = s.dve(nc.vector.scalar_tensor_tensor, zt[:, f, :], b1[:, :], w("b1", cols=(c, c + 1)), t2,
                         ALU.add, ALU.mult, after=[one, second, *(zfree if f == 0 else ())], link=False)
            ring.give(k1, both)
            z2.give(tk, both)
        hT, hfree, hk = hid.take()
        for g in range(L3_FFN_HALVES):
            cols = (g * P, (g + 1) * P)
            bg, freeg, kg = ring.take()
            for f in range(L3_FFN_HALVES):
                gate = s.mm(bg[:, :], w(f"gate{e}_{f}", cols=cols), zt[:, f, :], start=f == 0, stop=f == L3_FFN_HALVES - 1,
                            after=[*freeg, both] if f == 0 else (), signal=f == L3_FFN_HALVES - 1)
            bl, freel, kl = ring.take()
            for f in range(L3_FFN_HALVES):
                lin = s.mm(bl[:, :], w(f"lin{e}_{f}", cols=cols), zt[:, f, :], start=f == 0, stop=f == L3_FFN_HALVES - 1,
                           after=freel if f == 0 else (), signal=f == L3_FFN_HALVES - 1)
            c = e * L3_FFN_HALVES + g
            gb, gfree, gk = gg.take()
            silu = s.act(nc.scalar.activation, gb, bg[:, :], ACT.Silu, bias=w("bg", cols=(c, c + 1)),
                         after=[gate, *gfree])
            ring.give(kg, silu)
            out = s.dve(nc.vector.scalar_tensor_tensor, hT[:, g, :], bl[:, :], w("bl", cols=(c, c + 1)), gb,
                        ALU.add, ALU.mult, after=[lin, silu, *(hfree if g == 0 else ())], link=False)
            ring.give(kl, out)
            gg.give(gk, out)
        z.give(zk, lin)
        return hT, hk, out

    done = weighted_experts(kit, s, hidden_all, lambda e, t: share[:, t, e:e + 1], acc,
                            lambda e, f: w(f"down{e}_{f}"), L3_FFN_HALVES, hid, yring, [feats])
    bank, free, k = yring.take()
    for t in range(TILES):
        biases = s.mm(bank[:, t * P:(t + 1) * P], shareT[0:E, t * P:(t + 1) * P], w("out_bias"),
                      after=[shares, *free] if t == 0 else (), signal=(t == TILES - 1))
    s.dve(nc.vector.tensor_tensor, acc, acc, bank[:, :].rearrange("p (t d) -> p t d", d=P), ALU.add,
          after=[biases, done])
    s.dve(nc.vector.tensor_tensor, At(lambda o, i: X[:, ds(i * TILES, TILES), :]), xr, acc, ALU.add)
    s.emit(1, BATCH)




STAGES = [("L0_attn_", layout_l0_attn, stage_l0_attn), ("L0_ffn_", layout_l0_ffn, stage_l0_ffn),
          ("L1_attn_", layout_l1_attn, stage_l1_attn), ("L1_ffn_", layout_l1_ffn, stage_l1_ffn),
          ("L2_attn_", layout_l2_attn, stage_l2_attn), ("L2_ffn_", layout_l2_ffn, stage_l2_ffn),
          ("L3_attn_", layout_l3_attn, stage_l3_attn), ("L3_ffn_", layout_l3_ffn, stage_l3_ffn)]
WORK_COLUMNS = 20500


def build(nc, x, out, consts, consts_at, packs, places):
    ctx = ExitStack()
    with ctx:
        pr = Program(nc, ctx)

        def sbuf(name, columns):
            return ctx.enter_context(nc.sbuf_tensor(name, [P, columns], F32))

        X = sbuf("x_rows", BATCH * TILES * DIM)[:, :].rearrange("p (t d) -> p t d", d=DIM)
        C = sbuf("constants", consts.shape[1])
        sides = [sbuf(f"weights_{n}", max(a.shape[1] for a in packs[n::2])) for n in range(2)]
        work = sbuf("work", WORK_COLUMNS)
        rows = lambda a: a.rearrange("(t p) d -> p t d", p=P)

        s = Section(pr, "load")
        s.dma(0, X, rows(x))
        s.dma(1, C[:, :], consts)
        s.emit()
        pr.prefetch(sides[0][:, 0:packs[0].shape[1]], packs[0])
        kit = Kit(pr, Weights(C, consts_at), X)
        s = Section(pr, "first")
        column = kit.c("scratch")
        written = s.dve(nc.vector.memset, column, 0.0)
        written = s.pool(nc.gpsimd.memset, column, 0.0, after=[written])
        s.act(nc.scalar.copy, column, kit.c("ones", cols=(0, 1)), after=[written])
        s.mm(pr.banks[0][:, 0:1], kit.ident, kit.c("ones", cols=(0, 1)))
        s.emit()
        for n, (_, _, stage) in enumerate(STAGES):
            pr.weights_landed()
            if n + 1 < len(STAGES):
                pr.prefetch(sides[(n + 1) % 2][:, 0:packs[n + 1].shape[1]], packs[n + 1])
            stage(kit, Weights(sides[n % 2], places[n]), Arena(work, WORK_COLUMNS))
        s = Section(pr, "store")
        s.dma(0, rows(out), X)
        s.emit()
        for p in pr.producers:
            nc.sync.wait_ge(pr.sem[p], pr.base[p] * pr.unit[p])


def kernel(**inputs):
    import concourse.bacc as bacc
    from concourse.bass_utils import run_bass_kernel_spmd

    packs, places = [], []
    for prefix, layout, _ in STAGES:
        own = {k[len(prefix):]: np.asarray(v) for k, v in inputs.items() if k.startswith(prefix)}
        a, at = pack(layout(own))
        packs.append(a)
        places.append(at)
    consts, consts_at = pack(constants())
    arrays = {"x": np.ascontiguousarray(np.asarray(inputs["L0_attn_hidden_states"]).reshape(BATCH * SEQ, DIM)),
              "constants_dram": consts}
    arrays.update({f"weights_dram_{n}": a for n, a in enumerate(packs)})
    nc = bacc.Bacc("TRN2", target_bir_lowering=False, num_devices=1)
    dram = {k: nc.dram_tensor(k, list(a.shape), F32, kind="ExternalInput").ap() for k, a in arrays.items()}
    out = nc.dram_tensor("out", [BATCH * SEQ, DIM], F32, kind="ExternalOutput").ap()
    build(nc, dram["x"], out, dram["constants_dram"], consts_at, [dram[f"weights_dram_{n}"] for n in range(len(packs))],
          places)
    got = run_bass_kernel_spmd(nc, [arrays], core_ids=[0])
    return got.results[0]["out"].reshape(BATCH, SEQ, DIM)
```

```python
from contextlib import ExitStack



import numpy as np
import concourse.bass as bass
from concourse import mybir

F32 = mybir.dt.float32
ALU = mybir.AluOpType
ACT = mybir.ActivationFunctionType
AX = mybir.AxisListType.X
ds = bass.ds

P = 128
BATCH, SEQ, DIM = 8, 512, 128
TILES = SEQ // P
BANK = 512
LANES = 2
LANE_BANKS = 4
LN_EPS = 1e-5


class At:

    def __init__(self, view):
        self.view = view


class Token:

    def __init__(self, producer):
        self.producer, self.k = producer, 0


class Program:

    CHANNELS = 3

    def __init__(self, nc, ctx):
        self.nc = nc
        self.handle = {"PE": nc.tensor, "DVE": nc.vector, "ACT": nc.scalar, "POOL": nc.gpsimd, "SP": nc.sync}
        self.producers = ["PE", "DVE", "ACT", "POOL"] + [f"DMA{c}" for c in range(self.CHANNELS)]
        self.sem = {p: ctx.enter_context(nc.semaphore(f"done_{p}")) for p in self.producers}
        self.unit = {p: 16 if p.startswith("DMA") else 1 for p in self.producers}
        self.base = {p: 0 for p in self.producers}
        self.weights_sem = [ctx.enter_context(nc.semaphore(f"weights_landed_{side}")) for side in range(2)]
        self.loads = 0
        self.banks = [ctx.enter_context(nc.psum_tensor(f"bank{b}", [P, BANK], F32)) for b in range(8)]


    def prefetch(self, dst, src):
        for p in self.producers:
            self.nc.sync.wait_ge(self.sem[p], self.base[p] * self.unit[p])
        self.nc.sync.dma_start(dst, src).then_inc(self.weights_sem[self.loads % 2], 16)
        self.loads += 1

    def weights_landed(self):
        for engine in ("PE", "DVE", "ACT", "POOL"):
            self.handle[engine].wait_ge(self.weights_sem[(self.loads - 1) % 2], 16 * ((self.loads + 1) // 2))


class Section:

    def __init__(self, program, name, lanes=0):
        self.pr, self.name = program, name
        self.items = [[] for _ in range(lanes + 1)]
        self.last = [{} for _ in range(lanes + 1)]
        self.lane = 0

    def use(self, lane):
        self.lane = lane + 1

    def latest(self, producer):
        return self.last[self.lane].get(producer)

    def _put(self, issuer, producer, fn, args, kw, after, link, signal):
        waits = [t for t in after if t is not None]
        if link and self.latest(producer):
            waits.append(self.latest(producer))
        token = Token(producer) if signal else None
        if signal:
            self.last[self.lane][producer] = token
        self.items[self.lane].append((issuer, waits, fn, args, kw, token))
        return token

    def dve(self, fn, *args, after=(), link=True, **kw):
        return self._put("DVE", "DVE", fn, args, kw, after, link, True)

    def act(self, fn, *args, after=(), link=False, **kw):
        return self._put("ACT", "ACT", fn, args, kw, after, link, True)

    def pool(self, fn, *args, after=(), link=True, **kw):
        return self._put("POOL", "POOL", fn, args, kw, after, link, True)

    def mm(self, out, lhsT, rhs, start=True, stop=True, after=(), signal=True):
        return self._put("PE", "PE", self.pr.nc.tensor.matmul, (out, lhsT, rhs), dict(start=start, stop=stop),
                         after, False, signal)

    def tr(self, out, in_, ident, after=(), signal=True):
        return self._put("PE", "PE", self.pr.nc.tensor.transpose, (out, in_, ident), {}, after, False, signal)

    def dma(self, channel, out, in_, after=()):
        return self._put("SP", f"DMA{channel}", self.pr.nc.sync.dma_start, (out, in_), {}, after, False, True)

    def emit(self, outer=1, inner=1):
        pr, nc = self.pr, self.pr.nc
        engine_types = {"PE": mybir.EngineType.PE, "DVE": mybir.EngineType.DVE, "ACT": mybir.EngineType.Activation,
                        "POOL": mybir.EngineType.Pool, "SP": mybir.EngineType.SP}

        order = [(n if lane else -1, lane, n, item) for lane, items in enumerate(self.items)
                 for n, item in enumerate(items)]
        order.sort(key=lambda x: x[:3])
        queue = {e: [] for e in pr.handle}
        count = {p: 0 for p in pr.producers}
        for *_, (issuer, waits, fn, args, kw, token) in order:
            if token:
                count[token.producer] += 1
                token.k = count[token.producer]
            assert all(w.k for w in waits), "waits for an instruction behind it"
            queue[issuer].append((waits, fn, args, kw, token))

        def run(o, i):
            turn = o * inner + i

            def value(producer, k):
                n = count[producer]
                v = pr.base[producer] + k
                return (v + turn * n) * pr.unit[producer] if n else v * pr.unit[producer]

            for issuer, items in queue.items():
                if not items:
                    continue
                handle = pr.handle[issuer]
                for p in pr.producers:
                    if pr.base[p] or count[p]:
                        handle.wait_ge(pr.sem[p], value(p, 0))
                waited = {}
                for waits, fn, args, kw, token in items:
                    for t in waits:
                        if waited.get(t.producer, 0) < t.k:
                            handle.wait_ge(pr.sem[t.producer], value(t.producer, t.k))
                            waited[t.producer] = t.k
                    put = [a.view(o, i) if isinstance(a, At) else a for a in args]
                    ins = fn(*put, **kw)
                    if token:
                        ins.then_inc(pr.sem[token.producer], pr.unit[token.producer])

        engines = tuple(engine_types[e] for e in queue if queue[e])
        if outer == 1 and inner == 1:
            run(0, 0)
        elif outer == 1:
            with nc.Fori(0, inner, engines=engines) as i:
                run(0, i)
        else:
            with nc.Fori(0, outer, engines=engines) as o:
                with nc.Fori(0, inner, engines=engines) as i:
                    run(o, i)
        for p in pr.producers:
            pr.base[p] += count[p] * outer * inner


class Ring:

    def __init__(self, items):
        self.items, self.free, self.idle = items, [()] * len(items), list(range(len(items)))

    def take(self):
        assert self.idle, "every buffer is in use"
        k = self.idle.pop(0)
        return self.items[k], self.free[k], k

    def give(self, k, *readers):
        assert k not in self.idle
        self.free[k] = readers
        self.idle.append(k)


class Arena:

    def __init__(self, pieces):
        self.pieces = [list(p) for p in pieces]

    def take(self, *shape):
        n = int(np.prod(shape))
        for piece in self.pieces:
            tensor, at, columns = piece
            if n <= columns:
                piece[1], piece[2] = at + n, columns - n
                break
        else:
            raise AssertionError(f"no room for {n} columns in {[p[2] for p in self.pieces]}")
        v = tensor[:, at:at + n]
        if len(shape) > 1:
            names = "abcd"[:len(shape)]
            v = v.rearrange(f"p ({' '.join(names)}) -> p {' '.join(names)}", **{x: s for x, s in zip(names, shape)})
        return v


def pack(parts):
    where, cols, at = {}, [], 0
    for name, a in parts:
        a = np.asarray(a, np.float32)
        full = np.zeros((P, a.shape[1]), np.float32)
        full[:a.shape[0]] = a
        cols.append(full)
        where[name] = (at, a.shape[0], a.shape[1])
        at += a.shape[1]
    return np.ascontiguousarray(np.concatenate(cols, axis=1)), where


class Weights:

    def __init__(self, tensor, where, at=0):
        self.tensor, self.where, self.at = tensor, where, at

    def __call__(self, name, rows=None, cols=None):
        at, r, c = self.where[name]
        lo, hi = cols or (0, c)
        rlo, rhi = rows or (0, r)
        return self.tensor[rlo:rhi, self.at + at + lo:self.at + at + hi]





def constants():
    i = np.arange(P)
    parts = [("ident", np.eye(P)), ("neghalf", np.full((P, 64), -0.5)), ("ones", np.ones((P, P))),
             ("scratch", np.zeros((P, 1 + LANES))), ("tri_incl", (i[:, None] <= i[None, :]) * 1.0),
             ("tri_strict", (i[:, None] < i[None, :]) * 1.0), ("after", (i[:, None] > i[None, :]) * 1.0)]
    parts += [("causal", np.where(i[None, :] <= i[:, None], 0.0, -1e30)), ("heads16", np.kron(np.eye(4), np.ones((16, 16))))]
    for n in range(7):
        b = i >> n
        m = ((b[:, None] >> 1) == (b[None, :] >> 1)) & (b[:, None] % 2 == 1) & (b[None, :] % 2 == 0)
        parts += [(f"level{n}", m.T if n == 0 else m)]
    parts += [("blocks32", np.kron(np.eye(4), np.ones((32, 32)))), ("blocks64", np.kron(np.eye(4), np.ones((32, 64))))]
    c = np.arange(192)
    band = np.where((c[None, :] >= i[:, None]) & (c[None, :] <= i[:, None] + 64), 0.0, -1e30)
    parts += [("band", band)] + rotary_tables()
    parts += [("lag", np.maximum(i[None, :] - 1 - i[:, None], 0)), ("place", np.broadcast_to(i[None, :], (P, P))),
              ("left", (P - 1 - i)[:, None])]
    return parts


def rotary_tables():
    hd, window, n = 64, 64, SEQ
    half = np.arange(0, hd, 2, dtype=np.float32)
    inv_freq = (1.0 / np.float32(10000.0) ** (half / np.float32(hd))).astype(np.float32)
    t = np.arange(n, dtype=np.float32)
    freqs = (t[:, None] * inv_freq[None, :]).astype(np.float32).astype(np.float64)
    base = (half + 0.4 * hd) / (1.4 * hd)
    scale = base[None, :].astype(np.float64) ** ((t - n // 2) / float(window // 2))[:, None]
    out = []
    for side, m in (("q", scale), ("k", 1.0 / scale)):
        cos, sin = np.cos(freqs) * m, np.sin(freqs) * m
        for name, a in (("cos", np.concatenate([cos, cos], axis=1)), ("sin", np.concatenate([-sin, sin], axis=1))):
            out.append((f"{name}_{side}", a.reshape(TILES, P, hd).transpose(1, 0, 2).reshape(P, TILES * hd)))
    return out





class Kit:

    def __init__(self, pr, consts, X):
        self.pr, self.nc, self.c, self.X = pr, pr.nc, consts, X
        self.ident = consts("ident")

    def rows_of(self, A, lane):
        return At(lambda o, i: A[:, ds(i * (LANES * TILES) + lane * TILES, TILES), :])

    def banks(self, lane):
        return self.pr.banks[lane * LANE_BANKS:(lane + 1) * LANE_BANKS]


def over(view, n):
    m = view.shape[1]
    return view.unsqueeze(2).broadcast_to([view.shape[0], m, n])


def settle(kit, s):
    s.dve(kit.nc.vector.memset, kit.c("scratch", cols=(s.lane, s.lane + 1)), 0.0)


def norm_rows(kit, s, src, dst, mv, stats, rstd, eps, after=()):
    nc, tiles = kit.nc, src.shape[1]
    for t in range(tiles):
        s.dve(nc.vector.bn_stats, stats[:, t, :], src[:, t, :], after=after if t == 0 else (), link=(t == 0))
    settle(kit, s)
    for t in range(tiles):
        moments = s.dve(nc.vector.bn_aggr, mv[:, t, :], stats[:, t, :], link=False)
    shifted = s.dve(nc.vector.tensor_scalar, rstd, mv[:, :, 1], eps, None, ALU.add)
    root = s.pool(nc.gpsimd.tensor_tensor, rstd, rstd, kit.c("neghalf", cols=(0, tiles)), ALU.pow, after=[shifted])
    for t in range(tiles):
        done = s.dve(nc.vector.tensor_scalar, dst[:, t, :], src[:, t, :], mv[:, t, 0:1], rstd[:, t:t + 1],
                     ALU.subtract, ALU.mult, after=[root, moments] if t == 0 else (), link=False)
    return done


def to_features(kit, s, ring, blocks, dst, after, scale=None, bias=None, engine="ACT", width=P, rows=P):
    nc = kit.nc
    bank, free, k = ring.take()
    n = len(blocks)
    if rows < P:
        hold(kit, s, bank, [*after, *free])
        after = free = ()
    for t, block in enumerate(blocks):
        turned = s.tr(bank[0:rows, t * P:(t + 1) * P], block, kit.ident,
                      after=[*after, *free] if t == 0 else (), signal=(t == n - 1))
    src = bank[0:rows, 0:n * P]
    if engine == "ACT":
        if scale is None and bias is None:
            done = s.act(nc.scalar.copy, dst, src, after=[turned])
        else:
            done = s.act(nc.scalar.activation, dst, src, ACT.Identity, bias=bias if bias is not None else 0.0,
                         scale=scale if scale is not None else 1.0, after=[turned])
    else:
        done = s.dve(nc.vector.tensor_copy, dst, src, after=[turned], link=False)
    ring.give(k, done)
    return done


def log1p(kit, s, e, u, rest, out, after=()):
    nc = kit.nc
    one_more = s.dve(nc.vector.tensor_scalar, u, e, 1.0, None, ALU.add, after=after)
    s.dve(nc.vector.tensor_scalar, rest, u, -1.0, None, ALU.add)
    s.dve(nc.vector.tensor_tensor, rest, e, rest, ALU.subtract)
    log = s.act(nc.scalar.activation, out, u, ACT.Ln, after=[one_more])
    return s.dve(nc.vector.tensor_tensor, out, out, rest, ALU.add, after=[log])


def hold(kit, s, bank, after):
    s.mm(bank[:, 0:1], kit.ident, kit.c("ident", cols=(0, 1)), after=after, signal=False)




EXPERTS = 8


def prefix_exclusive(kit, s, eq, pre, n):
    nc = kit.nc
    a, b = pre
    s.dve(nc.vector.memset, a[:, :, 0:1], 0.0)
    s.dve(nc.vector.tensor_copy, a[:, :, 1:n], eq[:, :, 0:n - 1], link=False)
    step = 1
    while step < n:
        s.dve(nc.vector.tensor_copy, b[:, :, 0:step], a[:, :, 0:step])
        s.dve(nc.vector.tensor_tensor, b[:, :, step:n], a[:, :, step:n], a[:, :, 0:n - step], ALU.add, link=False)
        a, b = b, a
        step *= 2
    return a


def weighted_experts(kit, s, hidden_all, weight_of, acc, fc2, ff_tiles, hid, y_rings, started):
    nc = kit.nc

    def down(e, hT, k, last):
        bank, yfree, yk = y_rings.take()
        for t in range(TILES):
            for f in range(ff_tiles):
                y = s.mm(bank[:, t * P:(t + 1) * P], hT[:, f, t * P:(t + 1) * P], fc2(e, f),
                         start=(f == 0), stop=(f == ff_tiles - 1), after=[last, *yfree] if t == 0 and f == 0 else (),
                         signal=(t == TILES - 1 and f == ff_tiles - 1))
        hid.give(k, y)
        return bank, yk, y

    def add(e, bank, yk, y):
        for t in range(TILES):
            part, first = bank[:, t * P:(t + 1) * P], t == 0
            if e == 0:
                done = s.dve(nc.vector.tensor_scalar, acc[:, t, :], part, weight_of(e, t), None, ALU.mult,
                             after=[y] if first else (), link=first)
            else:
                done = s.dve(nc.vector.scalar_tensor_tensor, acc[:, t, :], part, weight_of(e, t), acc[:, t, :],
                             ALU.mult, ALU.add, after=[y] if first else (), link=first)
        y_rings.give(yk, done)
        return done

    previous, pending, done = None, None, None
    for e in range(EXPERTS):
        current = (e, *hidden_all(e, started if e == 0 else ()))
        if previous:
            pending = (previous[0], *down(*previous))
            done = add(*pending)
        previous = current
    return add(previous[0], *down(*previous))




HEADS, DK = 4, 32
LEVELS = 7


class Delta:

    def __init__(self, kit, arena, dv, out_scaled):
        self.kit, self.dv = kit, dv
        self.NT, self.AT, self.X, self.XT, self.T1 = (arena.take(2, HEADS, P) for _ in range(5))
        self.WT = Ring([arena.take(P) for _ in range(2)])
        self.U = Ring([arena.take(HEADS, dv) for _ in range(2)])
        self.S = arena.take(HEADS * dv)
        self.gain = arena.take(HEADS * dv)
        self.own = kit.c(f"blocks{dv}")
        self.qS = arena.take(HEADS, dv) if out_scaled else None

    def start(self, s):
        return s.dve(self.kit.nc.vector.memset, self.S, 0.0, link=False)

    def invert(self, s, ring, chunks, kT, kbq, gt, after, gt_masked=None, filler=None):
        kit, nc = self.kit, self.kit.nc
        banks = []
        for hh in range(HEADS):
            bank, free, k = ring.take()
            part = slice(DK * hh, DK * hh + DK)
            for j, c in enumerate(chunks):
                made = s.mm(bank[:, j * 2 * P:(j + 1) * 2 * P], kT(c)[part, :], kbq(c)[part, :],
                            after=[*after, *free] if j == 0 else (), signal=j == 1)
            banks.append((bank, k, made))
        for hh, (bank, k, made) in enumerate(banks):
            both = bank[:, :].rearrange("p (c a n) -> p c a n", c=2, a=2)
            if gt is None:
                a = s.act(nc.scalar.copy, self.NT[:, :, hh, :], both[:, :, 0, :], after=[made])
                b = s.dve(nc.vector.tensor_tensor, self.AT[:, :, hh, :], both[:, :, 1, :],
                          kit.c("tri_incl").unsqueeze(1).broadcast_to([P, 2, P]), ALU.mult, after=[made, a],
                          link=False)
            else:
                a = s.dve(nc.vector.tensor_tensor, self.NT[:, :, hh, :], both[:, :, 0, :], gt[:, :, hh, :], ALU.mult,
                          after=[made], link=False)
                b = s.dve(nc.vector.tensor_tensor, self.AT[:, :, hh, :], both[:, :, 1, :], gt_masked[:, :, hh, :],
                          ALU.mult, link=False)
            ring.give(k, b)
        flat = lambda m, j: m[:, j].rearrange("p h n -> p (h n)")
        bc = lambda name: kit.c(name).unsqueeze(1).broadcast_to([P, HEADS, P])
        xt = [None, None]
        for j in range(2):
            s.dve(nc.vector.tensor_tensor, self.T1[:, j], self.NT[:, j], bc("level0"), ALU.mult, after=[a])
            xt[j] = s.dve(nc.vector.tensor_tensor, self.XT[:, j], bc("ident"), self.T1[:, j], ALU.subtract)
        for n in range(1, LEVELS):
            x = [None, None]
            for j in range(2):
                bank, free, k = ring.take()
                for hh in range(HEADS):
                    made = s.tr(bank[:, hh * P:(hh + 1) * P], self.XT[:, j, hh, :], kit.ident,
                                after=[xt[j], *free] if hh == 0 else (), signal=hh == HEADS - 1)
                x[j] = s.act(nc.scalar.copy, flat(self.X, j), bank[:, :], after=[made])
                ring.give(k, x[j])
            t1 = [None, None]
            for j in range(2):
                bank, free, k = ring.take()
                for hh in range(HEADS):
                    made = s.mm(bank[:, hh * P:(hh + 1) * P], self.NT[:, j, hh, :], self.X[:, j, hh, :],
                                after=[x[j], a, *free] if hh == 0 else (), signal=hh == HEADS - 1)
                t1[j] = s.dve(nc.vector.tensor_tensor, self.T1[:, j],
                              bank[:, :].rearrange("p (h n) -> p h n", h=HEADS), bc(f"level{n}"), ALU.mult,
                              after=[made], link=False)
                ring.give(k, t1[j])
            for j in range(2):
                bank, free, k = ring.take()
                for hh in range(HEADS):
                    made = s.mm(bank[:, hh * P:(hh + 1) * P], self.T1[:, j, hh, :], self.XT[:, j, hh, :],
                                after=[t1[j], *free] if hh == 0 else (), signal=hh == HEADS - 1)
                xt[j] = s.dve(nc.vector.tensor_tensor, flat(self.XT, j), flat(self.XT, j), bank[:, :], ALU.subtract,
                              after=[made], link=False)
                ring.give(k, xt[j])
            if filler:
                filler()
        return xt, [a, b]

    def advance(self, s, ring, j, state, ready, qT, vb, kbe, kd, out, out_scale=None, chunk_decay=None):
        kit, nc, dv = self.kit, self.kit.nc, self.dv
        wt, wfree, wk = self.WT.take()
        bank, free, k = ring.take()
        for hh in range(HEADS):
            made = s.mm(bank[DK * hh:DK * hh + DK, 0:P], kbe[:, hh, :], self.XT[:, j, hh, :],
                        after=[*ready, *free] if hh == 0 else (), signal=hh == HEADS - 1)
        turned = s.act(nc.scalar.mul, wt, bank[:, 0:P], -1.0, after=[made, *wfree])
        ring.give(k, turned)
        u, ufree, uk = self.U.take()
        flat_u = u.rearrange("p h d -> p (h d)")
        width = HEADS * dv
        bank, free, k = ring.take()
        s.mm(bank[:, 0:width], wt, self.S, stop=False, after=[turned, state, *free], signal=False)
        for hh in range(HEADS):
            made = s.mm(bank[:, hh * dv:(hh + 1) * dv], self.XT[:, j, hh, :], vb[:, hh, :], start=False, stop=hh == HEADS - 1,
                        signal=hh == HEADS - 1)
        self.WT.give(wk, made)
        values = s.act(nc.scalar.copy, flat_u, bank[:, 0:width], after=[made, *ufree])
        ring.give(k, values)
        bank, free, k = ring.take()
        by_head = lambda v: v[:, 0:width].rearrange("p (h d) -> p h d", d=dv)
        if out_scale is None:
            s.mm(bank[:, 0:width], qT, self.S, stop=False, after=free, signal=False)
            for hh in range(HEADS):
                made = s.mm(bank[:, hh * dv:(hh + 1) * dv], self.AT[:, j, hh, :], u[:, hh, :], start=False, stop=hh == HEADS - 1,
                            after=[values] if hh == 0 else (), signal=hh == HEADS - 1)
            got = s.act(nc.scalar.copy, out, by_head(bank), after=[made])
        else:
            bank2, free2, k2 = ring.take()
            carried = s.mm(bank2[:, 0:width], qT, self.S, after=[*free, *free2])
            scaled = s.dve(nc.vector.tensor_tensor, self.qS, by_head(bank2), over(out_scale, dv), ALU.mult,
                           after=[carried])
            ring.give(k2, scaled)
            for hh in range(HEADS):
                made = s.mm(bank[:, hh * dv:(hh + 1) * dv], self.AT[:, j, hh, :], u[:, hh, :],
                            after=[values] if hh == 0 else (), signal=hh == HEADS - 1)
            got = s.dve(nc.vector.tensor_tensor, out, self.qS, by_head(bank), ALU.add, after=[made])
        ring.give(k, got)
        bank, free, k = ring.take()
        added = s.mm(bank[:, 0:width], kd, flat_u, after=free)
        self.U.give(uk, added)
        gained = s.dve(nc.vector.tensor_tensor, self.gain, bank[:, 0:width], self.own, ALU.mult, after=[added])
        ring.give(k, gained)
        if chunk_decay is None:
            state = s.dve(nc.vector.tensor_tensor, self.S, self.S, self.gain, ALU.add)
        else:
            state = s.dve(nc.vector.scalar_tensor_tensor, self.S, self.S, chunk_decay, self.gain, ALU.mult, ALU.add)
        return state, got




L0_ATTN_SHORT, L0_ATTN_LONG, L0_ATTN_CONV = 5, 64, 4
L0_ATTN_PAD = L0_ATTN_LONG - 1
L0_ATTN_STATS = 16
L0_ATTN_GROUPS = TILES * HEADS


def layout_l0_attn(w):
    bc = lambda v: np.broadcast_to(np.reshape(v, (1, -1)), (P, np.size(v)))
    stat_w = np.zeros((HEADS, 32, P), np.float32)
    stat_w[:, :L0_ATTN_STATS, :] = w["fuse_w1"][:, DIM:].T[None]
    return [("q", w["q_proj_w"].T), ("k", w["k_proj_w"].T), ("v", w["v_proj_w"].T), ("beta", w["b_proj_w"].T),
            ("q_conv", w["q_conv_w"]), ("k_conv", w["k_conv_w"]), ("v_conv", w["v_conv_w"]),
            ("short", w["fir_short_w"].reshape(P, L0_ATTN_SHORT)), ("long", w["fir_long_w"].reshape(P, L0_ATTN_LONG)),
            ("fuse_hidden", w["fuse_w1"][:, :DIM].T), ("fuse_stats", stat_w.reshape(P, P)),
            ("fuse_b1", w["fuse_b1"][:, None]), ("fuse_w2", w["fuse_w2"].T), ("fuse_b2", bc(w["fuse_b2"])),
            ("temp", bc(w["logit_temp"])), ("res", bc(np.concatenate([w["res_scale_short"], w["res_scale_long"]]))),
            ("o_norm", np.tile(w["o_norm_w"], HEADS)[:, None]), ("o", w["o_proj_w"].T)]


def depthwise(kit, s, dst, src, taps, first, n, after=()):
    nc = kit.nc
    for j in range(n):
        view = src[:, first + j:first + j + SEQ]
        if j == 0:
            done = s.dve(nc.vector.tensor_scalar, dst, view, taps[:, 0:1], None, ALU.mult, after=after)
        else:
            done = s.dve(nc.vector.scalar_tensor_tensor, dst, view, taps[:, j:j + 1], dst, ALU.mult, ALU.add)
    return done


def stage_l0_attn(kit, w, arena):
    nc, X = kit.nc, kit.X
    padded = [([arena.take(L0_ATTN_CONV - 1 + SEQ) for _ in range(3)], arena.take(L0_ATTN_PAD + SEQ), arena.take(TILES, HEADS, 32))
              for _ in range(LANES)]
    u1, u2, u3, temp_inv = (arena.take(1) for _ in range(4))
    s = Section(kit.pr, "l0_start")
    for before, vT, stat_rows in padded:
        for b in before:
            s.dve(nc.vector.memset, b[:, 0:L0_ATTN_CONV - 1], 0.0, link=False)
        s.dve(nc.vector.memset, vT[:, 0:L0_ATTN_PAD], 0.0, link=False)
        s.dve(nc.vector.memset, stat_rows, 0.0, link=False)
    s.dve(nc.vector.tensor_scalar, u1, w("temp"), -1.0, None, ALU.mult)
    low = s.dve(nc.vector.tensor_tensor, u1, u1, w("temp"), ALU.min)
    ex = s.act(nc.scalar.activation, u1, u1, ACT.Exp, after=[low])
    log1p(kit, s, u1, u2, u3, temp_inv, after=[ex])
    s.dve(nc.vector.tensor_scalar, u1, w("temp"), 0.0, 1e-4, ALU.max, ALU.add)
    s.dve(nc.vector.tensor_tensor, temp_inv, temp_inv, u1, ALU.add)
    s.dve(nc.vector.reciprocal, temp_inv, temp_inv)
    s.emit()

    s = Section(kit.pr, "l0_attn", LANES)
    def batch(lane):
        s.use(lane)
        before, vT, stat_rows = padded[lane]
        xr, z, zT = arena.take(TILES, P), arena.take(TILES, P), arena.take(SEQ)
        stats, mv, rstd = arena.take(TILES, 6), arena.take(TILES, 2), arena.take(TILES)
        qrow, krow, vrow = (arena.take(TILES, P) for _ in range(3))
        vb, kb = arena.take(TILES, P), arena.take(TILES, P)
        kT, kbq = arena.take(TILES, P), arena.take(TILES, 2, P)
        beta, ss, rn = arena.take(TILES, HEADS), arena.take(2, L0_ATTN_GROUPS), arena.take(2, L0_ATTN_GROUPS)
        drow = arena.take(TILES, P)
        delta = Delta(kit, arena, DK, False)
        shortT, longT = arena.take(SEQ), arena.take(SEQ)
        logits, lmax = arena.take(L0_ATTN_GROUPS, 4), arena.take(L0_ATTN_GROUPS)
        ring = Ring(kit.banks(lane))
        heads = lambda v: v.rearrange("p t (h d) -> p (t h) d", d=DK)

        loaded = s.dve(nc.vector.tensor_copy, xr, kit.rows_of(X, lane))
        rows = norm_rows(kit, s, xr, z, mv, stats, rstd, LN_EPS, after=[loaded])
        feats = to_features(kit, s, ring, [z[:, t, :] for t in range(TILES)], zT, [rows])
        shaped = []
        for name, src, dst in (("v", before[2], vT[:, L0_ATTN_PAD:]), ("k", before[1], longT), ("q", before[0], shortT)):
            bank, free, k = ring.take()
            made = s.mm(bank[:, :], w(name), zT, after=[feats, *free])
            moved = s.act(nc.scalar.copy, src[:, L0_ATTN_CONV - 1:], bank[:, :], after=[made])
            ring.give(k, moved)
            conv = depthwise(kit, s, kT.rearrange("p t n -> p (t n)") if name == "k" else
                             drow.rearrange("p t n -> p (t n)") if name == "v" else
                             kb.rearrange("p t n -> p (t n)"), src, w(f"{name}_conv"), 0, L0_ATTN_CONV, after=[moved])
            source = {"k": kT, "v": drow, "q": kb}[name].rearrange("p t n -> p (t n)")
            shaped.append(s.act(nc.scalar.activation, dst, source, ACT.Silu, after=[conv]))
        values_T, keys_T, queries_T = shaped
        bank, free, k = ring.take()
        for t in range(TILES):
            made = s.mm(bank[:, t * HEADS:(t + 1) * HEADS], zT[:, t * P:(t + 1) * P], w("beta"),
                        after=free if t == 0 else (), signal=t == TILES - 1)
        betas = s.act(nc.scalar.activation, beta, bank[:, 0:L0_ATTN_GROUPS].rearrange("p (t h) -> p t h", h=HEADS), ACT.Sigmoid,
                      after=[made])
        ring.give(k, betas)
        blocks = lambda v, first=0: [v[:, first + t * P:first + (t + 1) * P] for t in range(TILES)]
        flat = lambda v: v.rearrange("p t n -> p (t n)")
        vals = to_features(kit, s, ring, blocks(vT, L0_ATTN_PAD), flat(vrow), [values_T])
        for n, (src, dst, made) in enumerate(((longT, krow, keys_T), (shortT, qrow, queries_T))):
            raw = to_features(kit, s, ring, blocks(src), flat(dst), [made])
            sq = s.act(nc.scalar.activation, flat(vb), flat(dst), ACT.Square, after=[raw, s.latest("DVE")],
                       link=True)
            total = s.dve(nc.vector.tensor_reduce, ss[:, n, :], heads(vb), AX, ALU.add, after=[sq])
            root = s.pool(nc.gpsimd.tensor_tensor, rn[:, n, :], ss[:, n, :], kit.c("neghalf", cols=(0, L0_ATTN_GROUPS)), ALU.pow,
                          after=[total])
            unit = s.dve(nc.vector.tensor_tensor, heads(dst), heads(dst), over(rn[:, n, :], DK), ALU.mult, after=[root])
        by_beta = over(beta.rearrange("p t h -> p (t h)"), DK)
        s.dve(nc.vector.tensor_tensor, heads(vb), heads(vrow), by_beta, ALU.mult, after=[vals, betas])
        ready = s.dve(nc.vector.tensor_tensor, heads(kb), heads(krow), by_beta, ALU.mult)
        tok = lambda v: [v[:, t, :] for t in range(TILES)]
        turned = [to_features(kit, s, ring, tok(krow), flat(kT), [ready])]
        for n, src in enumerate((kb, qrow)):
            bank, free, k = ring.take()
            for t in range(TILES):
                made = s.tr(bank[:, t * P:(t + 1) * P], src[:, t, :], kit.ident, after=[ready, *free] if t == 0 else (),
                            signal=t == TILES - 1)
            turned.append(s.act(nc.scalar.copy, kbq[:, :, n, :], bank[:, :].rearrange("p (t n) -> p t n", n=P),
                                after=[made]))
            ring.give(k, turned[-1])

        taps = [("short", shortT, L0_ATTN_SHORT, j) for j in range(L0_ATTN_SHORT)] + [("long", longT, L0_ATTN_LONG, j) for j in range(L0_ATTN_LONG)]
        filters = [None]

        def filler(count=6):
            for _ in range(count):
                if not taps:
                    return
                name, dst, n, j = taps.pop(0)
                view = vT[:, L0_ATTN_PAD - (n - 1) + j:L0_ATTN_PAD - (n - 1) + j + SEQ]
                if j == 0:
                    filters[0] = s.dve(nc.vector.tensor_scalar, dst, view, w(name, cols=(0, 1)), None, ALU.mult,
                                       after=[values_T, *turned])
                else:
                    filters[0] = s.dve(nc.vector.scalar_tensor_tensor, dst, view, w(name, cols=(j, j + 1)), dst,
                                       ALU.mult, ALU.add)

        state = delta.start(s)
        chunk_heads = lambda v, c: v[:, c, :].rearrange("p (h d) -> p h d", d=DK)
        for pair in range(2):
            chunks = (2 * pair, 2 * pair + 1)
            xt, scored = delta.invert(s, ring, chunks, lambda c: kT[:, c, :], lambda c: kbq[:, c].rearrange("p a n -> p (a n)"),
                                      None, turned, filler=filler)
            for j, c in enumerate(chunks):
                state, got = delta.advance(s, ring, j, state, [*xt, *scored], kbq[:, c, 1, :], chunk_heads(vb, c),
                                           chunk_heads(kb, c), krow[:, c, :], chunk_heads(drow, c))
        while taps:
            filler()
        srow, lrow = qrow, krow
        outs = [to_features(kit, s, ring, blocks(shortT), flat(srow), [filters[0], got, state]),
                to_features(kit, s, ring, blocks(longT), flat(lrow), [filters[0], got, state])]
        tmp, m1, m2, m3 = vb, ss[:, 0, :], ss[:, 1, :], rn[:, 0, :]
        st4 = stat_rows.rearrange("p t h c -> p (t h) c")
        for n, src in enumerate((srow, lrow, drow, vrow)):
            col = lambda c: st4[:, :, 4 * n + c]
            s.dve(nc.vector.tensor_reduce, m1, heads(src), AX, ALU.add, after=[*outs, got])
            sq = s.act(nc.scalar.activation, flat(tmp), flat(src), ACT.Square, after=[*outs, s.latest("DVE")])
            s.dve(nc.vector.tensor_scalar, col(0), m1, 1.0 / DK, None, ALU.mult)
            s.dve(nc.vector.tensor_reduce, m3, heads(src), AX, ALU.add, apply_absolute_value=True)
            s.dve(nc.vector.tensor_scalar, col(2), m3, 1.0 / DK, None, ALU.mult)
            s.dve(nc.vector.tensor_reduce, m2, heads(tmp), AX, ALU.add, after=[sq])
            s.dve(nc.vector.tensor_tensor, m1, col(0), col(0), ALU.mult)
            s.dve(nc.vector.scalar_tensor_tensor, col(1), m2, 1.0 / DK, m1, ALU.mult, ALU.subtract)
            length = s.dve(nc.vector.tensor_copy, col(3), m2)
        lengths = s.act(nc.scalar.activation, stat_rows.rearrange("p t h (n c) -> p (t h) n c", c=4)[:, :, 0:4, 3],
                        stat_rows.rearrange("p t h (n c) -> p (t h) n c", c=4)[:, :, 0:4, 3], ACT.Sqrt, after=[length])
        statT = shortT
        stat_feats = to_features(kit, s, ring, [stat_rows[:, t].rearrange("p h c -> p (h c)") for t in range(TILES)],
                                 statT, [lengths])
        hidT = delta.X.rearrange("p a h n -> p (a h n)").rearrange("p (b n) -> p b n", n=SEQ)
        hids = Ring([hidT[:, 0, :], hidT[:, 1, :]])
        lbank, lfree, lk = ring.take()
        for hh in range(HEADS):
            bank, free, k = ring.take()
            s.mm(bank[:, :], w("fuse_hidden"), zT, stop=False, after=[stat_feats, got, *free], signal=False)
            part = (DK * hh, DK * hh + DK)
            made = s.mm(bank[:, :], w("fuse_stats", rows=part), statT[part[0]:part[1], :], start=False)
            dst, hfree, hk = hids.take()
            act = s.act(nc.scalar.activation, dst, bank[:, :], ACT.Gelu, bias=w("fuse_b1"), after=[made, *hfree])
            ring.give(k, act)
            for t in range(TILES):
                at = (t * HEADS + hh) * 4
                made = s.mm(lbank[:, at:at + 4], dst[:, t * P:(t + 1) * P], w("fuse_w2"),
                            after=[act, *lfree] if t == 0 else (), signal=t == TILES - 1)
            hids.give(hk, made)
        s.dve(nc.vector.tensor_tensor, logits, lbank[:, 0:L0_ATTN_GROUPS * 4].rearrange("p (g c) -> p g c", c=4),
              w("fuse_b2").unsqueeze(1).broadcast_to([P, L0_ATTN_GROUPS, 4]), ALU.add, after=[made])
        s.dve(nc.vector.tensor_reduce, lmax, logits, AX, ALU.max)
        centred = s.dve(nc.vector.tensor_tensor, logits, logits, over(lmax, 4), ALU.subtract)
        ring.give(lk, centred)
        exps = s.act(nc.scalar.activation, logits, logits, ACT.Exp, scale=temp_inv, after=[centred])
        s.dve(nc.vector.tensor_reduce, lmax, logits, AX, ALU.add, after=[exps])
        s.dve(nc.vector.reciprocal, lmax, lmax)
        s.dve(nc.vector.tensor_tensor, logits, logits, over(lmax, 4), ALU.mult)
        for n in range(2):
            s.dve(nc.vector.tensor_scalar, logits[:, :, n], logits[:, :, n], w("res", cols=(n, n + 1)), None, ALU.add)
        for n, src in enumerate((srow, lrow, drow, vrow)):
            s.dve(nc.vector.tensor_tensor, heads(src), heads(src), over(logits[:, :, n], DK), ALU.mult)
        s.dve(nc.vector.tensor_tensor, srow, srow, lrow, ALU.add)
        s.dve(nc.vector.tensor_tensor, drow, drow, vrow, ALU.add)
        mixed = s.dve(nc.vector.tensor_tensor, srow, srow, drow, ALU.add)
        sq = s.act(nc.scalar.activation, flat(tmp), flat(srow), ACT.Square, after=[mixed])
        s.dve(nc.vector.tensor_reduce, m1, heads(tmp), AX, ALU.add, after=[sq])
        shifted = s.dve(nc.vector.tensor_scalar, m1, m1, 1.0 / DK, 1e-5, ALU.mult, ALU.add)
        root = s.pool(nc.gpsimd.tensor_tensor, m2, m1, kit.c("neghalf", cols=(0, L0_ATTN_GROUPS)), ALU.pow, after=[shifted])
        normed = s.dve(nc.vector.tensor_tensor, heads(srow), heads(srow), over(m2, DK), ALU.mult, after=[root])
        oT = longT
        turned_o = to_features(kit, s, ring, tok(srow), oT, [normed], scale=w("o_norm"))
        bank, free, k = ring.take()
        for t in range(TILES):
            made = s.mm(bank[:, t * P:(t + 1) * P], oT[:, t * P:(t + 1) * P], w("o"),
                        after=[turned_o, *free] if t == 0 else (), signal=t == TILES - 1)
        s.dve(nc.vector.tensor_tensor, kit.rows_of(X, lane), xr,
              bank[:, :].rearrange("p (t d) -> p t d", d=P), ALU.add, after=[made])

    for lane in range(LANES):
        batch(lane)
    s.emit(1, BATCH // LANES)




L0_FFN_FF_TILES = 4


def layout_l0_ffn(w):
    parts = [("router", w["Wr"]), ("router_bias", np.broadcast_to(w["br"][None, :], (P, EXPERTS)))]
    for e in range(EXPERTS):
        parts.append((f"up{e}", w["W1"][e]))
        for f in range(4):
            parts.append((f"down{e}_{f}", w["W2"][e][f * P:(f + 1) * P]))
    return parts


def stage_l0_ffn(kit, w, arena):
    nc, X = kit.nc, kit.X
    s = Section(kit.pr, "l0_ffn", LANES)
    def batch(lane):
        s.use(lane)
        xr, h, xT = arena.take(TILES, P), arena.take(TILES, P), arena.take(SEQ)
        acc, hid0, hid1 = arena.take(TILES, P), arena.take(4, SEQ), arena.take(4, SEQ)
        stats, mv, rstd = arena.take(TILES, 6), arena.take(TILES, 2), arena.take(TILES)
        route, eq, pa, pb = (arena.take(TILES, EXPERTS) for _ in range(4))
        top, weight = arena.take(TILES), arena.take(TILES, EXPERTS)
        banks = kit.banks(lane)
        ring, yring, hid = Ring(banks[0:2]), Ring(banks[2:3]), Ring([hid0, hid1])

        loaded = s.dve(nc.vector.tensor_copy, xr, kit.rows_of(X, lane))
        rows = norm_rows(kit, s, xr, h, mv, stats, rstd, LN_EPS, after=[loaded])
        feats = to_features(kit, s, ring, [h[:, t, :] for t in range(TILES)], xT, [rows])
        for t in range(TILES):
            logits = s.mm(banks[3][:, t * EXPERTS:(t + 1) * EXPERTS], xT[:, t * P:(t + 1) * P], w("router"),
                          after=[feats] if t == 0 else (), signal=(t == TILES - 1))
        s.dve(nc.vector.tensor_tensor, route, banks[3][:, 0:TILES * EXPERTS].rearrange("p (t e) -> p t e", e=EXPERTS),
              w("router_bias").unsqueeze(1).broadcast_to([P, TILES, EXPERTS]), ALU.add, after=[logits])
        biased = s.latest("DVE")
        prob = s.act(nc.scalar.activation, route, route, ACT.Sigmoid, after=[biased])
        s.dve(nc.vector.tensor_reduce, top, route, AX, ALU.max, after=[prob])
        s.dve(nc.vector.tensor_tensor, eq, route, over(top, EXPERTS), ALU.is_equal)
        pre = prefix_exclusive(kit, s, eq, (pa, pb), EXPERTS)
        s.dve(nc.vector.tensor_scalar, pre, pre, 0.5, None, ALU.is_lt)
        s.dve(nc.vector.tensor_tensor, eq, eq, pre, ALU.mult)
        weights = s.dve(nc.vector.tensor_tensor, weight, eq, over(top, EXPERTS), ALU.mult)

        def hidden_all(e, started):
            hT, free, hk = hid.take()
            for f in range(L0_FFN_FF_TILES):
                bank, bfree, k = ring.take()
                up = s.mm(bank[:, :], w(f"up{e}", cols=(f * P, (f + 1) * P)), xT, after=[*bfree, *started])
                act = s.act(nc.scalar.activation, hT[:, f, :], bank[:, :], ACT.Gelu,
                            after=[up, *(free if f == 0 else ())])
                ring.give(k, act)
            return hT, hk, act

        done = weighted_experts(kit, s, hidden_all, lambda e, t: weight[:, t, e:e + 1], acc,
                                lambda e, f: w(f"down{e}_{f}"), L0_FFN_FF_TILES, hid, yring, [feats])
        s.dve(nc.vector.tensor_tensor, kit.rows_of(X, lane), xr, acc, ALU.add, after=[done])

    for lane in range(LANES):
        batch(lane)
    s.emit(1, BATCH // LANES)




L1_ATTN_LAYERS, L1_ATTN_HEADS, L1_ATTN_HD = 4, 8, 16
L1_ATTN_LOCAL = 4
L1_ATTN_HALF = L1_ATTN_LOCAL * L1_ATTN_HD
L1_ATTN_BUCKET = 64
L1_ATTN_BUCKETS = SEQ // L1_ATTN_BUCKET
L1_ATTN_FF = 4


def layout_l1_attn(w):
    parts = []
    for n in range(L1_ATTN_LAYERS):
        def padded(m):
            out = np.zeros((P, L1_ATTN_LOCAL, 32), np.float32)
            out[:, :, :L1_ATTN_HD] = m[:, :L1_ATTN_HALF].reshape(P, L1_ATTN_LOCAL, L1_ATTN_HD)
            return out.reshape(P, P)
        bc = lambda v: np.broadcast_to(v[None, :], (P, P))
        one = [("q", padded(w["Wq"][n])), ("k", padded(w["Wk"][n])),
               ("qkv", np.concatenate([w["Wq"][n][:, L1_ATTN_HALF:], w["Wk"][n][:, L1_ATTN_HALF:], w["Wv"][n]], axis=1)),
               ("o", w["Wo"][n]), ("up", w["W1"][n])]
        one += [(f"down{f}", w["W2"][n][f * P:(f + 1) * P]) for f in range(L1_ATTN_FF)]
        one += [("bo", bc(w["bo"][n])), ("b2", bc(w["b2"][n])), ("b1", w["b1"][n].reshape(L1_ATTN_FF, P).T)]
        one += [(c, w[c][n][:, None]) for c in ("ln1_g", "ln1_b", "ln2_g", "ln2_b")]
        parts += [(name if n == 0 else f"{name}@{n}", a) for name, a in one]
    return parts


def stage_l1_attn(kit, w, arena):
    nc, X = kit.nc, kit.X
    layer_cols = w.where["q@1"][0] - w.where["q"][0]
    Yall = arena.take(BATCH * TILES, P)
    static = arena.take(layer_cols)
    wl = Weights(static, w.where)

    s = Section(kit.pr, "l1_enter", LANES)
    small = [(arena.take(TILES, 2), arena.take(TILES, 6), arena.take(TILES)) for _ in range(LANES)]
    ys, hs = ([arena.take(TILES, P) for _ in range(LANES)] for _ in range(2))
    vs = [arena.take(TILES, P + 1) for _ in range(LANES)]

    def enter(lane):
        s.use(lane)
        y, h = ys[lane], hs[lane]
        loaded = s.dve(nc.vector.tensor_copy, h, kit.rows_of(X, lane))
        norm_rows(kit, s, h, y, *small[lane], LN_EPS, after=[loaded])
        s.dve(nc.vector.tensor_copy, kit.rows_of(Yall, lane), y)
        s.dve(nc.vector.memset, vs[lane][:, :, P:P + 1], 1.0, link=False)

    for lane in range(LANES):
        enter(lane)
    s.emit(1, BATCH // LANES)

    s = Section(kit.pr, "l1_layers", LANES)
    weights = s.pool(nc.gpsimd.tensor_copy, static, At(lambda o, i: w.tensor[:, ds(o * layer_cols + w.at, layer_cols)]))

    def batch(lane):
        s.use(lane)
        y, h, v = ys[lane], hs[lane], vs[lane]
        mv, stats, rstd = small[lane]
        hT, qT, kT, oT = arena.take(SEQ), arena.take(SEQ), arena.take(SEQ), arena.take(SEQ)
        qg, kg, kpos = arena.take(TILES, L1_ATTN_HALF), arena.take(TILES, L1_ATTN_HALF), arena.take(TILES, L1_ATTN_HALF)
        gmax = arena.take(TILES * L1_ATTN_LOCAL)
        ff = arena.take(L1_ATTN_FF, SEQ)
        probs = Ring([ff[:, 2 * n:2 * n + 2, :].rearrange("p a (h c) -> p (a h) c", c=2 * P) for n in range(2)])
        turned = Ring([arena.take(2 * L1_ATTN_LOCAL, P) for _ in range(2)])
        top, sums, inv = arena.take(TILES, L1_ATTN_LOCAL), arena.take(TILES, L1_ATTN_LOCAL), arena.take(TILES, L1_ATTN_LOCAL)
        orow = arena.take(TILES, L1_ATTN_HALF)
        qgT = arena.take(SEQ)
        cum = [arena.take(L1_ATTN_BUCKETS - 1, L1_ATTN_HALF + 1) for _ in range(2)]
        ctx_inv, ctx_n = arena.take(L1_ATTN_BUCKETS - 1), arena.take(L1_ATTN_BUCKETS - 1, L1_ATTN_HALF)
        ybo = arena.take(TILES, P)
        y2, yb2 = ybo, y
        ring = Ring(kit.banks(lane))

        loaded = s.dve(nc.vector.tensor_copy, y, kit.rows_of(Yall, lane))
        with_bo = s.pool(nc.gpsimd.tensor_tensor, ybo, y, wl("bo").unsqueeze(1).broadcast_to([P, TILES, P]), ALU.add,
                         after=[loaded, weights])
        rows = norm_rows(kit, s, y, h, mv, stats, rstd, LN_EPS, after=[loaded])
        feats = to_features(kit, s, ring, [h[:, t, :] for t in range(TILES)], hT, [rows, weights],
                            scale=wl("ln1_g"), bias=wl("ln1_b"))
        qk = []
        for name, dst in (("q", qT), ("k", kT)):
            bank, free, k = ring.take()
            made = s.mm(bank[:, :], wl(name), hT, after=[feats, *free])
            qk.append(s.act(nc.scalar.copy, dst, bank[:, :], after=[made]))
            ring.give(k, qk[-1])
        wide = 2 * L1_ATTN_HALF + P
        for pair in range(TILES // 2):
            bank, free, k = ring.take()
            for j in range(2):
                t = 2 * pair + j
                made = s.mm(bank[:, j * wide:(j + 1) * wide], hT[:, t * P:(t + 1) * P], wl("qkv"),
                            after=free if j == 0 else (), signal=j == 1)
            both = bank[:, :].rearrange("p (t d) -> p t d", t=2)
            at = slice(2 * pair, 2 * pair + 2)
            a = s.dve(nc.vector.tensor_copy, qg[:, at, :], both[:, :, 0:L1_ATTN_HALF], after=[made], link=False)
            b = s.dve(nc.vector.tensor_scalar, kg[:, at, :], both[:, :, L1_ATTN_HALF:2 * L1_ATTN_HALF], 0.0, None, ALU.min, link=False)
            c = s.dve(nc.vector.tensor_scalar, kpos[:, at, :], both[:, :, L1_ATTN_HALF:2 * L1_ATTN_HALF], 0.0, None, ALU.max, link=False)
            values = s.act(nc.scalar.copy, v[:, at, 0:P], both[:, :, 2 * L1_ATTN_HALF:wide], after=[c])
            ring.give(k, values)
        q16 = qg.rearrange("p t (h d) -> p (t h) d", d=L1_ATTN_HD)
        s.dve(nc.vector.tensor_reduce, gmax, q16, AX, ALU.max)
        centred = s.dve(nc.vector.tensor_tensor, q16, q16, over(gmax, L1_ATTN_HD), ALU.subtract)
        kexp = s.act(nc.scalar.activation, kg, kg, ACT.Exp, after=[centred])
        qexp = s.act(nc.scalar.activation, qg, qg, ACT.Exp)
        keys = s.dve(nc.vector.tensor_tensor, kg, kg, kpos, ALU.add, after=[kexp])
        s.dve(nc.vector.tensor_reduce, gmax, q16, AX, ALU.add, after=[qexp])
        s.dve(nc.vector.reciprocal, gmax, gmax)
        queries = s.dve(nc.vector.tensor_tensor, q16, q16, over(gmax, L1_ATTN_HD), ALU.mult)
        even, efree, ek = ring.take()
        odd, ofree, ok = ring.take()
        cw = L1_ATTN_HALF + 1
        hold(kit, s, even, [keys, values, *efree, *ofree])
        for u in range(L1_ATTN_BUCKETS - 1):
            t, lo = u // 2, (u % 2) * L1_ATTN_BUCKET
            into = odd if u % 2 else even
            made = s.mm(into[0:L1_ATTN_HALF, (u // 2) * cw:(u // 2 + 1) * cw], kg[lo:lo + L1_ATTN_BUCKET, t, :],
                        v[lo:lo + L1_ATTN_BUCKET, t, L1_ATTN_HALF:P + 1],
                        signal=u == L1_ATTN_BUCKETS - 2)
        n_even = L1_ATTN_BUCKETS // 2
        s.dve(nc.vector.tensor_copy, cum[0][0:L1_ATTN_HALF, 0:L1_ATTN_BUCKETS - 1:2, :],
              even[0:L1_ATTN_HALF, 0:n_even * cw].rearrange("p (u d) -> p u d", d=cw), after=[made])
        a0 = s.dve(nc.vector.tensor_copy, cum[0][0:L1_ATTN_HALF, 1:L1_ATTN_BUCKETS - 1:2, :],
                   odd[0:L1_ATTN_HALF, 0:(n_even - 1) * cw].rearrange("p (u d) -> p u d", d=cw), link=False)
        ring.give(ek, a0)
        ring.give(ok, a0)
        a, b, n = cum[0], cum[1], 1
        while n < L1_ATTN_BUCKETS - 1:
            s.dve(nc.vector.tensor_copy, b[0:L1_ATTN_HALF, 0:n, :], a[0:L1_ATTN_HALF, 0:n, :])
            s.dve(nc.vector.tensor_tensor, b[0:L1_ATTN_HALF, n:L1_ATTN_BUCKETS - 1, :], a[0:L1_ATTN_HALF, n:L1_ATTN_BUCKETS - 1, :],
                  a[0:L1_ATTN_HALF, 0:L1_ATTN_BUCKETS - 1 - n, :], ALU.add, link=False)
            a, b, n = b, a, 2 * n
        s.dve(nc.vector.tensor_scalar, ctx_inv[0:L1_ATTN_HALF, :], a[0:L1_ATTN_HALF, :, L1_ATTN_HALF], 1e-6, None, ALU.add)
        s.dve(nc.vector.reciprocal, ctx_inv[0:L1_ATTN_HALF, :], ctx_inv[0:L1_ATTN_HALF, :])
        s.dve(nc.vector.tensor_tensor, ctx_n[0:L1_ATTN_HALF, :, :], a[0:L1_ATTN_HALF, :, 0:L1_ATTN_HALF], over(ctx_inv[0:L1_ATTN_HALF, :], L1_ATTN_HALF), ALU.mult)
        contexts = s.dve(nc.vector.tensor_tensor, ctx_n[0:L1_ATTN_HALF, :, :], ctx_n[0:L1_ATTN_HALF, :, :],
                         kit.c("heads16").unsqueeze(1).broadcast_to([L1_ATTN_HALF, L1_ATTN_BUCKETS - 1, L1_ATTN_HALF]), ALU.mult)
        gqueries = to_features(kit, s, ring, [qg[:, t, :] for t in range(TILES)], qgT[0:L1_ATTN_HALF, :], [queries], rows=L1_ATTN_HALF)
        first = s.dve(nc.vector.memset, oT[L1_ATTN_HALF:P, 0:L1_ATTN_BUCKET], 0.0, link=False)
        bank, free, k = ring.take()
        hold(kit, s, bank, [contexts, gqueries, *free])
        for u in range(1, L1_ATTN_BUCKETS):
            made = s.mm(bank[L1_ATTN_HALF:P, u * L1_ATTN_BUCKET:(u + 1) * L1_ATTN_BUCKET], ctx_n[0:L1_ATTN_HALF, u - 1, :],
                        qgT[0:L1_ATTN_HALF, u * L1_ATTN_BUCKET:(u + 1) * L1_ATTN_BUCKET], signal=u == L1_ATTN_BUCKETS - 1)
        linear_out = s.act(nc.scalar.copy, oT[L1_ATTN_HALF:P, L1_ATTN_BUCKET:SEQ], bank[L1_ATTN_HALF:P, L1_ATTN_BUCKET:SEQ], after=[made, first])
        ring.give(k, linear_out)

        scale = L1_ATTN_HD ** -0.5

        def scores(t):
            got = [ring.take() for _ in range(2)]
            made = [None, None]
            for j in range(2):
                for side, (bank, free, _) in enumerate(got):
                    hh, at = 2 * side + j, 2 * P * j
                    part = slice(32 * hh, 32 * hh + 32)
                    lhs = qT[part, t * P:(t + 1) * P]
                    s.mm(bank[:, at + P:at + 2 * P], kit.ident, kit.c("causal"), stop=False,
                         after=[*qk, *free] if j == 0 else [made[side]], signal=False)
                    made[side] = s.mm(bank[:, at + P:at + 2 * P], lhs, kT[part, t * P:(t + 1) * P], start=False,
                                      signal=t == 0)
                    if t:
                        made[side] = s.mm(bank[:, at:at + P], lhs, kT[part, (t - 1) * P:t * P])
            lo = 0 if t else P
            for side, (bank, _, _) in enumerate(got):
                s.dve(nc.vector.tensor_reduce, top[:, t, 2 * side:2 * side + 2],
                      bank[:, :].rearrange("p (h c) -> p h c", h=2)[:, :, lo:], AX, ALU.max, after=[made[side]],
                      link=False)
            neg = s.dve(nc.vector.tensor_scalar, top[:, t, :], top[:, t, :], -scale, None, ALU.mult)
            return got, neg, lo

        def softmax(t, got, neg, lo):
            pr, pfree, pk = probs.take()
            for hh in range(L1_ATTN_LOCAL):
                bank, _, k = got[hh // 2]
                at = 2 * P * (hh % 2)
                done = s.act(nc.scalar.activation, pr[:, hh, lo:2 * P], bank[:, at + lo:at + 2 * P],
                             ACT.Exp, scale=scale, bias=top[:, t, hh:hh + 1], accum_out=sums[:, t, hh:hh + 1],
                             after=[neg, *(pfree if hh == 0 else ())])
                if hh % 2:
                    ring.give(k, done)
            return pr, pk, done

        def turn(t, pr, pk, done):
            sides = (0, 1) if t else (1,)
            dst, dfree, dk = turned.take()
            for side in sides:
                bank, free, k = ring.take()
                for hh in range(L1_ATTN_LOCAL):
                    made = s.tr(bank[:, hh * P:(hh + 1) * P], pr[:, hh, side * P:(side + 1) * P], kit.ident,
                                after=[done, *free] if hh == 0 else (), signal=hh == L1_ATTN_LOCAL - 1)
                to = dst[:, side * L1_ATTN_LOCAL:(side + 1) * L1_ATTN_LOCAL, :].rearrange("p h q -> p (h q)")
                if side:
                    last = moved = s.act(nc.scalar.copy, to, bank[:, :], after=[made, *dfree])
                else:
                    before = moved = s.dve(nc.vector.tensor_copy, to, bank[:, :], after=[made, *dfree], link=False)
                ring.give(k, moved)
            probs.give(pk, made)
            return dst, dk, [last, before] if t else [last]

        def values_of(t, dst, dk, ready):
            bank, free, k = ring.take()
            sides = (0, 1) if t else (1,)
            for hh in range(L1_ATTN_LOCAL):
                for side in sides:
                    made = s.mm(bank[:, hh * L1_ATTN_HD:(hh + 1) * L1_ATTN_HD], dst[:, side * L1_ATTN_LOCAL + hh, :],
                                v[:, t - 1 + side, hh * L1_ATTN_HD:(hh + 1) * L1_ATTN_HD], start=side == sides[0], stop=side == 1,
                                after=[*ready, *free, values] if hh == 0 and side == sides[0] else (),
                                signal=hh == L1_ATTN_LOCAL - 1 and side == 1)
            turned.give(dk, made)
            s.dve(nc.vector.reciprocal, inv[:, t, :], sums[:, t, :], after=[made])
            done = s.dve(nc.vector.tensor_tensor, orow[:, t, :].rearrange("p (h d) -> p h d", d=L1_ATTN_HD),
                         bank[:, 0:L1_ATTN_HALF].rearrange("p (h d) -> p h d", d=L1_ATTN_HD), over(inv[:, t, :], L1_ATTN_HD), ALU.mult)
            ring.give(k, done)
            return done

        ahead = scores(0)
        for t in range(TILES):
            weights_of = softmax(t, *ahead)
            if t + 1 < TILES:
                ahead = scores(t + 1)
            local = values_of(t, *turn(t, *weights_of))
        local_out = to_features(kit, s, ring, [orow[:, t, :] for t in range(TILES)], oT[0:L1_ATTN_HALF, :], [local], rows=L1_ATTN_HALF)
        bank, free, k = ring.take()
        for t in range(TILES):
            made = s.mm(bank[:, t * P:(t + 1) * P], oT[:, t * P:(t + 1) * P], wl("o"),
                        after=[local_out, linear_out, *free] if t == 0 else (), signal=t == TILES - 1)
        attended = s.dve(nc.vector.tensor_tensor, y2, ybo, bank[:, :].rearrange("p (t d) -> p t d", d=P), ALU.add,
                         after=[made, with_bo])
        ring.give(k, attended)
        with_b2 = s.pool(nc.gpsimd.tensor_tensor, yb2, y2, wl("b2").unsqueeze(1).broadcast_to([P, TILES, P]), ALU.add,
                         after=[attended])
        rows = norm_rows(kit, s, y2, h, mv, stats, rstd, LN_EPS, after=[attended])
        feats = to_features(kit, s, ring, [h[:, t, :] for t in range(TILES)], hT, [rows],
                            scale=wl("ln2_g"), bias=wl("ln2_b"))
        for f in range(L1_ATTN_FF):
            bank, free, k = ring.take()
            made = s.mm(bank[:, :], wl("up", cols=(f * P, (f + 1) * P)), hT, after=[feats, *free])
            act = s.act(nc.scalar.activation, ff[:, f, :], bank[:, :], ACT.Gelu, bias=wl("b1", cols=(f, f + 1)),
                        after=[made])
            ring.give(k, act)
        bank, free, k = ring.take()
        for t in range(TILES):
            for f in range(L1_ATTN_FF):
                made = s.mm(bank[:, t * P:(t + 1) * P], ff[:, f, t * P:(t + 1) * P], wl(f"down{f}"), start=f == 0,
                            stop=f == L1_ATTN_FF - 1, after=[act, *free] if t == 0 and f == 0 else (),
                            signal=t == TILES - 1 and f == L1_ATTN_FF - 1)
        s.dve(nc.vector.tensor_tensor, kit.rows_of(Yall, lane), yb2, bank[:, :].rearrange("p (t d) -> p t d", d=P), ALU.add,
              after=[made, with_b2])

    for lane in range(LANES):
        batch(lane)
    s.emit(L1_ATTN_LAYERS, BATCH // LANES)

    s = Section(kit.pr, "l1_leave")
    s.dve(nc.vector.tensor_tensor, X, X, Yall, ALU.add)
    s.emit()




L1_FFN_FF1 = 4
L1_FFN_ALL = BATCH * TILES
L1_FFN_PLACES = BATCH * SEQ // EXPERTS
L1_FFN_SCORE_BITS = 26


def layout_l1_ffn(w):
    parts = [("gate", w["gate_w"].T), ("gamma", w["ln_gamma"][:, None]), ("beta", w["ln_beta"][:, None]),
             ("b1", w["b1s"].reshape(EXPERTS * L1_FFN_FF1, P).T), ("b2", w["b2s"])]
    for e in range(EXPERTS):
        parts.append((f"up{e}", w["fc1s"][e].T))
        for f in range(L1_FFN_FF1):
            parts.append((f"down{e}_{f}", w["fc2s"][e][:, f * P:(f + 1) * P].T))
    return parts


def stage_l1_ffn(kit, w, arena):
    nc, X, E = kit.nc, kit.X, EXPERTS
    banks = kit.pr.banks
    scores = arena.take(L1_FFN_ALL, E)
    taken = arena.take(L1_FFN_ALL, E)
    own = [(arena.take(TILES, P), arena.take(TILES, P), arena.take(TILES, P), arena.take(SEQ), arena.take(TILES, 2),
            arena.take(TILES, 6), arena.take(TILES)) for _ in range(LANES)]

    s = Section(kit.pr, "l1_scores", LANES)
    def score(lane):
        s.use(lane)
        xr, z, y, zT, mv, stats, rstd = own[lane]
        ring, logit_bank = Ring(kit.banks(lane)[0:2]), kit.banks(lane)[3]
        loaded = s.dve(nc.vector.tensor_copy, xr, kit.rows_of(X, lane))
        rows = norm_rows(kit, s, xr, z, mv, stats, rstd, LN_EPS, after=[loaded])
        feats = to_features(kit, s, ring, [z[:, t, :] for t in range(TILES)], zT, [rows])
        for t in range(TILES):
            logits = s.mm(logit_bank[:, t * E:(t + 1) * E], zT[:, t * P:(t + 1) * P], w("gate"),
                          after=[feats] if t == 0 else (), signal=(t == TILES - 1))
        part = y[:, 0, 0:TILES * E].rearrange("p (t e) -> p t e", e=E)
        tanh = s.act(nc.scalar.activation, part, logit_bank[:, 0:TILES * E].rearrange("p (t e) -> p t e", e=E), ACT.Tanh,
                     after=[logits])
        s.dve(nc.vector.tensor_scalar, kit.rows_of(scores, lane), part, 1.0, 0.5,
              ALU.add, ALU.mult, after=[tanh])

    for lane in range(LANES):
        score(lane)
    s.emit(1, BATCH // LANES)

    s = Section(kit.pr, "l1_threshold_start")
    cand, thr, step, keep, part8 = (arena.take(E) for _ in range(5))
    flags = arena.take(L1_FFN_ALL, E)
    s.dve(nc.vector.memset, thr, 0.0)
    s.dve(nc.vector.memset, step, 1.0, link=False)
    s.emit()
    s = Section(kit.pr, "l1_threshold")
    everyone = kit.c("ones")

    def count_flags():
        own = s.dve(nc.vector.tensor_reduce, part8, flags.rearrange("p t e -> p e t"), AX, ALU.add)
        return s.mm(banks[6][:, 0:E], everyone, part8, after=[own])

    s.dve(nc.vector.tensor_tensor, cand, thr, step, ALU.add)
    s.dve(nc.vector.tensor_tensor, flags, scores, cand.unsqueeze(1).broadcast_to([P, L1_FFN_ALL, E]), ALU.is_ge)
    total = count_flags()
    s.dve(nc.vector.tensor_scalar, keep, banks[6][:, 0:E], L1_FFN_PLACES - 0.5, None, ALU.is_gt, after=[total])
    s.dve(nc.vector.tensor_tensor, keep, keep, step, ALU.mult)
    s.dve(nc.vector.tensor_tensor, thr, thr, keep, ALU.add)
    s.dve(nc.vector.tensor_scalar, step, step, 0.5, None, ALU.mult)
    s.emit(1, L1_FFN_SCORE_BITS)

    s = Section(kit.pr, "l1_taken")
    need, pre0, pre1, sums = arena.take(E), arena.take(L1_FFN_ALL, E), arena.take(L1_FFN_ALL, E), arena.take(L1_FFN_ALL, E)
    bound = thr.unsqueeze(1).broadcast_to([P, L1_FFN_ALL, E])
    s.dve(nc.vector.tensor_tensor, flags, scores, bound, ALU.is_gt)
    total = count_flags()
    s.dve(nc.vector.tensor_scalar, need, banks[6][:, 0:E], -1.0, float(L1_FFN_PLACES), ALU.mult, ALU.add, after=[total])
    above = s.dve(nc.vector.tensor_copy, taken, flags)
    equal = s.dve(nc.vector.tensor_tensor, flags, scores, bound, ALU.is_equal)
    width = L1_FFN_ALL * E
    flat = flags.rearrange("p t e -> p (t e)")
    within = s.mm(banks[5][:, 0:width], kit.c("tri_strict"), flat, after=[equal])
    tile_sums = s.mm(banks[4][:, 0:width], everyone, flat)
    s.dve(nc.vector.tensor_copy, sums, banks[4][:, 0:width].rearrange("p (t e) -> p t e", e=E), after=[tile_sums])
    s.dve(nc.vector.memset, pre0[:, 0:1, :], 0.0)
    s.dve(nc.vector.tensor_copy, pre0[:, 1:L1_FFN_ALL, :], sums[:, 0:L1_FFN_ALL - 1, :])
    a, b, n = pre0, pre1, 1
    while n < L1_FFN_ALL:
        s.dve(nc.vector.tensor_copy, b[:, 0:n, :], a[:, 0:n, :])
        s.dve(nc.vector.tensor_tensor, b[:, n:L1_FFN_ALL, :], a[:, n:L1_FFN_ALL, :], a[:, 0:L1_FFN_ALL - n, :], ALU.add, link=False)
        a, b, n = b, a, n * 2
    s.dve(nc.vector.tensor_tensor, a, a, banks[5][:, 0:width].rearrange("p (t e) -> p t e", e=E), ALU.add,
          after=[within])
    s.dve(nc.vector.tensor_tensor, a, a, need.unsqueeze(1).broadcast_to([P, L1_FFN_ALL, E]), ALU.is_lt)
    s.dve(nc.vector.tensor_tensor, a, a, flags, ALU.mult)
    s.dve(nc.vector.tensor_tensor, taken, taken, a, ALU.add)
    s.dve(nc.vector.tensor_tensor, taken, taken, scores, ALU.mult)
    s.emit()

    s = Section(kit.pr, "l1_experts", LANES)
    def batch(lane):
        s.use(lane)
        xr, z, y, zT, mv, stats, rstd = own[lane]
        acc, yT, shareT = arena.take(TILES, P), arena.take(SEQ), arena.take(SEQ)
        share = arena.take(TILES, E)
        hid = Ring([arena.take(L1_FFN_FF1, SEQ), arena.take(L1_FFN_FF1, SEQ)])
        banks = kit.banks(lane)
        ring, yring = Ring(banks[0:3]), Ring(banks[3:4])
        loaded = s.dve(nc.vector.tensor_copy, xr, kit.rows_of(X, lane))
        weights = s.dve(nc.vector.tensor_copy, share, kit.rows_of(taken, lane))
        rows = norm_rows(kit, s, xr, z, mv, stats, rstd, LN_EPS, after=[loaded])
        settle(kit, s)
        rows = norm_rows(kit, s, z, y, mv, stats, rstd, LN_EPS, after=[rows])
        feats = to_features(kit, s, ring, [y[:, t, :] for t in range(TILES)], yT, [rows], scale=w("gamma"), bias=w("beta"))
        shares = to_features(kit, s, ring, [share[:, t, :] for t in range(TILES)], shareT[0:E, :], [weights], rows=E)

        def hidden_all(e, started):
            hT, free, hk = hid.take()
            for f in range(L1_FFN_FF1):
                bank, bfree, k = ring.take()
                up = s.mm(bank[:, :], w(f"up{e}", cols=(f * P, (f + 1) * P)), yT, after=[*bfree, *started])
                c = e * L1_FFN_FF1 + f
                act = s.act(nc.scalar.activation, hT[:, f, :], bank[:, :], ACT.Gelu_apprx_tanh,
                            bias=w("b1", cols=(c, c + 1)), after=[up, *(free if f == 0 else ())])
                ring.give(k, act)
            return hT, hk, act

        done = weighted_experts(kit, s, hidden_all, lambda e, t: share[:, t, e:e + 1], acc,
                                lambda e, f: w(f"down{e}_{f}"), L1_FFN_FF1, hid, yring, [feats])
        bank, free, k = yring.take()
        for t in range(TILES):
            biases = s.mm(bank[:, t * P:(t + 1) * P], shareT[0:E, t * P:(t + 1) * P], w("b2"),
                          after=[shares, *free] if t == 0 else (), signal=(t == TILES - 1))
        s.dve(nc.vector.tensor_tensor, acc, acc, bank[:, :].rearrange("p (t d) -> p t d", d=P), ALU.add,
              after=[biases, done])
        s.dve(nc.vector.tensor_tensor, acc, acc, z, ALU.add)
        s.dve(nc.vector.tensor_tensor, kit.rows_of(X, lane), xr, acc, ALU.add)

    for lane in range(LANES):
        batch(lane)
    s.emit(1, BATCH // LANES)




L2_ATTN_CONV, L2_ATTN_DV = 4, 64
L2_ATTN_VAL = HEADS * L2_ATTN_DV
L2_ATTN_GROUPS = TILES * HEADS


def layout_l2_attn(w):
    bc = lambda v: np.broadcast_to(np.reshape(v, (1, -1)), (P, np.size(v)))
    parts = [("q", w["Wq"]), ("k", w["Wk"]), ("v", w["Wv"]), ("ab", np.concatenate([w["Wa"], w["Wb"]], axis=1)),
             ("gate", w["Wg"]), ("q_conv", w["conv_q_w"]), ("k_conv", w["conv_k_w"]),
             ("v_conv0", w["conv_v_w"][:P]), ("v_conv1", w["conv_v_w"][P:]), ("o0", w["Wo"][:P]), ("o1", w["Wo"][P:]),
             ("w2", w["W2"]), ("b2", bc(w["b2"])), ("ln1_g", bc(w["ln1_g"])), ("ln1_b", bc(w["ln1_b"])),
             ("dt", bc(w["dt_bias"])), ("A", bc(w["A_log"])), ("o_norm", np.tile(w["o_norm_w"], 2)[:, None])]
    return parts + [(c, w[c][:, None]) for c in ("rms_in_w", "ln2_g", "ln2_b")]


def stage_l2_attn(kit, w, arena):
    nc, X = kit.nc, kit.X
    padded = [[arena.take(L2_ATTN_CONV - 1 + SEQ) for _ in range(2)] for _ in range(LANES)]
    rate = arena.take(HEADS)
    s = Section(kit.pr, "l2_start")
    for b in padded[0] + padded[1]:
        s.dve(nc.vector.memset, b[:, 0:L2_ATTN_CONV - 1], 0.0, link=False)
    grown = s.act(nc.scalar.activation, rate, w("A"), ACT.Exp)
    s.dve(nc.vector.tensor_scalar, rate, rate, -1.0, None, ALU.mult, after=[grown])
    s.emit()

    s = Section(kit.pr, "l2_attn", LANES)
    def batch(lane):
        s.use(lane)
        z, a, hT = arena.take(TILES, P), arena.take(TILES, P), arena.take(SEQ)
        stats, mv, rstd = arena.take(TILES, 6), arena.take(TILES, 2), arena.take(TILES)
        qrow, krow, kb = (arena.take(TILES, P) for _ in range(3))
        xr = qrow
        vrow, gates, orow = (arena.take(TILES, L2_ATTN_VAL) for _ in range(3))
        kT, kbq = arena.take(TILES, P), arena.take(TILES, 2, P)
        gt = arena.take(2, HEADS, P)
        gtm = arena.take(2, HEADS, P)
        conv = [gt[:, 0], gt[:, 1], gtm[:, 0], gtm[:, 1]]
        conv = [c.rearrange("p h n -> p (h n)") for c in conv]
        gtri = a
        beta, g, spread = arena.take(TILES, HEADS), arena.take(TILES, HEADS), arena.take(TILES, HEADS)
        t1, t2, t3 = (arena.take(TILES, HEADS) for _ in range(3))
        dec = arena.take(2 * L2_ATTN_GROUPS + TILES)
        ss, rn = arena.take(2, L2_ATTN_GROUPS), arena.take(2, L2_ATTN_GROUPS)
        delta = Delta(kit, arena, L2_ATTN_DV, True)
        ring = Ring(kit.banks(lane))
        flat = lambda v: v.rearrange("p t n -> p (t n)")
        heads = lambda v, d=DK: v.rearrange("p t (h d) -> p (t h) d", d=d)
        tok = lambda v: [v[:, t, :] for t in range(TILES)]
        blocks = lambda v: [v[:, t * P:(t + 1) * P] for t in range(TILES)]
        rows_of = lambda name: w(name).unsqueeze(1).broadcast_to([P, TILES, P])

        def inverse_root(dst, src, scale, eps, width, after):
            shifted = s.dve(nc.vector.tensor_scalar, src, src, scale, eps, ALU.mult, ALU.add, after=after)
            return s.pool(nc.gpsimd.tensor_tensor, dst, src, kit.c("neghalf", cols=(0, width)), ALU.pow, after=[shifted])

        loaded = s.dve(nc.vector.tensor_copy, xr, kit.rows_of(X, lane))
        rows = norm_rows(kit, s, xr, z, mv, stats, rstd, LN_EPS, after=[loaded])
        settle(kit, s)
        norm_rows(kit, s, z, a, mv, stats, rstd, LN_EPS, after=[rows])
        s.dve(nc.vector.tensor_tensor, a, a, rows_of("ln1_g"), ALU.mult)
        affine = s.dve(nc.vector.tensor_tensor, a, a, rows_of("ln1_b"), ALU.add)
        sq = s.act(nc.scalar.activation, kb, a, ACT.Square, after=[affine])
        s.dve(nc.vector.tensor_reduce, rstd, kb, AX, ALU.add, after=[sq])
        root = inverse_root(mv[:, :, 0], rstd, 1.0 / P, 1e-6, TILES, ())
        scaled = s.dve(nc.vector.tensor_tensor, a, a, over(mv[:, :, 0], P), ALU.mult, after=[root])
        feats = to_features(kit, s, ring, tok(a), hT, [scaled], scale=w("rms_in_w"))
        bank, free, k = ring.take()
        for t in range(TILES):
            made = s.mm(bank[:, t * 8:(t + 1) * 8], hT[:, t * P:(t + 1) * P], w("ab"), after=[feats, *free] if t == 0 else (),
                        signal=t == TILES - 1)
        ab = bank[:, 0:TILES * 8].rearrange("p (t c) -> p t c", c=8)
        betas = s.act(nc.scalar.activation, beta, ab[:, :, HEADS:8], ACT.Sigmoid, after=[made])
        s.dve(nc.vector.tensor_tensor, g, ab[:, :, 0:HEADS], w("dt").unsqueeze(1).broadcast_to([P, TILES, HEADS]), ALU.add,
              after=[made, betas])
        given = s.dve(nc.vector.tensor_scalar, t1, g, -1.0, None, ALU.mult)
        ring.give(k, given)
        low = s.dve(nc.vector.tensor_tensor, t1, t1, g, ALU.min)
        ex = s.act(nc.scalar.activation, t1, t1, ACT.Exp, after=[low])
        log1p(kit, s, t1, t2, t3, spread, after=[ex])
        s.dve(nc.vector.tensor_scalar, g, g, 0.0, None, ALU.max)
        s.dve(nc.vector.tensor_tensor, g, g, spread, ALU.add)
        logs = s.dve(nc.vector.tensor_tensor, g, g, rate.unsqueeze(1).broadcast_to([P, TILES, HEADS]), ALU.mult)
        gflat = g.rearrange("p t h -> p (t h)")
        wide = s.dve(nc.vector.tensor_copy, heads(orow[:, 0:2, :].rearrange("p a b -> p (a b)").rearrange(
            "p (t n) -> p t n", t=TILES)), over(gflat, DK))
        bank, free, k = ring.take()
        s.mm(bank[:, 0:L2_ATTN_GROUPS], kit.c("tri_incl"), gflat, after=[logs, wide, *free], signal=False)
        s.mm(bank[:, L2_ATTN_GROUPS:2 * L2_ATTN_GROUPS], kit.c("after"), gflat, signal=False)
        wide_rows = orow[:, 0:2, :].rearrange("p a b -> p (a b)")
        for t in range(TILES):
            made = s.mm(bank[:, 2 * L2_ATTN_GROUPS + t:2 * L2_ATTN_GROUPS + t + 1], wide_rows[:, t * P:(t + 1) * P],
                        kit.c("ones", cols=(0, 1)), signal=t == TILES - 1)
        decayed = s.act(nc.scalar.activation, dec, bank[:, 0:2 * L2_ATTN_GROUPS + TILES], ACT.Exp, after=[made])
        ring.give(k, decayed)
        from_start, to_end, whole = dec[:, 0:L2_ATTN_GROUPS], dec[:, L2_ATTN_GROUPS:2 * L2_ATTN_GROUPS], dec[:, 2 * L2_ATTN_GROUPS:]
        shaped, convolved = [], []
        for n, (name, cols, taps) in enumerate((("q", (0, P), "q_conv"), ("k", (0, P), "k_conv"),
                                                ("v", (0, P), "v_conv0"), ("v", (P, 2 * P), "v_conv1"))):
            bank, free, k = ring.take()
            made = s.mm(bank[:, :], w(name, cols=cols), hT, after=[feats, *free])
            before = padded[lane][n % 2]
            moved = s.act(nc.scalar.copy, before[:, L2_ATTN_CONV - 1:], bank[:, :], after=[made, *convolved[-2:-1]])
            ring.give(k, moved)
            for j in range(L2_ATTN_CONV):
                view = before[:, j:j + SEQ]
                if j == 0:
                    done = s.dve(nc.vector.tensor_scalar, conv[n], view, w(taps, cols=(0, 1)), None, ALU.mult,
                                 after=[moved])
                else:
                    done = s.dve(nc.vector.scalar_tensor_tensor, conv[n], view, w(taps, cols=(j, j + 1)), conv[n],
                                 ALU.mult, ALU.add)
            convolved.append(done)
            shaped.append(s.act(nc.scalar.activation, conv[n], conv[n], ACT.Silu, after=[done]))
        for pair in range(2):
            bank, free, k = ring.take()
            for j in range(2):
                t = 2 * pair + j
                made = s.mm(bank[:, j * L2_ATTN_VAL:(j + 1) * L2_ATTN_VAL], hT[:, t * P:(t + 1) * P], w("gate"),
                            after=free if j == 0 else (), signal=j == 1)
            gated = s.act(nc.scalar.activation, gates[:, 2 * pair:2 * pair + 2, :],
                          bank[:, :].rearrange("p (t n) -> p t n", n=L2_ATTN_VAL), ACT.Silu, after=[made])
            ring.give(k, gated)
        turned = [to_features(kit, s, ring, blocks(conv[2 + n]), vrow[:, :, n * P:(n + 1) * P], [shaped[2 + n]])
                  for n in range(2)]
        for n, dst in enumerate((qrow, krow)):
            raw = to_features(kit, s, ring, blocks(conv[n]), flat(dst), [shaped[n]])
            turned.append(raw)
            sq = s.act(nc.scalar.activation, kb, dst, ACT.Square, after=[raw, s.latest("DVE")], link=True)
            s.dve(nc.vector.tensor_reduce, ss[:, n, :], heads(kb), AX, ALU.add, after=[sq])
            factor = float(DK) if n == 0 else 1.0
            root = inverse_root(rn[:, n, :], ss[:, n, :], factor, factor * 1e-6, L2_ATTN_GROUPS, ())
            unit = s.dve(nc.vector.tensor_tensor, heads(dst), heads(dst), over(rn[:, n, :], DK), ALU.mult, after=[root])
        by_beta = beta.rearrange("p t h -> p (t h)")
        s.dve(nc.vector.tensor_tensor, heads(kb), heads(krow), over(by_beta, DK), ALU.mult, after=[betas])
        ready = s.dve(nc.vector.tensor_tensor, heads(vrow, L2_ATTN_DV), heads(vrow, L2_ATTN_DV), over(by_beta, L2_ATTN_DV), ALU.mult,
                      after=turned)
        keyed = [to_features(kit, s, ring, tok(krow), flat(kT), [ready])]
        for n, src in enumerate((kb, qrow)):
            bank, free, k = ring.take()
            for t in range(TILES):
                made = s.tr(bank[:, t * P:(t + 1) * P], src[:, t, :], kit.ident, after=[ready, *free] if t == 0 else (),
                            signal=t == TILES - 1)
            keyed.append(s.act(nc.scalar.copy, kbq[:, :, n, :], bank[:, :].rearrange("p (t n) -> p t n", n=P),
                               after=[made]))
            ring.give(k, keyed[-1])
        s.dve(nc.vector.tensor_tensor, heads(kb), heads(kb), over(from_start, DK), ALU.mult, after=[decayed, *keyed])
        weighed = s.dve(nc.vector.tensor_tensor, heads(krow), heads(krow), over(to_end, DK), ALU.mult)

        state = delta.start(s)
        chunk_heads = lambda v, c, d=DK: v[:, c, :].rearrange("p (h d) -> p h d", d=d)
        for pair in range(2):
            chunks = (2 * pair, 2 * pair + 1)
            for j, c in enumerate(chunks):
                steps = s.dve(nc.vector.tensor_tensor, gtri, kit.c("tri_incl").unsqueeze(1).broadcast_to([P, HEADS, P]),
                              over(g[:, c, :], P), ALU.mult, after=[weighed, feats])
                bank, free, k = ring.take()
                made = s.mm(bank[:, :], kit.c("after"), flat(gtri), after=[steps, *free])
                pairwise = s.act(nc.scalar.activation, gt[:, j].rearrange("p h n -> p (h n)"), bank[:, :], ACT.Exp,
                                 after=[made, s.latest("DVE")])
                ring.give(k, pairwise)
                s.dve(nc.vector.tensor_tensor, gtm[:, j], gt[:, j],
                      kit.c("tri_incl").unsqueeze(1).broadcast_to([P, HEADS, P]), ALU.mult, after=[pairwise])
            settle(kit, s)
            xt, scored = delta.invert(s, ring, chunks, lambda c: kT[:, c, :],
                                      lambda c: kbq[:, c].rearrange("p a n -> p (a n)"), gt, keyed, gt_masked=gtm)
            for j, c in enumerate(chunks):
                state, got = delta.advance(s, ring, j, state, [*xt, *scored, weighed], kbq[:, c, 1, :],
                                           chunk_heads(vrow, c, L2_ATTN_DV), chunk_heads(kb, c), krow[:, c, :],
                                           chunk_heads(orow, c, L2_ATTN_DV), out_scale=from_start[:, c * HEADS:(c + 1) * HEADS],
                                           chunk_decay=whole[:, c:c + 1])
        sq = s.act(nc.scalar.activation, vrow, orow, ACT.Square, after=[got, state])
        s.dve(nc.vector.tensor_reduce, ss[:, 0, :], heads(vrow, L2_ATTN_DV), AX, ALU.add, after=[sq])
        root = inverse_root(rn[:, 0, :], ss[:, 0, :], 1.0 / L2_ATTN_DV, 1e-6, L2_ATTN_GROUPS, ())
        s.dve(nc.vector.tensor_tensor, orow, orow, gates, ALU.mult, after=[gated])
        ready = s.dve(nc.vector.tensor_tensor, heads(orow, L2_ATTN_DV), heads(orow, L2_ATTN_DV), over(rn[:, 0, :], L2_ATTN_DV), ALU.mult,
                      after=[root])
        oT = [conv[0], conv[1]]
        out_feats = [to_features(kit, s, ring, [orow[:, t, n * P:(n + 1) * P] for t in range(TILES)], oT[n], [ready],
                                 scale=w("o_norm")) for n in range(2)]
        bank, free, k = ring.take()
        for t in range(TILES):
            for n in range(2):
                made = s.mm(bank[:, t * P:(t + 1) * P], oT[n][:, t * P:(t + 1) * P], w(f"o{n}"), start=n == 0,
                            stop=n == 1, after=[*out_feats, *free] if t == 0 and n == 0 else (),
                            signal=t == TILES - 1 and n == 1)
        by_tile = lambda bank: bank[:, :].rearrange("p (t d) -> p t d", d=P)
        added = s.dve(nc.vector.tensor_tensor, z, z, by_tile(bank), ALU.add, after=[made])
        ring.give(k, added)
        rows = norm_rows(kit, s, z, a, mv, stats, rstd, LN_EPS, after=[added])
        feats = to_features(kit, s, ring, tok(a), hT, [rows], scale=w("ln2_g"), bias=w("ln2_b"))
        bank, free, k = ring.take()
        for t in range(TILES):
            made = s.mm(bank[:, t * P:(t + 1) * P], hT[:, t * P:(t + 1) * P], w("w2"),
                        after=[feats, *free] if t == 0 else (), signal=t == TILES - 1)
        biased = s.dve(nc.vector.tensor_tensor, a, by_tile(bank), rows_of("b2"), ALU.add, after=[made])
        gelu = s.act(nc.scalar.activation, a, a, ACT.Gelu, after=[biased])
        s.dve(nc.vector.tensor_tensor, z, z, a, ALU.add, after=[gelu])
        s.dve(nc.vector.tensor_tensor, kit.rows_of(X, lane), kit.rows_of(X, lane), z, ALU.add)

    for lane in range(LANES):
        batch(lane)
    s.emit(1, BATCH // LANES)




L2_FFN_DEPTH, L2_FFN_HEADS, L2_FFN_HD = 2, 8, 64
L2_FFN_PAIRS = L2_FFN_HEADS // 2
L2_FFN_BACK = 64
L2_FFN_SPAN = L2_FFN_BACK + P
L2_FFN_HID = 341
L2_FFN_FF = 3
L2_FFN_WIDTH = [P, P, L2_FFN_HID - 2 * P]
L2_FFN_QK_SCALE = 8.0


def layout_l2_ffn(w):
    parts = []
    for n in range(L2_FFN_DEPTH):
        bc = lambda v: np.broadcast_to(v[None, :], (P, v.shape[0]))
        one = [("qkv", w["wqkv"][n]), ("up", w["w1"][n]), ("b2", bc(w["b2"][n]))]
        one += [(f"o{j}", w["wo"][n][j * P:(j + 1) * P]) for j in range(L2_FFN_PAIRS)]
        one += [(f"down{f}", w["w2"][n][f * P:f * P + L2_FFN_WIDTH[f]]) for f in range(L2_FFN_FF)]
        for half in range(2):
            one += [(f"b1_{half}_{f}", w["b1"][n][half * L2_FFN_HID + f * P:half * L2_FFN_HID + f * P + L2_FFN_WIDTH[f], None])
                    for f in range(L2_FFN_FF)]
        one += [(c, w[c][n][:, None]) for c in ("ln_g", "ln_b")]
        one += [(c, bc(w[c][n])) for c in ("q_scale", "k_scale")]
        parts += [(name if n == 0 else f"{name}@{n}", a) for name, a in one]
    return parts


def stage_l2_ffn(kit, w, arena):
    nc, X = kit.nc, kit.X
    layer_cols = w.where["qkv@1"][0] - w.where["qkv"][0]
    Yall = arena.take(BATCH * TILES, P)
    static = arena.take(layer_cols)
    wl = Weights(static, w.where)
    small = [(arena.take(TILES, 2), arena.take(TILES, 6), arena.take(TILES)) for _ in range(LANES)]
    ys, hs = ([arena.take(TILES, P) for _ in range(LANES)] for _ in range(2))
    shifted_of = [arena.take(SEQ + 1) for _ in range(LANES)]
    probs_of = [[arena.take(4, 2 * P) for _ in range(2)] for _ in range(LANES)]

    s = Section(kit.pr, "l2f_enter", LANES)

    def enter(lane):
        s.use(lane)
        y, h = ys[lane], hs[lane]
        loaded = s.dve(nc.vector.tensor_copy, h, kit.rows_of(X, lane))
        norm_rows(kit, s, h, y, *small[lane], LN_EPS, after=[loaded])
        s.dve(nc.vector.tensor_copy, kit.rows_of(Yall, lane), y)

    for lane in range(LANES):
        enter(lane)
    s.emit(1, BATCH // LANES)
    s = Section(kit.pr, "l2f_zero")
    for shifted in shifted_of:
        s.dve(nc.vector.memset, shifted[:, 0:1], 0.0)
    for pr in probs_of[0] + probs_of[1]:
        s.dve(nc.vector.memset, pr[:, :, 0:L2_FFN_BACK], 0.0, link=False)
    s.emit()

    s = Section(kit.pr, "l2f_layers", LANES)
    rope = {n: arena.take(TILES, L2_FFN_HD) for n in ("cos_q", "sin_q", "cos_k", "sin_k")}
    weights = s.pool(nc.gpsimd.tensor_copy, static, At(lambda o, i: w.tensor[:, ds(o * layer_cols + w.at, layer_cols)]))
    for side in "qk":
        sc = wl(f"{side}_scale")
        for name, lo, hi, frm in ((f"cos_{side}", 0, L2_FFN_HD, 0), (f"sin_{side}", 0, L2_FFN_HD // 2, L2_FFN_HD // 2),
                                  (f"sin_{side}", L2_FFN_HD // 2, L2_FFN_HD, 0)):
            tab = kit.c(name).rearrange("p (t d) -> p t d", d=L2_FFN_HD)
            s.dve(nc.vector.tensor_tensor, rope[name][:, :, lo:hi], tab[:, :, lo:hi],
                           sc[:, frm:frm + hi - lo].unsqueeze(1).broadcast_to([P, TILES, hi - lo]), ALU.mult,
                           after=[weights], link=False)
    tables = s.dve(nc.vector.memset, kit.c("scratch", cols=(0, 1)), 0.0)

    def batch(lane):
        s.use(lane)
        y, h, shifted = ys[lane], hs[lane], shifted_of[lane]
        probs = Ring(probs_of[lane])
        mv, stats, rstd = small[lane]
        qT = Ring([arena.take(L2_FFN_PAIRS, P) for _ in range(2)])
        kT = arena.take(L2_FFN_PAIRS, SEQ)
        v = arena.take(TILES, L2_FFN_HEADS * L2_FFN_HD)
        scratch = arena.take(4, L2_FFN_HEADS * L2_FFN_HD)
        cos_part, sin_part = scratch[:, 0], scratch[:, 1]
        square = sin_part
        orow = Ring([scratch[:, 2]])
        oT = Ring([scratch[:, 3]])
        turned = Ring([arena.take(8, P) for _ in range(1)])
        ss, rn = arena.take(L2_FFN_HEADS), arena.take(2, L2_FFN_HEADS)
        top, sums, inv = arena.take(L2_FFN_HEADS), arena.take(L2_FFN_HEADS), arena.take(L2_FFN_HEADS)
        ff = kT.rearrange("p a b -> p (a b)")[:, 0:L2_FFN_FF * SEQ].rearrange("p (f c) -> p f c", f=L2_FFN_FF)
        gel = Ring([scratch[:, 0], scratch[:, 1]])
        ring = Ring(kit.banks(lane))

        loaded = s.dve(nc.vector.tensor_copy, y, kit.rows_of(Yall, lane))

        def shift(rows, after):
            bank, free, k = ring.take()
            for t in range(TILES):
                made = s.tr(bank[:, t * P:(t + 1) * P], rows[:, t, :], kit.ident,
                            after=[*after, *free] if t == 0 else (), signal=t == TILES - 1)
            s.act(nc.scalar.copy, shifted[0:64, 0:SEQ], bank[0:64, :], after=[made])
            done = s.act(nc.scalar.copy, shifted[64:P, 1:SEQ + 1], bank[64:P, :])
            ring.give(k, done)
            return done

        feats = shift(y, [loaded])
        xT = shifted[:, 0:SEQ]
        def heads3(view):
            return view.rearrange("p (h d) -> p h d", d=L2_FFN_HD)

        def project(t):
            made = []
            for part in range(3):
                bank, free, k = ring.take()
                made.append((bank, k, s.mm(bank[:, :], xT[:, t * P:(t + 1) * P],
                                           wl("qkv", cols=(part * 512, (part + 1) * 512)),
                                           after=[feats, weights, *free])))
            q_dst, qfree, qk = qT.take()
            moved = []
            for part, side in enumerate("qk"):
                bank, k, got = made[part]
                sq = s.act(nc.scalar.activation, square, bank[:, :], ACT.Square,
                           after=[got, s.latest("DVE")])
                s.dve(nc.vector.tensor_reduce, ss, heads3(square), AX, ALU.add, after=[sq])
                floor = s.dve(nc.vector.tensor_scalar, ss, ss, 1e-24, None, ALU.max)
                root = s.pool(nc.gpsimd.tensor_tensor, rn[:, part, :], ss, kit.c("neghalf", cols=(0, L2_FFN_HEADS)), ALU.pow,
                              after=[floor])
                cos, sin = rope[f"cos_{side}"][:, t, :], rope[f"sin_{side}"][:, t, :]
                src = heads3(bank[:, :])
                free_before = moved[-1:] if moved else []
                s.dve(nc.vector.tensor_tensor, heads3(cos_part), src,
                      cos.unsqueeze(1).broadcast_to([P, L2_FFN_HEADS, L2_FFN_HD]), ALU.mult, after=[tables, *free_before])
                for lo, frm in ((0, L2_FFN_HD // 2), (L2_FFN_HD // 2, 0)):
                    last = s.dve(nc.vector.tensor_tensor, heads3(sin_part)[:, :, lo:lo + L2_FFN_HD // 2],
                                 src[:, :, frm:frm + L2_FFN_HD // 2],
                                 sin[:, lo:lo + L2_FFN_HD // 2].unsqueeze(1).broadcast_to([P, L2_FFN_HEADS, L2_FFN_HD // 2]), ALU.mult,
                                 link=False)
                ring.give(k, last)
                s.dve(nc.vector.tensor_tensor, cos_part, cos_part, sin_part, ALU.add)
                done = s.dve(nc.vector.tensor_tensor, heads3(cos_part), heads3(cos_part), over(rn[:, part, :], L2_FFN_HD),
                             ALU.mult, after=[root])
                bank, free, k = ring.take()
                for j in range(L2_FFN_PAIRS):
                    flipped = s.tr(bank[:, j * P:(j + 1) * P], cos_part[:, j * P:(j + 1) * P], kit.ident,
                                   after=[done, *free] if j == 0 else (), signal=j == L2_FFN_PAIRS - 1)
                dst = q_dst if side == "q" else kT[:, :, t * P:(t + 1) * P]
                moved.append(s.act(nc.scalar.copy, dst, bank[:, :].rearrange("p (j c) -> p j c", j=L2_FFN_PAIRS),
                                   after=[flipped, *(qfree if side == "q" else ())]))
                ring.give(k, moved[-1])
            bank, k, got = made[2]
            values = s.act(nc.scalar.copy, v[:, t, :], bank[:, :], after=[got])
            ring.give(k, values)
            return q_dst, qk, [*moved, values]

        def attend(t, q_src, qk, ready):
            keys_at = slice(max(t * P - L2_FFN_BACK, 0), (t + 1) * P)
            lo = 0 if t else L2_FFN_BACK
            n = L2_FFN_SPAN - lo
            obank, ofree, okk = ring.take()
            for group in range(2):
                got = []
                for side in range(2):
                    bank, free, k = ring.take()
                    part = slice(64 * side, 64 * side + 64)
                    for j in range(2):
                        out = bank[:, j * L2_FFN_SPAN:j * L2_FFN_SPAN + n]
                        s.mm(out, kit.ident, kit.c("band", cols=(lo, L2_FFN_SPAN)), stop=False,
                             after=[*ready, *free] if j == 0 else (), signal=False)
                        made = s.mm(out, q_src[part, 2 * group + j, :], kT[part, 2 * group + j, keys_at], start=False,
                                    signal=j == 1)
                    got.append((bank, k, made))
                pr, pfree, pk = probs.take()
                for side, (bank, k, made) in enumerate(got):
                    for j in range(2):
                        c = 4 * group + 2 * j + side
                        s.dve(nc.vector.tensor_reduce, top[:, c:c + 1], bank[:, j * L2_FFN_SPAN:j * L2_FFN_SPAN + n], AX, ALU.max,
                              after=[made], link=False)
                these = slice(4 * group, 4 * group + 4)
                neg = s.dve(nc.vector.tensor_scalar, top[:, these], top[:, these], -L2_FFN_QK_SCALE, None, ALU.mult)
                for side, (bank, k, made) in enumerate(got):
                    for j in range(2):
                        hh = 2 * j + side
                        c = 4 * group + hh
                        done = s.act(nc.scalar.activation, pr[:, hh, L2_FFN_BACK + lo:2 * P], bank[:, j * L2_FFN_SPAN:j * L2_FFN_SPAN + n],
                                     ACT.Exp, scale=L2_FFN_QK_SCALE, bias=top[:, c:c + 1], accum_out=sums[:, c:c + 1],
                                     after=[neg, *pfree])
                        pfree = ()
                    ring.give(k, done)
                dst, dfree, dk = turned.take()
                flips = []
                for side in ((0, 1) if t else (1,)):
                    bank, free, k = ring.take()
                    for hh in range(4):
                        made = s.tr(bank[:, hh * P:(hh + 1) * P], pr[:, hh, side * P:(side + 1) * P], kit.ident,
                                    after=[done, *free] if hh == 0 else (), signal=hh == 3)
                    to = dst[:, 4 * side:4 * side + 4, :].rearrange("p h q -> p (h q)")
                    if side:
                        flips.append(s.act(nc.scalar.copy, to, bank[:, :], after=[made, *dfree]))
                    else:
                        flips.append(s.dve(nc.vector.tensor_copy, to, bank[:, :], after=[made, *dfree], link=False))
                    ring.give(k, flips[-1])
                probs.give(pk, made)
                for hh in range(4):
                    c = 4 * group + hh
                    cols = slice(c * L2_FFN_HD, (c + 1) * L2_FFN_HD)
                    for side in ((0, 1) if t else (1,)):
                        out = s.mm(obank[:, cols], dst[:, 4 * side + hh, :], v[:, t - 1 + side, cols],
                                   start=side == 1 and t == 0 or side == 0, stop=side == 1,
                                   after=[*flips, *ofree] if hh == 0 else (), signal=hh == 3 and side == 1)
                turned.give(dk, out)
            qT.give(qk, out)
            s.dve(nc.vector.reciprocal, inv, sums, after=[out])
            row, rfree, rk = orow.take()
            normed = s.dve(nc.vector.tensor_tensor, heads3(row), heads3(obank[:, :]), over(inv, L2_FFN_HD), ALU.mult,
                           after=rfree)
            ring.give(okk, normed)
            oT_, tfree, tk = oT.take()
            flipped = to_features(kit, s, ring, [row[:, j * P:(j + 1) * P] for j in range(L2_FFN_PAIRS)], oT_, [normed, *tfree])
            orow.give(rk, flipped)
            bank, free, k = ring.take()
            for j in range(L2_FFN_PAIRS):
                made = s.mm(bank[:, 0:P], oT_[:, j * P:(j + 1) * P], wl(f"o{j}"), start=j == 0, stop=j == L2_FFN_PAIRS - 1,
                            after=[flipped, *free] if j == 0 else (), signal=j == L2_FFN_PAIRS - 1)
            oT.give(tk, made)
            done = s.dve(nc.vector.tensor_tensor, y[:, t, :], y[:, t, :], bank[:, 0:P], ALU.add, after=[made])
            ring.give(k, done)
            return done

        for t in range(TILES):
            attended = attend(t, *project(t))

        with_b2 = s.pool(nc.gpsimd.tensor_tensor, h, y, wl("b2").unsqueeze(1).broadcast_to([P, TILES, P]), ALU.add,
                         after=[attended])
        feats = shift(y, [attended])
        bank, free, k = ring.take()
        for t in range(TILES):
            made = s.tr(bank[:, t * P:(t + 1) * P], xT[:, t * P:(t + 1) * P], kit.ident,
                        after=[feats, *free] if t == 0 else (), signal=t == TILES - 1)
        normed = norm_rows(kit, s, bank[:, :].rearrange("p (t d) -> p t d", d=P), y, mv, stats, rstd, LN_EPS,
                           after=[made, feats, with_b2])
        ring.give(k, normed)
        hT = v[:, 0, :]
        feats = to_features(kit, s, ring, [y[:, t, :] for t in range(TILES)], hT, [normed],
                            scale=wl("ln_g"), bias=wl("ln_b"))
        for f in range(L2_FFN_FF):
            n = L2_FFN_WIDTH[f]
            parts = []
            for half in range(2):
                bank, free, k = ring.take()
                at = half * L2_FFN_HID + f * P
                parts.append((bank, k, s.mm(bank[0:n, :], wl("up", cols=(at, at + n)), hT, after=[feats, *free])))
            g, gfree, gk = gel.take()
            bank, k, made = parts[1]
            gelu = s.act(nc.scalar.activation, g[0:n, :], bank[0:n, :], ACT.Gelu, bias=wl(f"b1_1_{f}"),
                         after=[made, *gfree])
            ring.give(k, gelu)
            bank, k, made = parts[0]
            gated = s.dve(nc.vector.scalar_tensor_tensor, ff[0:n, f, :], bank[0:n, :], wl(f"b1_0_{f}"), g[0:n, :],
                          ALU.add, ALU.mult, after=[made, gelu], link=False)
            ring.give(k, gated)
            gel.give(gk, gated)
        bank, free, k = ring.take()
        for t in range(TILES):
            for f in range(L2_FFN_FF):
                made = s.mm(bank[:, t * P:(t + 1) * P], ff[0:L2_FFN_WIDTH[f], f, t * P:(t + 1) * P], wl(f"down{f}"),
                            start=f == 0, stop=f == L2_FFN_FF - 1, after=[gated, *free] if t == 0 and f == 0 else (),
                            signal=t == TILES - 1 and f == L2_FFN_FF - 1)
        s.dve(nc.vector.tensor_tensor, kit.rows_of(Yall, lane), h, bank[:, :].rearrange("p (t d) -> p t d", d=P), ALU.add,
              after=[made])

    for lane in range(LANES):
        batch(lane)
    s.emit(L2_FFN_DEPTH, BATCH // LANES)

    s = Section(kit.pr, "l2f_leave")
    s.dve(nc.vector.tensor_tensor, X, X, Yall, ALU.add)
    s.emit()





def layout_l3_attn(w):
    col = lambda a: np.broadcast_to(np.reshape(a, (1, 1)), (P, 1))
    return [("write", w["W_write"].T), ("read", w["W_read"].T), ("decay", col(w["decay"])),
            ("log_alpha", col(w["log_alpha"]))]


def stage_l3_attn(kit, w, arena):
    nc, X = kit.nc, kit.X
    s = Section(kit.pr, "l3_powers")
    e, u, rest, lg, chunk_decay, alpha = (arena.take(1) for _ in range(6))
    decay_to, from_start, to_end, read = arena.take(P), arena.take(P), arena.take(1), arena.take(P)
    ex = s.act(nc.scalar.activation, e, w("decay"), ACT.Exp, scale=-1.0)
    log = log1p(kit, s, e, u, rest, lg, after=[ex])
    neg = s.dve(nc.vector.tensor_scalar, lg, lg, -1.0, None, ALU.mult)
    p1 = s.act(nc.scalar.activation, decay_to, kit.c("lag"), ACT.Exp, scale=lg, after=[neg])
    s.act(nc.scalar.activation, from_start, kit.c("place"), ACT.Exp, scale=lg)
    s.act(nc.scalar.activation, to_end, kit.c("left"), ACT.Exp, scale=lg)
    s.act(nc.scalar.activation, chunk_decay, lg, ACT.Exp, scale=float(P))
    p2 = s.act(nc.scalar.activation, alpha, w("log_alpha"), ACT.Exp)
    s.dve(nc.vector.tensor_tensor, decay_to, decay_to, kit.c("tri_strict"), ALU.mult, after=[p1])
    s.dve(nc.vector.tensor_scalar, read, w("read"), alpha, None, ALU.mult, after=[p2])
    s.emit()

    s = Section(kit.pr, "l3_attn", LANES)
    def batch(lane):
        s.use(lane)
        xr, z, zT, vT = arena.take(TILES, P), arena.take(TILES, P), arena.take(SEQ + 1), arena.take(TILES, P)
        stats, mv, rstd = arena.take(TILES, 6), arena.take(TILES, 2), arena.take(TILES)
        v, vg, wk, st, qd = (arena.take(TILES, P) for _ in range(5))
        reads = arena.take(SEQ)
        Wm = Ring([arena.take(P), arena.take(P)])
        ring = Ring(kit.banks(lane))
        loaded = s.dve(nc.vector.tensor_copy, xr, kit.rows_of(X, lane))
        rows = norm_rows(kit, s, xr, z, mv, stats, rstd, LN_EPS, after=[loaded])
        cleared = s.dve(nc.vector.memset, zT[:, 0:1], 0.0, link=False)
        key, query = zT[:, 0:SEQ], zT[:, 1:SEQ + 1]
        feats = to_features(kit, s, ring, [z[:, t, :] for t in range(TILES)], query, [rows])
        bank, free, k = ring.take()
        for t in range(TILES):
            values = s.mm(bank[:, t * P:(t + 1) * P], query[:, t * P:(t + 1) * P], w("write"),
                          after=[feats, *free] if t == 0 else (), signal=t == TILES - 1)
        bank4 = bank[:, :].rearrange("p (t d) -> p t d", d=P)
        vals = s.act(nc.scalar.copy, v, bank4, after=[values])
        vals_end = s.dve(nc.vector.tensor_scalar, vg, bank4, to_end, None, ALU.mult, after=[values, vals])
        ring.give(k, vals, vals_end)
        keys = to_features(kit, s, ring, [key[:, t * P:(t + 1) * P] for t in range(TILES)],
                           wk.rearrange("p t d -> p (t d)"), [feats, cleared])
        decayed = s.dve(nc.vector.tensor_tensor, qd, query.rearrange("p (t d) -> p t d", d=P),
                        from_start.unsqueeze(1).broadcast_to([P, TILES, P]), ALU.mult, after=[feats])
        bank, free, k = ring.take()
        for t in range(TILES):
            cols = slice(t * P, (t + 1) * P)
            pairs = s.mm(bank[:, cols], key[:, cols], query[:, cols], after=free if t == 0 else (), signal=t == TILES - 1)
        weighed = s.dve(nc.vector.tensor_tensor, st, bank[:, :].rearrange("p (t d) -> p t d", d=P),
                        decay_to.unsqueeze(1).broadcast_to([P, TILES, P]), ALU.mult, after=[pairs])
        ring.give(k, weighed)
        memory, ready = None, None
        rbank, rfree, rk = ring.take()
        for t in range(TILES):
            cols = slice(t * P, (t + 1) * P)
            out = s.mm(rbank[:, cols], v[:, t, :], st[:, t, :], stop=(t == 0), after=[vals, weighed, *rfree],
                       signal=(t == 0))
            if t > 0:
                out = s.mm(rbank[:, cols], memory, qd[:, t, :], start=False, after=[ready, decayed])
            if t < TILES - 1:
                mbank, mfree, mk = ring.take()
                added = s.mm(mbank[:, 0:P], wk[:, t, :], vg[:, t, :], after=[keys, vals_end, *mfree])
                new, nfree, nk = Wm.take()
                if t == 0:
                    ready = s.dve(nc.vector.tensor_copy, new, mbank[:, 0:P], after=[added])
                else:
                    ready = s.dve(nc.vector.scalar_tensor_tensor, new, memory, chunk_decay, mbank[:, 0:P], ALU.mult,
                                  ALU.add, after=[added, *nfree])
                ring.give(mk, ready)
                if t > 0:
                    Wm.give(memory_k, out)
                memory, memory_k = new, nk
        copied = s.act(nc.scalar.copy, reads, rbank[:, :], after=[out])
        ring.give(rk, copied)
        bank, free, k = ring.take()
        for t in range(TILES):
            back = s.mm(bank[:, t * P:(t + 1) * P], reads[:, t * P:(t + 1) * P], read,
                        after=[copied, *free] if t == 0 else (), signal=t == TILES - 1)
        s.dve(nc.vector.tensor_tensor, z, z, bank[:, :].rearrange("p (t d) -> p t d", d=P), ALU.add, after=[back])
        s.dve(nc.vector.tensor_tensor, kit.rows_of(X, lane), xr, z, ALU.add)

    for lane in range(LANES):
        batch(lane)
    s.emit(1, BATCH // LANES)




L3_FFN_GLU = 256
L3_FFN_HALVES = L3_FFN_GLU // P


def layout_l3_ffn(w):
    parts = [("router", w["Wgate"]), ("router_bias", np.broadcast_to(w["bgate"][None, :], (P, EXPERTS))),
             ("out_bias", w["b3"])]
    for n in ("b1", "b2", "bg", "bl"):
        parts.append((n, w[n].reshape(EXPERTS * L3_FFN_HALVES, P).T))
    for e in range(EXPERTS):
        parts += [(f"one{e}", w["W1"][e]), (f"two{e}", w["W2"][e])]
        for f in range(L3_FFN_HALVES):
            rows = slice(f * P, (f + 1) * P)
            parts += [(f"gate{e}_{f}", w["Wg"][e][rows]), (f"lin{e}_{f}", w["Wl"][e][rows]),
                      (f"down{e}_{f}", w["W3"][e][rows])]
    return parts


def stage_l3_ffn(kit, w, arena):
    nc, X = kit.nc, kit.X
    s = Section(kit.pr, "l3_ffn", LANES)
    def batch(lane):
        s.use(lane)
        xr, h, xT = arena.take(TILES, P), arena.take(TILES, P), arena.take(SEQ)
        acc, hid0, hid1 = arena.take(TILES, P), arena.take(L3_FFN_HALVES, SEQ), arena.take(L3_FFN_HALVES, SEQ)
        z, z2 = Ring([arena.take(L3_FFN_HALVES, SEQ) for _ in range(2)]), Ring([arena.take(SEQ) for _ in range(2)])
        sg, gg = Ring([arena.take(SEQ) for _ in range(2)]), Ring([arena.take(SEQ) for _ in range(2)])
        stats, mv, rstd = arena.take(TILES, 6), arena.take(TILES, 2), arena.take(TILES)
        logit, above, equal, pa, pb, share = (arena.take(TILES, EXPERTS) for _ in range(6))
        best, count, need = arena.take(TILES, 8), arena.take(TILES), arena.take(TILES)
        shareT = arena.take(SEQ)
        banks = kit.banks(lane)
        ring, yring, hid = Ring(banks[0:3]), Ring(banks[3:4]), Ring([hid0, hid1])
        E = EXPERTS

        loaded = s.dve(nc.vector.tensor_copy, xr, kit.rows_of(X, lane))
        rows = norm_rows(kit, s, xr, h, mv, stats, rstd, LN_EPS, after=[loaded])
        feats = to_features(kit, s, ring, [h[:, t, :] for t in range(TILES)], xT, [rows])
        logit_bank, lfree, lk = ring.take()
        for t in range(TILES):
            logits = s.mm(logit_bank[:, t * E:(t + 1) * E], xT[:, t * P:(t + 1) * P], w("router"),
                          after=[feats, *lfree] if t == 0 else (), signal=(t == TILES - 1))
        s.dve(nc.vector.tensor_tensor, logit, logit_bank[:, 0:TILES * E].rearrange("p (t e) -> p t e", e=E),
              w("router_bias").unsqueeze(1).broadcast_to([P, TILES, E]), ALU.add, after=[logits])
        ring.give(lk, s.latest("DVE"))
        settle(kit, s)
        for t in range(TILES):
            s.dve(nc.vector.max, best[:, t, :], logit[:, t, :], link=False)
        s.dve(nc.vector.tensor_tensor, above, logit, over(best[:, :, 1], E), ALU.is_gt)
        s.dve(nc.vector.tensor_tensor, equal, logit, over(best[:, :, 1], E), ALU.is_equal, link=False)
        s.dve(nc.vector.tensor_reduce, count, above, AX, ALU.add)
        s.dve(nc.vector.tensor_scalar, need, count, -1.0, 2.0, ALU.mult, ALU.add)
        pre = prefix_exclusive(kit, s, equal, (pa, pb), E)
        s.dve(nc.vector.tensor_tensor, pre, pre, over(need, E), ALU.is_lt)
        s.dve(nc.vector.tensor_tensor, equal, equal, pre, ALU.mult)
        s.dve(nc.vector.tensor_tensor, above, above, equal, ALU.add)
        centred = s.dve(nc.vector.tensor_tensor, logit, logit, over(best[:, :, 0], E), ALU.subtract)
        powers = s.act(nc.scalar.activation, logit, logit, ACT.Exp, after=[centred])
        s.dve(nc.vector.tensor_tensor, share, logit, above, ALU.mult, after=[powers])
        s.dve(nc.vector.tensor_reduce, count, share, AX, ALU.add)
        s.dve(nc.vector.reciprocal, count, count)
        weights = s.dve(nc.vector.tensor_tensor, share, share, over(count, E), ALU.mult)
        shares = to_features(kit, s, ring, [share[:, t, :] for t in range(TILES)], shareT[0:E, :], [weights], rows=E)

        def hidden_all(e, started):
            zt, zfree, zk = z.take()
            for f in range(L3_FFN_HALVES):
                b1, free1, k1 = ring.take()
                one = s.mm(b1[:, :], w(f"one{e}", cols=(f * P, (f + 1) * P)), xT, after=[*free1, *started])
                b2, free2, k2 = ring.take()
                two = s.mm(b2[:, :], w(f"two{e}", cols=(f * P, (f + 1) * P)), xT, after=free2)
                c = e * L3_FFN_HALVES + f
                t2, tfree, tk = z2.take()
                second = s.act(nc.scalar.activation, t2, b2[:, :], ACT.Identity, bias=w("b2", cols=(c, c + 1)),
                               after=[two, *tfree])
                ring.give(k2, second)
                both = s.dve(nc.vector.scalar_tensor_tensor, zt[:, f, :], b1[:, :], w("b1", cols=(c, c + 1)), t2,
                             ALU.add, ALU.mult, after=[one, second, *(zfree if f == 0 else ())], link=False)
                ring.give(k1, both)
                z2.give(tk, both)
            hT, hfree, hk = hid.take()
            for g in range(L3_FFN_HALVES):
                cols = (g * P, (g + 1) * P)
                bg, freeg, kg = ring.take()
                for f in range(L3_FFN_HALVES):
                    gate = s.mm(bg[:, :], w(f"gate{e}_{f}", cols=cols), zt[:, f, :], start=f == 0, stop=f == L3_FFN_HALVES - 1,
                                after=[*freeg, both] if f == 0 else (), signal=f == L3_FFN_HALVES - 1)
                bl, freel, kl = ring.take()
                for f in range(L3_FFN_HALVES):
                    lin = s.mm(bl[:, :], w(f"lin{e}_{f}", cols=cols), zt[:, f, :], start=f == 0, stop=f == L3_FFN_HALVES - 1,
                               after=freel if f == 0 else (), signal=f == L3_FFN_HALVES - 1)
                c = e * L3_FFN_HALVES + g
                gb, gfree, gk = gg.take()
                silu = s.act(nc.scalar.activation, gb, bg[:, :], ACT.Silu, bias=w("bg", cols=(c, c + 1)),
                             after=[gate, *gfree])
                ring.give(kg, silu)
                out = s.dve(nc.vector.scalar_tensor_tensor, hT[:, g, :], bl[:, :], w("bl", cols=(c, c + 1)), gb,
                            ALU.add, ALU.mult, after=[lin, silu, *(hfree if g == 0 else ())], link=False)
                ring.give(kl, out)
                gg.give(gk, out)
            z.give(zk, lin)
            return hT, hk, out

        done = weighted_experts(kit, s, hidden_all, lambda e, t: share[:, t, e:e + 1], acc,
                                lambda e, f: w(f"down{e}_{f}"), L3_FFN_HALVES, hid, yring, [feats])
        bank, free, k = yring.take()
        for t in range(TILES):
            biases = s.mm(bank[:, t * P:(t + 1) * P], shareT[0:E, t * P:(t + 1) * P], w("out_bias"),
                          after=[shares, *free] if t == 0 else (), signal=(t == TILES - 1))
        s.dve(nc.vector.tensor_tensor, acc, acc, bank[:, :].rearrange("p (t d) -> p t d", d=P), ALU.add,
              after=[biases, done])
        s.dve(nc.vector.tensor_tensor, kit.rows_of(X, lane), xr, acc, ALU.add)

    for lane in range(LANES):
        batch(lane)
    s.emit(1, BATCH // LANES)




STAGES = [("L0_attn_", layout_l0_attn, stage_l0_attn), ("L0_ffn_", layout_l0_ffn, stage_l0_ffn),
          ("L1_attn_", layout_l1_attn, stage_l1_attn), ("L1_ffn_", layout_l1_ffn, stage_l1_ffn),
          ("L2_attn_", layout_l2_attn, stage_l2_attn), ("L2_ffn_", layout_l2_ffn, stage_l2_ffn),
          ("L3_attn_", layout_l3_attn, stage_l3_attn), ("L3_ffn_", layout_l3_ffn, stage_l3_ffn)]
SBUF_COLUMNS = 53180


def build(nc, x, out, consts, consts_at, packs, places):
    ctx = ExitStack()
    with ctx:
        pr = Program(nc, ctx)

        def sbuf(name, columns):
            return ctx.enter_context(nc.sbuf_tensor(name, [P, columns], F32))

        X = sbuf("x_rows", BATCH * TILES * DIM)[:, :].rearrange("p (t d) -> p t d", d=DIM)
        C = sbuf("constants", consts.shape[1])
        sides = [sbuf(f"weights_{n}", max(a.shape[1] for a in packs[n::2])) for n in range(2)]
        widths = [a.shape[1] for a in packs]
        work_columns = SBUF_COLUMNS - X.shape[1] * DIM - consts.shape[1] - max(widths[0::2]) - max(widths[1::2])
        work = sbuf("work", work_columns)
        rows = lambda a: a.rearrange("(t p) d -> p t d", p=P)

        s = Section(pr, "load")
        s.dma(0, X, rows(x))
        s.dma(1, C[:, :], consts)
        s.emit()
        pr.prefetch(sides[0][:, 0:packs[0].shape[1]], packs[0])
        kit = Kit(pr, Weights(C, consts_at), X)
        s = Section(pr, "first")
        column = kit.c("scratch", cols=(0, 1))
        written = s.dve(nc.vector.memset, column, 0.0)
        written = s.pool(nc.gpsimd.memset, column, 0.0, after=[written])
        s.act(nc.scalar.copy, column, kit.c("ones", cols=(0, 1)), after=[written])
        s.mm(pr.banks[0][:, 0:1], kit.ident, kit.c("ones", cols=(0, 1)))
        s.emit()
        for n, (_, _, stage) in enumerate(STAGES):
            pr.weights_landed()
            if n + 1 < len(STAGES):
                pr.prefetch(sides[(n + 1) % 2][:, 0:packs[n + 1].shape[1]], packs[n + 1])
            spare = [(side, used, side.shape[1] - used) for side, used in
                     ((sides[n % 2], widths[n]), (sides[(n + 1) % 2], widths[n + 1] if n + 1 < len(STAGES) else 0))]
            stage(kit, Weights(sides[n % 2], places[n]), Arena([(work, 0, work_columns), *spare]))
        s = Section(pr, "store")
        s.dma(0, rows(out), X)
        s.emit()
        for p in pr.producers:
            nc.sync.wait_ge(pr.sem[p], pr.base[p] * pr.unit[p])


def kernel(**inputs):
    import concourse.bacc as bacc
    from concourse.bass_utils import run_bass_kernel_spmd

    packs, places = [], []
    for prefix, layout, _ in STAGES:
        own = {k[len(prefix):]: np.asarray(v) for k, v in inputs.items() if k.startswith(prefix)}
        a, at = pack(layout(own))
        packs.append(a)
        places.append(at)
    consts, consts_at = pack(constants())
    arrays = {"x": np.ascontiguousarray(np.asarray(inputs["L0_attn_hidden_states"]).reshape(BATCH * SEQ, DIM)),
              "constants_dram": consts}
    arrays.update({f"weights_dram_{n}": a for n, a in enumerate(packs)})
    nc = bacc.Bacc("TRN2", target_bir_lowering=False, num_devices=1)
    dram = {k: nc.dram_tensor(k, list(a.shape), F32, kind="ExternalInput").ap() for k, a in arrays.items()}
    out = nc.dram_tensor("out", [BATCH * SEQ, DIM], F32, kind="ExternalOutput").ap()
    build(nc, dram["x"], out, dram["constants_dram"], consts_at, [dram[f"weights_dram_{n}"] for n in range(len(packs))],
          places)
    got = run_bass_kernel_spmd(nc, [arrays], core_ids=[0])
    return got.results[0]["out"].reshape(BATCH, SEQ, DIM)
```
